# Optimizing a Trainium2 kernel written in Bass

```python
import numpy as np
import jax
import jax.numpy as jnp

def _softmax(x, axis=-1):
    return jax.nn.softmax(x, axis=axis)

def _gelu(x):
    return jax.nn.gelu(x, approximate=True)

def _silu(x):
    return jax.nn.silu(x)

def _sigmoid(x):
    return jax.nn.sigmoid(x)

def _layernorm(x, axis=-1, eps=1e-05):
    m = jnp.mean(x, axis=axis, keepdims=True)
    v = jnp.var(x, axis=axis, keepdims=True)
    return (x - m) / jnp.sqrt(v + eps)

def _scatter_add(tgt, idx, src, axis=0):
    return tgt.at[idx].add(src)

def _segment_sum(src, seg, n):
    return jax.ops.segment_sum(src, seg, n)
kernel_name = 'mk_hybrid_d1_jaxref_r8_38593b'

def setup_inputs(seed: int=0):
    np.random.seed(seed)
    _w = jnp.asarray

    def _L0_attn_a_setup():
        import jax, jax.numpy as jnp
        import numpy as np
        HIDDEN = 128
        HEADS = 16
        HEAD_DIM = HIDDEN // HEADS
        SCALE = HEAD_DIM ** (-0.5)
        key = jax.random.key(seed)
        ks = jax.random.split(key, 9)
        init = 1.0 / np.sqrt(HIDDEN)
        hidden_states = jax.random.normal(ks[0], (8, 128, HIDDEN), dtype=jnp.float32)

        def lin(k):
            kw, kb = jax.random.split(k)
            W = jax.random.uniform(kw, (HIDDEN, HIDDEN), jnp.float32, -init, init)
            b = jax.random.uniform(kb, (HIDDEN,), jnp.float32, -init, init)
            return (W, b)
        Wq, bq = lin(ks[1])
        Wk, bk = lin(ks[2])
        Wv, bv = lin(ks[3])
        Wo, bo = lin(ks[4])
        return {'hidden_states': hidden_states, 'Wq': Wq, 'bq': bq, 'Wk': Wk, 'bk': bk, 'Wv': Wv, 'bv': bv, 'Wo': Wo, 'bo': bo}
    _L0_attn_a_in = _L0_attn_a_setup()

    def _L0_attn_b_setup():
        import jax, jax.numpy as jnp
        import numpy as np
        B, T, D_DENSE = (4, 256, 128)
        SPARSE = 128
        NH = 8
        HD = SPARSE // NH
        K = 32
        WIN = 64
        RANK = HD // 4
        key = jax.random.key(seed)
        ks = jax.random.split(key, 8)
        n = lambda k, shape, scale=1.0: jax.random.normal(k, shape, dtype=jnp.float32) * scale
        return {'x': n(ks[0], (B, T, D_DENSE)), 'encoder_query': n(ks[1], (NH, D_DENSE, HD), 0.02), 'encoder_value': n(ks[2], (NH, D_DENSE, HD), 0.02), 'mn_w1': n(ks[3], (SPARSE, SPARSE // 2), 1.0 / np.sqrt(SPARSE)), 'mn_b1': jnp.zeros((SPARSE // 2,), jnp.float32), 'mn_w2': n(ks[4], (SPARSE // 2, NH * HD), 1.0 / np.sqrt(SPARSE // 2)), 'mn_b2': jnp.zeros((NH * HD,), jnp.float32), 'base_metric': jnp.ones((NH, HD), jnp.float32) * 0.1, 'decoder': n(ks[5], (NH * HD, D_DENSE), 0.02), 'hebbian_U': n(ks[6], (NH, HD, RANK), 0.01), 'hebbian_V': n(ks[7], (NH, RANK, HD), 0.01)}
    _L0_attn_b_in = _L0_attn_b_setup()

    def _L0_ffn_setup():
        import jax, jax.numpy as jnp
        import numpy as np
        import math
        D_IN = 128
        FEATURES = (512, 512, 128)
        BATCH, SEQ = (8, 256)

        def _conn_dense(kernel_bool, x):
            w = jnp.where(kernel_bool, jnp.float32(1.0), jnp.float32(-1.0))
            return x @ w
        key = jax.random.key(seed)
        kx, kk0, kk1, kk2 = jax.random.split(key, 4)
        x = jax.random.normal(kx, (BATCH, SEQ, D_IN), dtype=jnp.float32)
        k0 = jax.random.randint(kk0, (2 * D_IN, FEATURES[0]), 0, 2).astype(jnp.bool_)
        k1 = jax.random.randint(kk1, (FEATURES[0], FEATURES[1]), 0, 2).astype(jnp.bool_)
        k2 = jax.random.randint(kk2, (FEATURES[1], FEATURES[2]), 0, 2).astype(jnp.bool_)
        s0 = jnp.asarray(1.0 / math.sqrt(2 * D_IN), dtype=jnp.float32)
        s1 = jnp.asarray(1.0 / math.sqrt(FEATURES[0]), dtype=jnp.float32)
        s2 = jnp.asarray(1.0 / math.sqrt(FEATURES[1]), dtype=jnp.float32)
        return {'x': x, 'k0': k0, 'k1': k1, 'k2': k2, 's0': s0, 's1': s1, 's2': s2}
    _L0_ffn_in = _L0_ffn_setup()
    _d = {'L0_attn_a_hidden_states': _L0_attn_a_in['hidden_states'], 'L0_attn_a_Wq': _L0_attn_a_in['Wq'], 'L0_attn_a_bq': _L0_attn_a_in['bq'], 'L0_attn_a_Wk': _L0_attn_a_in['Wk'], 'L0_attn_a_bk': _L0_attn_a_in['bk'], 'L0_attn_a_Wv': _L0_attn_a_in['Wv'], 'L0_attn_a_bv': _L0_attn_a_in['bv'], 'L0_attn_a_Wo': _L0_attn_a_in['Wo'], 'L0_attn_a_bo': _L0_attn_a_in['bo'], 'L0_attn_b_encoder_query': _L0_attn_b_in['encoder_query'], 'L0_attn_b_encoder_value': _L0_attn_b_in['encoder_value'], 'L0_attn_b_mn_w1': _L0_attn_b_in['mn_w1'], 'L0_attn_b_mn_b1': _L0_attn_b_in['mn_b1'], 'L0_attn_b_mn_w2': _L0_attn_b_in['mn_w2'], 'L0_attn_b_mn_b2': _L0_attn_b_in['mn_b2'], 'L0_attn_b_base_metric': _L0_attn_b_in['base_metric'], 'L0_attn_b_decoder': _L0_attn_b_in['decoder'], 'L0_attn_b_hebbian_U': _L0_attn_b_in['hebbian_U'], 'L0_attn_b_hebbian_V': _L0_attn_b_in['hebbian_V'], 'L0_ffn_k0': _L0_ffn_in['k0'], 'L0_ffn_k1': _L0_ffn_in['k1'], 'L0_ffn_k2': _L0_ffn_in['k2'], 'L0_ffn_s0': _L0_ffn_in['s0'], 'L0_ffn_s1': _L0_ffn_in['s1'], 'L0_ffn_s2': _L0_ffn_in['s2']}
    _x0 = _d['L0_attn_a_hidden_states']
    _d['L0_attn_a_hidden_states'] = jax.random.normal(jax.random.fold_in(jax.random.key(seed), 1), (8, 1024, 128), dtype=_x0.dtype)
    del _x0
    return _d

def reference(L0_attn_a_hidden_states, L0_attn_a_Wq, L0_attn_a_bq, L0_attn_a_Wk, L0_attn_a_bk, L0_attn_a_Wv, L0_attn_a_bv, L0_attn_a_Wo, L0_attn_a_bo, L0_attn_b_encoder_query, L0_attn_b_encoder_value, L0_attn_b_mn_w1, L0_attn_b_mn_b1, L0_attn_b_mn_w2, L0_attn_b_mn_b2, L0_attn_b_base_metric, L0_attn_b_decoder, L0_attn_b_hebbian_U, L0_attn_b_hebbian_V, L0_ffn_k0, L0_ffn_k1, L0_ffn_k2, L0_ffn_s0, L0_ffn_s1, L0_ffn_s2):

    def _L0_attn_a_ref(hidden_states, Wq, bq, Wk, bk, Wv, bv, Wo, bo):
        import jax, jax.numpy as jnp
        import numpy as np
        HIDDEN = 128
        HEADS = 16
        HEAD_DIM = HIDDEN // HEADS
        SCALE = HEAD_DIM ** (-0.5)
        b, s, d = hidden_states.shape
        q = (hidden_states @ Wq.T + bq).reshape(b, s, HEADS, HEAD_DIM)
        k = (hidden_states @ Wk.T + bk).reshape(b, s, HEADS, HEAD_DIM)
        v = (hidden_states @ Wv.T + bv).reshape(b, s, HEADS, HEAD_DIM)
        q = q * SCALE
        scores = jnp.einsum('bqhd,bkhd->bhqk', q, k)
        probs = jax.nn.softmax(scores.astype(jnp.float32), axis=-1).astype(scores.dtype)
        out = jnp.einsum('bhqk,bkhd->bqhd', probs, v).reshape(b, s, d)
        return out @ Wo.T + bo

    def _L0_attn_b_ref(x, encoder_query, encoder_value, mn_w1, mn_b1, mn_w2, mn_b2, base_metric, decoder, hebbian_U, hebbian_V):
        import jax, jax.numpy as jnp
        import numpy as np
        B, T, D_DENSE = (4, 256, 128)
        SPARSE = 128
        NH = 8
        HD = SPARSE // NH
        K = 32
        WIN = 64
        RANK = HD // 4
        Bv, Tv, _ = x.shape
        q = jax.nn.relu(jnp.einsum('btd,nde->btne', x, encoder_query))
        v = jax.nn.relu(jnp.einsum('btd,nde->btne', x, encoder_value))
        qflat = q.reshape(Bv, Tv, -1)
        sig = qflat.mean(axis=1)
        if Tv >= 8:
            sig = sig + qflat[:, ::8].mean(axis=1) * 0.5
        hidden = jax.nn.gelu(sig @ mn_w1 + mn_b1, approximate=False)
        mod = (hidden @ mn_w2 + mn_b2).reshape(Bv, NH, HD)
        metric = jax.nn.softplus(base_metric[None] + 0.1 * mod)
        pos = jnp.arange(Tv)
        offs = jnp.arange(0, -WIN, -1)
        idx = jnp.clip(pos[:, None] + offs[None, :], 0, Tv - 1)
        mask = idx <= pos[:, None]
        k_act = min(K, WIN)
        batch_ix = jnp.arange(Bv)[:, None, None]
        outs = []
        for h in range(NH):
            q_h = q[:, :, h, :]
            v_h = v[:, :, h, :]
            kw = q_h[:, idx, :]
            diff = kw - q_h[:, :, None, :]
            wsq = diff * diff * metric[:, h][:, None, None, :]
            dist = jnp.sqrt(wsq.sum(-1) + 1e-08)
            dist = jnp.where(mask[None], dist, jnp.inf)
            neg, loc = jax.lax.top_k(-dist, k_act)
            topd = -neg
            topi = jnp.take_along_axis(jnp.broadcast_to(idx[None], (Bv, Tv, WIN)), loc, axis=2)
            infl = jnp.exp(-topd)
            infl = infl / (infl.sum(-1, keepdims=True) + 1e-08)
            nv = v_h[batch_ix, topi]
            context = jnp.einsum('btk,btkd->btd', infl, nv)
            q_norm = jnp.linalg.norm(q_h, axis=-1, keepdims=True)
            gate = (q_norm > 0.2).astype(q_h.dtype)
            Hm = hebbian_U[h] @ hebbian_V[h]
            qhat = q_h / jnp.maximum(q_norm, 1e-12)
            context = context + gate * 0.1 * (qhat @ Hm)
            outs.append(q_h * context)
        out_sparse = jnp.stack(outs, axis=2).reshape(Bv, Tv, -1)
        return out_sparse @ decoder

    def _L0_ffn_ref(x, k0, k1, k2, s0, s1, s2):
        import jax, jax.numpy as jnp
        import numpy as np
        import math
        D_IN = 128
        FEATURES = (512, 512, 128)
        BATCH, SEQ = (8, 256)

        def _conn_dense(kernel_bool, x):
            w = jnp.where(kernel_bool, jnp.float32(1.0), jnp.float32(-1.0))
            return x @ w
        h = jnp.concatenate([x, -x], axis=-1)
        h = s0 * _conn_dense(k0, h)
        h = jax.nn.relu(h) * 2
        h = s1 * _conn_dense(k1, h)
        h = jax.nn.relu(h) * 2
        h = s2 * _conn_dense(k2, h)
        return h
    x = L0_attn_a_hidden_states
    x = x + _L0_attn_a_ref(_layernorm(x, axis=-1), L0_attn_a_Wq, L0_attn_a_bq, L0_attn_a_Wk, L0_attn_a_bk, L0_attn_a_Wv, L0_attn_a_bv, L0_attn_a_Wo, L0_attn_a_bo)
    x = x + _L0_ffn_ref(_layernorm(x, axis=-1), L0_ffn_k0, L0_ffn_k1, L0_ffn_k2, L0_ffn_s0, L0_ffn_s1, L0_ffn_s2)
    x = x + _L0_attn_b_ref(_layernorm(x, axis=-1), L0_attn_b_encoder_query, L0_attn_b_encoder_value, L0_attn_b_mn_w1, L0_attn_b_mn_b1, L0_attn_b_mn_w2, L0_attn_b_mn_b2, L0_attn_b_base_metric, L0_attn_b_decoder, L0_attn_b_hebbian_U, L0_attn_b_hebbian_V)
    x = x + _L0_ffn_ref(_layernorm(x, axis=-1), L0_ffn_k0, L0_ffn_k1, L0_ffn_k2, L0_ffn_s0, L0_ffn_s1, L0_ffn_s2)
    return x

_drawn_inputs = setup_inputs


def setup_inputs(seed=0):
    import zlib

    import numpy as np

    out = dict(_drawn_inputs(seed))
    spreads = {'L0_attn_b_mn_b1': (0.0, 2.0),
     'L0_attn_b_mn_b2': (0.0, 2.0),
     'L0_attn_b_base_metric': (0.10000000149011612, 0.6)}
    factors = {'L0_attn_a_Wq': 5.988,
     'L0_attn_a_bq': 8.0,
     'L0_attn_a_Wk': 5.995,
     'L0_attn_a_bk': 64.0,
     'L0_attn_a_Wv': 4.299,
     'L0_attn_b_encoder_query': 8.0,
     'L0_attn_b_encoder_value': 8.0,
     'L0_attn_b_mn_w1': 8.0,
     'L0_attn_b_mn_w2': 8.0,
     'L0_attn_b_decoder': 8.0,
     'L0_attn_b_hebbian_U': 64.0,
     'L0_attn_b_hebbian_V': 64.0}
    for name, (base, spread) in spreads.items():
        noise = np.random.default_rng([zlib.crc32(name.encode()), seed]).standard_normal(out[name].shape)
        drawn = base * np.exp(spread * noise) if base else spread * noise
        out[name] = jnp.asarray(drawn.astype(out[name].dtype))
    for name, factor in factors.items():
        out[name] = (out[name] * factor).astype(out[name].dtype)
    return out
```

```python
from contextlib import ExitStack

import concourse.bass as bass
from concourse import mybir

F32 = mybir.dt.float32
BF16 = mybir.dt.bfloat16
U8 = mybir.dt.uint8
U32 = mybir.dt.uint32
ALU = mybir.AluOpType
ACT = mybir.ActivationFunctionType
AX = mybir.AxisListType

P = 128
NB, T = 8, 1024
NU = T // P
HALF = 512
NH, HD = 16, 8
NQUAD = NH // 4
SCALE = float(HD) ** -0.5
PARTS = 3
QPART = (0, 0, 0, 1, 1, 2)
KPART = (0, 1, 2, 0, 1, 0)
MROW = len(QPART) * HD
VW = 32
NF, FC = 512, 4
SH, SE = 8, 16
WIN, TOPK, BLK = 64, 32, 64
RPAD = T + WIN
BIG = 1.0e18
LN_EPS = 1e-5
EXP_LN = "natural_log_exp_and_others"
LOADS = 37
LINKS_A, LINKS_P = 31, 56

STEPS = 16
STAGES_A = [("ln1", 0), ("qkv", 0), ("load", 0)] + [("max", (0, i)) for i in range(STEPS)] + [("mrow", 0)]
for _n in range(NQUAD):
    if _n + 1 < NQUAD:
        STAGES_A.append(("load", _n + 1))
    for _i in range(STEPS):
        STAGES_A.append(("exp", (_n, _i)))
        if _n + 1 < NQUAD:
            STAGES_A.append(("max", (_n + 1, _i)))
    STAGES_A.append(("fin", _n))
    if _n + 1 < NQUAD:
        STAGES_A.append(("mrow", _n + 1))
STAGES_A += [("otr", u) for u in range(NU)]
STAGES_P = [("ln", 0), ("ffn", 0), ("ffn", 1), ("ln", 1), ("proj", 0)]
for _u in range(NU + 2):
    STAGES_P += [(s, _u - d) for d, s in enumerate(("dist", "top", "ctx")) if 0 <= _u - d < NU]
STAGES_P += [("ln", 2), ("ffn", 2), ("ffn", 3), ("out", 0)]
USES = dict(ln1=2, qkv=6, load=0, max=4, mrow=1, exp=0, fin=0, otr=3,
            ln=2, ffn=9, proj=24, dist=2, top=0, ctx=5, out=0)
NA = sum(USES[s] for s, _ in STAGES_A)
NP = sum(USES[s] for s, _ in STAGES_P)
assert NA % 2 == 0 and NP % 2 == 0


def numbered(stages):
    k, said = 0, []
    for stage, n in stages:
        said.append((stage, n, k))
        k += USES[stage]
    return said


WORK = [("a",) + x for x in numbered(STAGES_A)] + [("p",) + x for x in numbered(STAGES_P)]


class Count:
    made = []

    def __init__(self, sem, per, unit=1):
        self.sem, self.per, self.unit = sem, per, unit
        Count.made.append(sem)

    def at(self, b, k):
        return self.sem, b * (self.per * self.unit) + (k * self.unit + 1)


class Ring:

    def __init__(self, banks, sem, name, uses):
        self.banks = banks
        self.ready = Count(sem(f"{name}_ready"), uses)
        self.evicted = [Count(sem(f"{name}_evicted{i}"), uses // 2) for i in range(2)]

    def bank(self, k):
        return self.banks[k % 2]

    def free(self, b, k):
        return self.evicted[k % 2].at(b, k // 2)

    def filled(self, b, k):
        return self.ready.at(b, k + 1)

    def moved(self, b, k):
        return self.evicted[k % 2].at(b, k // 2 + 1)

    def emptied(self, k):
        return self.evicted[k % 2].sem


def hybrid_block_kernel(nc, x, Wq, bq, Wk, bk, Wv, bv, Wo, bo, enc_q, enc_v, mn_w1, mn_b1, mn_w2, mn_b2,
                        base_metric, decoder, heb_U, heb_V, k0, k1, k2, s0, s1, s2, out):
    with ExitStack() as ctx:
        def sb(name, shape, dt=F32):
            return ctx.enter_context(nc.sbuf_tensor(name, shape, dt))

        def sem(name):
            return ctx.enter_context(nc.semaphore(name))

        def count(name, per, unit=1):
            return Count(sem(name), per, unit)

        Count.made.clear()
        psum = [ctx.enter_context(nc.psum_tensor(f"bank{i}", [P, HALF], F32)) for i in range(8)]
        A = Ring(psum[0:2], sem, "a", NA)
        R = Ring(psum[2:4], sem, "p", NP)
        st_bank = psum[4:7]
        ov_bank = psum[7]

        scratch_qk = nc.dram_tensor("scratch_qk", [2 * PARTS, P, T], BF16, kind="Internal").ap()
        scratch_m = nc.dram_tensor("scratch_m", [PARTS * 32, P], BF16, kind="Internal").ap()

        ident = sb("ident", [P, P])
        flip = sb("flip", [P, P])
        identb = sb("identb", [P, P], BF16)
        wT = sb("wT", [P, 4, P])
        wqkb = sb("wqkb", [P, 2])
        bvb = sb("bvb", [P, P])
        bob = sb("bob", [P, P])
        W0 = sb("W0", [P, NF])
        W1 = sb("W1", [P, FC, NF])
        W2 = sb("W2", [P, FC, P])
        scol = sb("scol", [P, 3])
        eq = sb("eq", [P, P])
        ev = sb("ev", [P, P])
        eqd = sb("eqd", [P, 2, P])
        w1m = sb("w1m", [P, P // 2])
        b1m = sb("b1m", [P // 2, 1])
        w2d = sb("w2d", [P // 2, 3, P])
        rows = sb("rows", [1, 2, 3, P])
        cols = sb("cols", [P, 2, 3])
        dec = sb("dec", [P, P])
        up = sb("up", [P, 4])
        ub = sb("ub", [P, SH, 4])
        uT = sb("uT", [32, P])
        vh = sb("vh", [32, SE])
        bdh = sb("bdh", [P, SH, SE])
        blk = sb("blk", [P, SH])
        half0 = sb("half0", [P, 4])
        half1 = sb("half1", [P, 4])
        any0 = sb("any0", [P, 1])
        any1 = sb("any1", [P, 1])
        minus1 = sb("minus1", [P, 4])
        offself = sb("offself", [P, 2, P])
        outside = sb("outside", [P, P])
        zeros3 = sb("zeros3", [PARTS, T], BF16)
        ones3 = sb("ones3", [PARTS, T], BF16)
        ones1 = sb("ones1", [1, 1])
        eps8 = sb("eps8", [P, 1])

        xa = sb("xa", [P, NU, P])
        xTa = sb("xTa", [P, T])
        pq = sb("pq", [P, 2 * PARTS, T], BF16)
        xna = pq[:, 0:2, :].bitcast(F32).rearrange("p a (u c) -> p (a u) c", c=P)
        Q = sb("Q", [P, 2, 2, T], BF16)
        K = sb("K", [P, 2, 4, T], BF16)
        Vg = sb("Vg", [P, NU, NH, VW])
        mred = sb("mred", [P, 32, 2])
        nm = sb("nm", [P, 3, 32])
        mb = sb("mb", [P, PARTS, 32], BF16)
        mT = sb("mT", [PARTS * 32, P], BF16)
        PT = sb("PT", [P, 8, HALF])
        oT = sb("oT", [P, NQUAD, T])
        qkf = oT[:, 0:2, :]
        rden = sb("rden", [P, NH])
        on = sb("on", [P, P])
        onT = sb("onT", [P, P])

        xr = sb("xr", [P, NU, P])
        stat = sb("stat", [P, 2, NU, 6])
        mv = sb("mv", [P, 2, NU, 2])
        ls = sb("ls", [P, 2, 8, NU])
        xn = sb("xn", [P, NU, P])
        xT = sb("xT", [P, T])
        h1 = sb("h1", [P, FC, HALF])
        h2 = sb("h2", [P, FC, HALF])
        xrev = sb("xrev", [P, RPAD])
        qd = sb("qd", [P, 2, T])
        B = sb("B", [P, 2, RPAD])
        Bs = sb("Bs", [P, RPAD])
        qh = sb("qh", [P, T])
        sq = sb("sq", [P, T])
        sig = sb("sig", [P, 4])
        hid = sb("hid", [P // 2, 1])
        met = sb("met", [P, 6, 3])
        alpha = sb("alpha", [P, SH])
        beta = sb("beta", [P, 2])
        nb = sb("nb", [P, 16])
        an = sb("an", [P, NU, 16])
        gn = sb("gn", [P, 3, NU, SH])
        qtok = sb("qtok", [P, NU, P])
        hb = sq[:, :].rearrange("p (u c) -> p u c", c=P)
        Vw = sb("Vw", [P, 2 * NU, SH, SE + 1])
        Aop = sb("Aop", [P, SH, P])
        D = h1[:, :, :].rearrange("p (i a) (b c) -> p i (a b) c", i=2, c=P)
        E = h2[:, :, :].rearrange("p (i a) (b c) -> p i (a b) c", i=2, c=P)
        Rm = xn
        m8 = sb("m8", [P, SH, 8])
        WT = Bs[:, 0:T].rearrange("p (h c) -> p h c", h=SH)
        rd = sb("rd", [P, 2, SH])
        s_tok = sb("s_tok", [P, P])
        s_T = sb("s_T", [P, P])
        wload = oT[:, 0, :].rearrange("p (a c) -> p a c", a=8)[:, 0:4, :]
        kw0, kw1, kw2 = (PT[:, a:b, 0:w].bitcast(U32) for a, b, w in ((0, 2, P), (2, 6, P), (6, 7, P)))
        kw2 = kw2.rearrange("p o (a c) -> p (o a) c", a=FC)
        kb0, kb1, kb2 = kw0.bitcast(U8), kw1.bitcast(U8), kw2.bitcast(U8)
        kf = h1[:, 0:2, :]

        loaded = sem("weights_loaded")
        loadk = sem("signs_loaded")
        masks = sem("masks_made")
        setup_pe = sem("setup_products")
        setup_v = sem("setup_vector")
        u_spread = sem("u_spread")
        u_turned = sem("u_turned")
        rows_set = sem("one_rows_set")
        waits_passed = sem("waits_passed")
        links = {"a": count("vector_steps_a", LINKS_A), "p": count("vector_steps_p", LINKS_P)}
        x_in = count("x_in", 1, 16)
        ln_a = count("ln_a", 1)
        ln_p = count("ln_p", 3)
        xpad = count("first_repeated", 1)
        met_z = count("metric_in", 1)
        met_e = count("metric_exp", 1)
        met_l = count("metric_ln", 1)
        gn_l = count("gate_ln", 1)
        e_steps = count("e_steps", 2 * NU)
        top8 = count("top8", NU * 8 * SH)
        var_a = count("var_a", 1)
        rs_a = count("rstd_a", 1)
        xn_a = count("xn_a", 1)
        xb_a = count("bias_added", 1)
        act_a = count("part_rounded", 4)
        pool_a = count("part_left", 4)
        split_out = count("split_out", 1, 16)
        quad_in = count("quad_in", NQUAD, 28 * 16)
        m_red = count("max_split", NQUAD)
        m_T = count("max_transposed", NQUAD)
        m_out = count("max_out", NQUAD, 16)
        m_in = count("max_in", NQUAD, 32)
        scores = count("scores", NQUAD * 64)
        probs = count("probs", NQUAD * 64)
        pv = count("pv", NQUAD * 16)
        o_out = count("o_out", NQUAD * 2)
        rd_a = count("rden_a", NU)
        var_p = count("var_p", 3)
        rs_p = count("rstd_p", 3)
        xn_p = count("xn_p", 3)
        sq_p = count("squares", 1)
        sig_p = count("sig_p", 1)
        met_p = count("metric", 1)
        bop = count("b_operand", 2)
        gn_v = count("gate_in", 1)
        gn_a = count("gate_norm", 1)
        aop_p = count("a_operand", NU)
        d_act = count("d_clamped", NU)
        d_scaled = count("d_scaled", NU)
        d_pool = count("d_masked", NU)
        e_act = count("e_done", NU)
        w_v = count("w_done", NU)
        s_v = count("s_done", NU)
        out_p = count("out_done", 1, 16)
        block = ctx.enter_context(nc.Block())

        x_t = x.rearrange("b (u p) c -> b p u c", p=P)
        out_t = out.rearrange("b (u p) c -> b p u c", p=P)
        qk_t = scratch_qk.rearrange("s (h d) t -> s d h t", d=HD)
        m_t = scratch_m.rearrange("(s a i u) t -> s a i (u t)", s=PARTS, a=2, i=2)

        def pass_waits(eng):
            eng.sem_inc(waits_passed, 1)

        k_proj = next(k for _, stage, _, k in WORK if stage == "proj")
        k_qd, k_vw = k_proj + 8, k_proj + 20

        def window(w):
            return slice(T - BLK * (w + 1), T - BLK * (w + 1) + P)

        def rows_of(bank, r):
            return bank[:, :].rearrange("p (a r) -> p a r", r=r)

        def cast(ap, dims):
            return ap.unsqueeze(len(dims) - 1).broadcast_to(dims)

        @block.sync
        def _(sp):
            n = 0

            for s in Count.made:
                sp.sem_inc(s, 1)

            def load(dst, src):
                nonlocal n
                sp.dma_start(dst, src).then_inc(loaded, 16)
                n += 1

            for i, w in enumerate((Wq, Wk, Wv, Wo)):
                load(wload[:, i, :], w)
            load(wqkb[:, 0:1], bq.rearrange("(p o) -> p o", o=1))
            load(wqkb[:, 1:2], bk.rearrange("(p o) -> p o", o=1))
            load(bvb[:, :], bv.partition_broadcast(P))
            load(bob[:, :], bo.partition_broadcast(P))
            for i, s in enumerate((s0, s1, s2)):
                load(scol[:, i:i + 1], s.partition_broadcast(P))
            load(eq[:, :].rearrange("d (n e) -> d n e", e=SE), enc_q.rearrange("n d e -> d n e"))
            load(ev[:, :].rearrange("d (n e) -> d n e", e=SE), enc_v.rearrange("n d e -> d n e"))
            ed = eqd[:, :, :].rearrange("d f (g s e) -> d f g s e", g=4, s=2)
            wd = w2d[:, :, :].rearrange("d f (g s e) -> d f g s e", g=4, s=2)
            rw = rows[:, :, :, :].rearrange("o v f (g s e) -> o v f g s e", g=4, s=2)
            vecs = (mn_b2.rearrange("(o n) -> o n", o=1), base_metric.rearrange("h e -> (h e)").rearrange("(o n) -> o n", o=1))
            for f in range(2):
                for s in range(2):
                    load(ed[:, f, :, s, :], enc_q[4 * f:4 * f + 4].rearrange("n d e -> d n e"))
                    load(wd[:, f, :, s, :], mn_w2[:, 64 * f:64 * f + 64].rearrange("d (g e) -> d g e", e=SE))
                    for v in range(2):
                        load(rw[:, v, f, :, s, :], vecs[v][:, 64 * f:64 * f + 64].rearrange("o (g e) -> o g e", e=SE))
            load(w2d[:, 2, :], mn_w2)
            for v in range(2):
                load(rows[:, v, 2, :], vecs[v])
            load(w1m[:, :], mn_w1)
            load(b1m[:, :], mn_b1.rearrange("(p o) -> p o", o=1))
            load(dec[:, :], decoder)
            load(vh[:, :], heb_V.rearrange("h r e -> (h r) e"))
            load(up[:, :], heb_U.rearrange("h e r -> (h e) r"))
            assert n == LOADS, n
            sp.dma_start(kw0, k0.rearrange("(a p) n -> p a n", p=P)).then_inc(loadk, 16)
            sp.dma_start(kw1, k1.rearrange("(a p) n -> p a n", p=P)).then_inc(loadk, 16)
            sp.dma_start(kw2, k2.rearrange("(a p) n -> p a n", p=P)).then_inc(loadk, 16)
            sp.wait_ge(masks, 1)
            for slot in range(2):
                for j in range(4):
                    r = 64 * (j % 2) + MROW
                    sp.dma_start(K[r:r + PARTS, slot, j, :], ones3[:, :]).then_inc(rows_set, 16)

            def go(work, ba, bp):
                for side, stage, n, k in work:
                    b = ba if side == "a" else bp
                    if stage == "ln1":
                        sp.wait_ge(*A.ready.at(b, 0))
                        pass_waits(sp)
                        sp.wait_ge(*A.moved(b, -1))
                        pass_waits(sp)
                        sp.dma_start(xa[:, :, :], x_t[b]).then_inc(x_in.sem, 16)
                    if stage == "qkv":
                        sp.wait_ge(*act_a.at(b, 4))
                        pass_waits(sp)
                        sp.wait_ge(*pool_a.at(b, 4))
                        pass_waits(sp)
                        sp.wait_ge(*quad_in.at(b, 0))
                        pass_waits(sp)
                        sp.dma_start(scratch_qk.rearrange("s c t -> c s t"), pq[:, :, :]).then_inc(split_out.sem, 16)
                    if stage == "load":
                        slot = n % 2
                        sp.wait_ge(*split_out.at(b, 1))
                        pass_waits(sp)
                        sp.wait_ge(*scores.at(b, 4 * STEPS * max(n - 1, 0)))
                        pass_waits(sp)
                        for par in range(2):
                            for g in range(6):
                                r = 64 * par + HD * g
                                h = slice(4 * n + par, 4 * n + par + 3, 2)
                                sp.dma_start(Q[r:r + HD, slot, :, :], qk_t[QPART[g], :, h, :]).then_inc(quad_in.sem, 16)
                                sp.dma_start(K[r:r + HD, slot, par:par + 3:2, :], qk_t[PARTS + KPART[g], :, h, :]).then_inc(quad_in.sem, 16)
                            r = 64 * par + MROW
                            for i in range(2):
                                sp.dma_start(Q[r:r + PARTS, slot, i, :], zeros3[:, :]).then_inc(quad_in.sem, 16)
                    if stage == "mrow":
                        sp.wait_ge(*A.moved(b, k))
                        pass_waits(sp)
                        sp.wait_ge(*m_in.at(b, n))
                        pass_waits(sp)
                        sp.dma_start(scratch_m, mT[:, :]).then_inc(m_out.sem, 16)
                        sp.wait_ge(*m_out.at(b, n + 1))
                        pass_waits(sp)
                        for par in range(2):
                            r = 64 * par + MROW
                            sp.dma_start(Q[r:r + PARTS, n % 2, :, :], m_t[:, par]).then_inc(m_in.sem, 16)
                    if stage == "out":
                        sp.wait_ge(*R.moved(b, k - 1))
                        pass_waits(sp)
                        sp.dma_start(out_t[b], xr[:, :, :]).then_inc(out_p.sem, 16)

            sp.wait_ge(rows_set, 16 * 8)
            with sp.Fori(0, NB) as b:
                go(WORK, b, b)
            sp.wait_ge(*out_p.at(NB, 0))
            pass_waits(sp)

        @block.gpsimd
        def _(pool):
            def select(dst, pattern, base, mult, fill, op=ALU.is_ge):
                link(pool.affine_select(out=dst, in_=dst, compare_op=op, fill=fill, base=base,
                                        pattern=pattern, channel_multiplier=mult))

            step = sem("pool_setup")
            done = [0]

            def link(ins):
                done[0] += 1
                ins.then_inc(step, 1)
                pool.wait_ge(step, done[0])

            link(pool.memset(K[:, :, :, :], 0.0))
            link(pool.memset(zeros3[:, :], 0.0))
            link(pool.memset(ones3[:, :], 1.0))
            pool.sem_inc(masks, 1)
            link(pool.memset(Q[:, :, :, :], 0.0))
            link(pool.memset(Vg[:, :, :, :], 0.0))
            link(pool.memset(Vg[:, :, :, HD:HD + 1], 1.0))
            link(pool.memset(Vw[:, :, :, SE:SE + 1], 1.0))
            link(pool.memset(ones1[:, :], 1.0))
            link(pool.memset(eps8[:, :], 1e-8))
            for t in (ident, flip, identb):
                link(pool.memset(t[:, :], 0.0))
            select(ident[:, :], [[-1, P]], 0, 1, 1.0, ALU.not_equal)
            select(identb[:, :], [[-1, P]], 0, 1, 1.0, ALU.not_equal)
            select(flip[:, :], [[1, P]], 1 - P, 1, 1.0, ALU.not_equal)
            for t, width, step_, lo in ((blk, SH, SE, 0), (half0, 4, 2 * SE, 0), (half1, 4, 2 * SE, SE)):
                link(pool.memset(t[:, :], 1.0))
                select(t[:, :], [[-step_, width]], -lo, 1, 0.0)
                select(t[:, :], [[step_, width]], lo + SE - 1, -1, 0.0)
            link(pool.memset(outside[:, :], 0.0))
            link(pool.memset(offself[:, :, :], -1.0))
            for i in range(2):
                o = outside[64 * i:64 * i + 64, :]
                select(o, [[1, P]], 1 - WIN, 1, -BIG)
                select(o, [[-1, P]], 2 * (WIN - 1), -1, -BIG)
                for v in range(2):
                    select(offself[64 * i:64 * i + 64, v, :], [[1, P]], 1 - WIN, 1, 0.0, ALU.not_equal)
            link(pool.memset(offself[0:1, 1, :], 0.0))
            pool.sem_inc(masks, 1)

            def go(work, ba, bp):
                for side, stage, n, k in work:
                    b = ba if side == "a" else bp
                    if stage == "ln1":
                        pool.wait_ge(*xn_a.at(b, 1))
                        pool.tensor_tensor(xa[:, :, :], xa[:, :, :], bob[:, :].unsqueeze(1).broadcast_to([P, NU, P]),
                                           ALU.add).then_inc(xb_a.sem, 1)
                    if stage == "qkv":
                        for w in range(2):
                            pool.wait_ge(*act_a.at(b, w + 1))
                            pool.tensor_tensor(qkf[:, w, :], qkf[:, w, :], pq[:, 3 * w, :], ALU.subtract).then_inc(pool_a.sem, 1)
                        for w in range(2):
                            pool.wait_ge(*act_a.at(b, w + 3))
                            pool.tensor_tensor(pq[:, 3 * w + 2, :], qkf[:, w, :], pq[:, 3 * w + 1, :],
                                               ALU.subtract).then_inc(pool_a.sem, 1)
                    if stage == "proj":
                        pool.wait_ge(*R.moved(b, k + 2))
                        pool.wait_ge(*R.moved(b, k + 3))
                        pool.tensor_tensor(sq[:, :], qh[:, :], qh[:, :], ALU.mult).then_inc(sq_p.sem, 1)
                    if stage == "dist":
                        d = D[:, n % 2, :, :]
                        pool.wait_ge(*d_act.at(b, n + 1))
                        m = offself[:, 1 if n == 0 else 0, :].unsqueeze(1).broadcast_to([P, SH, P])
                        pool.tensor_tensor(d, d, m, ALU.mult).then_inc(d_scaled.sem, 1)
                        pool.wait_ge(*d_scaled.at(b, n + 1))
                        pool.tensor_tensor(d, d, outside[:, :].unsqueeze(1).broadcast_to([P, SH, P]),
                                           ALU.add).then_inc(d_pool.sem, 1)

            with pool.Fori(0, NB) as b:
                go(WORK, b, b)

        @block.tensor
        def _(pe):
            def mm(o, l, r, start=True, stop=True):
                return pe.matmul(o, l, r, start=start, stop=stop)

            pe.wait_ge(loaded, LOADS * 16)
            pe.wait_ge(masks, 2)
            for i in range(4):
                ins = pe.transpose(psum[0][:, P * i:P * i + P], wload[:, i, :], ident[:, :])
            for v in range(2):
                for f in range(3):
                    ins = mm(psum[1][:, 3 * v + f:3 * v + f + 1], rows[0:1, v, f, :], ones1[:, :])
            ins.then_inc(setup_pe, 1)
            pe.wait_ge(u_spread, 1)
            pe.transpose(psum[3][0:32, 0:P], ub[:, :, :].rearrange("p h r -> p (h r)"), ident[:, :]).then_inc(setup_pe, 1)
            pe.wait_ge(u_turned, 1)
            mm(psum[2][:, 0:SE], uT[:, :], vh[:, :]).then_inc(setup_pe, 1)

            def transposed(ring, b, k, src, perm, order):
                for i in range(2):
                    pe.wait_ge(*ring.free(b, k + i))
                    for q in range(4):
                        ins = pe.transpose(ring.bank(k + i)[:, P * q:P * q + P], src[:, order(4 * i + q), :], perm)
                    ins.then_inc(ring.ready.sem, 1)

            def one(ring, b, k, products):
                pe.wait_ge(*ring.free(b, k))
                for o, l, r, start, stop in products:
                    ins = mm(o, l, r, start, stop)
                ins.then_inc(ring.ready.sem, 1)

            def pv_step(b, n, i):
                s = STEPS * n + i
                pe.wait_ge(*probs.at(b, 4 * (s + 1)))
                if i % 8 == 0:
                    pe.wait_ge(*o_out.at(b, 2 * n + i // 8))
                for j in range(4):
                    ins = mm(ov_bank[VW * j:VW * j + VW, :], Vg[:, i % 8, 4 * n + j, :], PT[:, (4 * s + j) % 8, :],
                             i % 8 == 0, i % 8 == 7)
                ins.then_inc(pv.sem, 1)

            def go(work, ba, bp):
                for side, stage, n, k in work:
                    b = ba if side == "a" else bp
                    if stage == "ln1":
                        pe.wait_ge(*xn_a.at(b, 1))
                        transposed(A, b, k, xna, ident[:, :], lambda u: u)
                    if stage == "qkv":
                        pe.wait_ge(*A.moved(b, k - 2))
                        pe.wait_ge(*A.moved(b, k - 1))
                        for w in range(2):
                            for h in range(2):
                                use = k + 2 * w + h
                                one(A, b, use, [(A.bank(use)[:, :], wT[:, w, :], xTa[:, HALF * h:HALF * h + HALF], True, True)])
                        for i in range(2):
                            use = k + 4 + i
                            one(A, b, use, [(A.bank(use)[:, P * q:P * q + P], xTa[:, P * (4 * i + q):P * (4 * i + q) + P],
                                             wT[:, 2, :], True, True) for q in range(4)])
                    if stage == "max":
                        n, i = n
                        if i == 0:
                            pe.wait_ge(*quad_in.at(b, n + 1))
                        for y in range(4):
                            j, qt, h = (4 * i + y) // 16, (4 * i + y) // 2 % 8, y % 2
                            one(A, b, k + y, [(A.bank(k + y)[:, :], Q[:, n % 2, j // 2, P * qt:P * qt + P],
                                               K[:, n % 2, j, HALF * h:HALF * h + HALF], True, True)])
                    if stage == "mrow":
                        pe.wait_ge(*m_red.at(b, n + 1))
                        pe.wait_ge(*A.free(b, k))
                        pe.transpose(A.bank(k)[0:PARTS * 32, 0:P // 2].bitcast(BF16), mb[:, :], identb[:, :]).then_inc(A.ready.sem, 1)
                    if stage == "exp":
                        n, i = n
                        if i == 0:
                            pe.wait_ge(*m_in.at(b, n + 1))
                        for j in range(4):
                            g = 4 * (STEPS * n + i) + j
                            pe.wait_ge(*probs.at(b, max(g - 2, 0)))
                            ins = mm(st_bank[g % 3][:, :], K[:, n % 2, j, P * (i % 8):P * (i % 8) + P],
                                     Q[:, n % 2, j // 2, HALF * (i // 8):HALF * (i // 8) + HALF])
                            ins.then_inc(scores.sem, 1)
                        if i >= 1:
                            pv_step(b, n, i - 1)
                    if stage == "fin":
                        pv_step(b, n, STEPS - 1)
                    if stage == "otr":
                        if n == 0:
                            pe.wait_ge(*o_out.at(b, 2 * NQUAD))
                        pe.wait_ge(*A.free(b, k))
                        for q in range(NQUAD):
                            ins = pe.transpose(A.bank(k)[:, P * q:P * q + P], oT[:, q, P * n:P * n + P], ident[:, :])
                        ins.then_inc(A.ready.sem, 1)
                        pe.wait_ge(*A.moved(b, k))
                        pe.wait_ge(*A.free(b, k + 1))
                        pe.transpose(A.bank(k + 1)[:, 0:P], on[:, :], ident[:, :]).then_inc(A.ready.sem, 1)
                        pe.wait_ge(*A.moved(b, k + 1))
                        one(A, b, k + 2, [(A.bank(k + 2)[:, 0:P], onT[:, :], wT[:, 3, :], True, True)])
                    if stage == "ln":
                        pe.wait_ge(*xn_p.at(b, n + 1))
                        transposed(R, b, k, xn, ident[:, :], lambda u: u)
                    if stage == "ffn":
                        cols_ = slice(HALF * (n % 2), HALF * (n % 2) + HALF)
                        if n % 2 == 0:
                            pe.wait_ge(*R.moved(b, k - 2))
                            pe.wait_ge(*R.moved(b, k - 1))
                        for o in range(FC):
                            one(R, b, k + o, [(R.bank(k + o)[:, :], W0[:, P * o:P * o + P], xT[:, cols_], True, True)])
                        pe.wait_ge(*R.moved(b, k + 2))
                        pe.wait_ge(*R.moved(b, k + 3))
                        for o in range(FC):
                            use = k + 4 + o
                            one(R, b, use, [(R.bank(use)[:, :], W1[:, c, P * o:P * o + P], h1[:, c, :], c == 0, c == FC - 1)
                                            for c in range(FC)])
                        pe.wait_ge(*R.moved(b, k + 6))
                        pe.wait_ge(*R.moved(b, k + 7))
                        one(R, b, k + 8, [(R.bank(k + 8)[:, P * q:P * q + P], h2[:, c, P * q:P * q + P], W2[:, c, :],
                                           c == 0, c == FC - 1) for q in range(4) for c in range(FC)])
                    if stage == "proj":
                        transposed(R, b, k, xn, flip[:, :], lambda u: NU - 1 - u)
                        for h in range(2):
                            one(R, b, k + 2 + h, [(R.bank(k + 2 + h)[:, :], eq[:, :], xT[:, HALF * h:HALF * h + HALF], True, True)])
                        pe.wait_ge(*sig_p.at(b, 1))
                        one(R, b, k + 4, [(R.bank(k + 4)[0:P // 2, 0:1], w1m[:, :], sig[:, 3:4], True, True)])
                        pe.wait_ge(*R.moved(b, k + 4))
                        one(R, b, k + 5, [(R.bank(k + 5)[:, f:f + 1], w2d[:, f, :], hid[:, :], True, True) for f in range(3)])
                        for f in range(2):
                            for h in range(2):
                                use = k + 6 + 2 * f + h
                                one(R, b, use, [(R.bank(use)[:, :], eqd[:, f, :], xT[:, HALF * h:HALF * h + HALF], True, True)])
                        pe.wait_ge(*R.moved(b, k))
                        pe.wait_ge(*R.moved(b, k + 1))
                        for f in range(2):
                            for h in range(2):
                                use = k + 10 + 2 * f + h
                                one(R, b, use, [(R.bank(use)[:, :], eqd[:, f, :], xrev[:, HALF * h:HALF * h + HALF], True, True)])
                        pe.wait_ge(*xpad.at(b, 1))
                        one(R, b, k + 14, [(R.bank(k + 14)[:, WIN * f:WIN * f + WIN], eqd[:, f, :], xrev[:, T:RPAD], True, True)
                                           for f in range(2)])
                        pe.wait_ge(*met_p.at(b, 1))
                        pe.wait_ge(*sq_p.at(b, 1))
                        one(R, b, k + 15, [(R.bank(k + 15)[:, 16 * u:16 * u + 16], sq[:, P * u:P * u + P], nb[:, :], True, True)
                                           for u in range(NU)])
                        for i in range(2):
                            one(R, b, k + 16 + i, [(R.bank(k + 16 + i)[:, P * q:P * q + P], xT[:, P * (4 * i + q):P * (4 * i + q) + P],
                                                    eq[:, :], True, True) for q in range(4)])
                        for i in range(2):
                            one(R, b, k + 18 + i, [(R.bank(k + 18 + i)[:, P * q:P * q + P], qh[:, P * (4 * i + q):P * (4 * i + q) + P],
                                                    bdh[:, :, :], True, True) for q in range(4)])
                        for i in range(4):
                            one(R, b, k + 20 + i, [(R.bank(k + 20 + i)[:, P * q:P * q + P], xrev[:, window(4 * i + q)],
                                                    ev[:, :], True, True) for q in range(4)])
                    if stage == "dist":
                        pe.wait_ge(*aop_p.at(b, n + 1))
                        if n == 0:
                            pe.wait_ge(*bop.at(b, 2))
                        for f in range(2):
                            one(R, b, k + f, [(R.bank(k + f)[BLK * i:BLK * i + BLK, P * j:P * j + P],
                                               Aop[:, 4 * f + j, BLK * i:BLK * i + BLK], B[:, f, window(2 * n + i)], True, True)
                                              for j in range(4) for i in range(2)])
                    if stage == "ctx":
                        pe.wait_ge(*w_v.at(b, n + 1))
                        for i in range(2):
                            pe.wait_ge(*R.free(b, k + i))
                            for q in range(4):
                                ins = pe.transpose(R.bank(k + i)[:, P * q:P * q + P], E[:, n % 2, 4 * i + q, :], ident[:, :])
                            ins.then_inc(R.ready.sem, 1)
                        pe.wait_ge(*R.moved(b, k))
                        pe.wait_ge(*R.moved(b, k + 1))
                        if n == 0:
                            pe.wait_ge(*R.moved(b, k_vw + 3))
                            pe.wait_ge(*R.moved(b, k_vw + 2))
                        one(R, b, k + 2, [(R.bank(k + 2)[BLK * i:BLK * i + BLK, 32 * h:32 * h + SE + 1], WT[:, h, BLK * i:BLK * i + BLK],
                                           Vw[:, 2 * n + i, h, :], True, True) for h in range(SH) for i in range(2)])
                        pe.wait_ge(*s_v.at(b, n + 1))
                        pe.wait_ge(*R.free(b, k + 3))
                        pe.transpose(R.bank(k + 3)[:, 0:P], s_tok[:, :], ident[:, :]).then_inc(R.ready.sem, 1)
                        pe.wait_ge(*R.moved(b, k + 3))
                        one(R, b, k + 4, [(R.bank(k + 4)[:, 0:P], s_T[:, :], dec[:, :], True, True)])

            pe.wait_ge(setup_v, 1)
            with pe.Fori(0, NB) as b:
                go(WORK, b, b)

        @block.scalar
        def _(act):
            def evict(ring, b, k, dst, src, func=ACT.Identity, **kw):
                act.wait_ge(*ring.filled(b, k))
                return act.activation(dst, src, func, **kw).then_inc(ring.emptied(k), 1)

            def copy_out(b, n, h):
                act.wait_ge(*pv.at(b, STEPS * n + 8 * (h + 1)))
                act.activation(oT[:, n, HALF * h:HALF * h + HALF], ov_bank[:, :], ACT.Identity).then_inc(o_out.sem, 1)

            act.wait_ge(setup_v, 1)
            act.preload_act_table_set(EXP_LN)

            def go(work, ba, bp):
                for side, stage, n, k in work:
                    b = ba if side == "a" else bp
                    if stage in ("ln1", "ln"):
                        ring, l, dst = (A, ls[:, 0], xTa) if stage == "ln1" else (R, ls[:, 1], xT)
                        var, ln, rs, i = (var_a, ln_a, rs_a, 1) if stage == "ln1" else (var_p, ln_p, rs_p, n + 1)
                        act.wait_ge(*var.at(b, i))
                        act.activation(l[:, 1, :], l[:, 0, :], ACT.Ln).then_inc(ln.sem, 1)
                        act.wait_ge(*ln.at(b, i))
                        act.activation(l[:, 2, :], l[:, 1, :], ACT.Exp, scale=-0.5).then_inc(rs.sem, 1)
                        for i in range(2):
                            evict(ring, b, k + i, dst[:, HALF * i:HALF * i + HALF], ring.bank(k + i)[:, :])
                    if stage == "qkv":
                        for w in range(2):
                            for h in range(2):
                                evict(A, b, k + 2 * w + h, qkf[:, w, HALF * h:HALF * h + HALF], A.bank(k + 2 * w + h)[:, :],
                                      bias=wqkb[:, w:w + 1], scale=SCALE if w == 0 else 1.0)
                            act.wait_ge(*A.moved(b, k + 2 * w))
                            act.wait_ge(*A.moved(b, k + 2 * w + 1))
                            if w == 0:
                                act.wait_ge(*split_out.at(b, 0))
                            act.activation(pq[:, 3 * w, :], qkf[:, w, :], ACT.Identity).then_inc(act_a.sem, 1)
                        for w in range(2):
                            act.wait_ge(*pool_a.at(b, w + 1))
                            act.activation(pq[:, 3 * w + 1, :], qkf[:, w, :], ACT.Identity).then_inc(act_a.sem, 1)
                    if stage == "mrow":
                        act.wait_ge(*m_out.at(b, n))
                        evict(A, b, k, mT[:, :], A.bank(k)[0:PARTS * 32, 0:P // 2].bitcast(BF16))
                    if stage == "exp":
                        n, i = n
                        s = STEPS * n + i
                        act.wait_ge(*pv.at(b, max(s - 1, 0)))
                        for j in range(4):
                            act.wait_ge(*scores.at(b, 4 * s + j + 1))
                            act.activation(PT[:, (4 * s + j) % 8, :], st_bank[(4 * s + j) % 3][:, :], ACT.Exp).then_inc(probs.sem, 1)
                        if i == 8:
                            copy_out(b, n, 0)
                    if stage == "fin":
                        copy_out(b, n, 1)
                    if stage == "otr":
                        evict(A, b, k + 1, onT[:, :], A.bank(k + 1)[:, 0:P])
                    if stage == "ffn":
                        for o in range(FC):
                            evict(R, b, k + o, h1[:, o, :], R.bank(k + o)[:, :], ACT.Relu, scale=scol[:, 0:1])
                        for o in range(FC):
                            evict(R, b, k + 4 + o, h2[:, o, :], R.bank(k + 4 + o)[:, :], ACT.Relu, scale=scol[:, 1:2])
                    if stage == "proj":
                        for i in range(2):
                            evict(R, b, k + i, xrev[:, HALF * i:HALF * i + HALF], R.bank(k + i)[:, :])
                        for h in range(2):
                            act.wait_ge(*R.filled(b, k + 2 + h))
                            act.activation(qh[:, HALF * h:HALF * h + HALF], R.bank(k + 2 + h)[:, :], ACT.Relu,
                                           accum_out=sig[:, h:h + 1]).then_inc(R.emptied(k + 2 + h), 1)
                        evict(R, b, k + 4, hid[:, :], R.bank(k + 4)[0:P // 2, 0:1], ACT.Gelu, bias=b1m[:, :])
                        act.preload_act_table_set(EXP_LN)
                        act.wait_ge(*met_z.at(b, 1))
                        act.activation(met[:, 3, :], met[:, 2, :], ACT.Exp, scale=-1.0).then_inc(met_e.sem, 1)
                        act.wait_ge(*met_e.at(b, 1))
                        act.activation(met[:, 4, :], met[:, 3, :], ACT.Ln, bias=1.0).then_inc(met_l.sem, 1)
                        for f in range(2):
                            for h in range(2):
                                use = k + 6 + 2 * f + h
                                evict(R, b, use, qd[:, f, HALF * h:HALF * h + HALF], R.bank(use)[:, :], ACT.Relu)
                        for f in range(2):
                            for h in range(2):
                                use = k + 10 + 2 * f + h
                                evict(R, b, use, B[:, f, HALF * h:HALF * h + HALF], R.bank(use)[:, :], ACT.Relu)
                        evict(R, b, k + 14, B[:, :, T:RPAD], R.bank(k + 14)[:, 0:2 * WIN].rearrange("p (f w) -> p f w", f=2), ACT.Relu)
                        evict(R, b, k + 15, an[:, :, :], R.bank(k + 15)[:, 0:P].rearrange("p (u h) -> p u h", u=NU))
                        for i in range(2):
                            evict(R, b, k + 16 + i, qtok[:, 4 * i:4 * i + 4, :], rows_of(R.bank(k + 16 + i), P), ACT.Relu)
                        act.wait_ge(*gn_v.at(b, 1))
                        act.activation(gn[:, 1, :, :], gn[:, 0, :, :], ACT.Ln).then_inc(gn_l.sem, 1)
                        act.wait_ge(*gn_l.at(b, 1))
                        act.activation(gn[:, 1, :, :], gn[:, 1, :, :], ACT.Exp, scale=-0.5).then_inc(gn_a.sem, 1)
                        for i in range(4):
                            use = k + 20 + i
                            evict(R, b, use, Vw[:, 4 * i:4 * i + 4, :, 0:SE],
                                  R.bank(use)[:, :].rearrange("p (w h e) -> p w h e", w=4, h=SH), ACT.Relu)
                    if stage == "dist":
                        d = D[:, n % 2, :, :]
                        act.wait_ge(*R.moved(b, k))
                        act.wait_ge(*R.moved(b, k + 1))
                        act.activation(d, d, ACT.Relu, scale=-1.0).then_inc(d_act.sem, 1)
                    if stage == "top":
                        e = E[:, n % 2, :, :]
                        act.wait_ge(*d_pool.at(b, n + 1))
                        act.activation(e, D[:, n % 2, :, :], ACT.Ln, scale=-1.0, bias=eps8[:, :]).then_inc(e_steps.sem, 1)
                        act.wait_ge(*e_steps.at(b, 2 * n + 1))
                        act.activation(e, e, ACT.Exp, scale=0.5).then_inc(e_steps.sem, 1)
                        act.wait_ge(*e_steps.at(b, 2 * n + 2))
                        act.activation(e, e, ACT.Exp, scale=-1.0).then_inc(e_act.sem, 1)
                    if stage == "ctx":
                        for i in range(2):
                            evict(R, b, k + i, WT[:, 4 * i:4 * i + 4, :], rows_of(R.bank(k + i), P))
                        evict(R, b, k + 3, s_T[:, :], R.bank(k + 3)[:, 0:P])

            with act.Fori(0, NB) as b:
                go(WORK, b, b)

        @block.vector
        def _(dve):
            setup_step = sem("vector_setup")
            done = [0]

            def then(ins):
                done[0] += 1
                ins.then_inc(setup_step, 1)
                dve.wait_ge(setup_step, done[0])

            dve.wait_ge(loaded, LOADS * 16)
            dve.wait_ge(loadk, 48)
            dve.wait_ge(masks, 2)
            then(dve.tensor_copy(kf, kb0))
            then(dve.tensor_tensor(kf[:, 0, :], kf[:, 0, :], kf[:, 1, :], ALU.subtract))
            then(dve.tensor_scalar(W0[:, :], kf[:, 0, :], 2.0, None, ALU.mult))
            then(dve.tensor_scalar(W1[:, :, :], kb1, 2.0, -1.0, ALU.mult, ALU.add))
            then(dve.tensor_scalar(W2[:, :, :], kb2, 2.0, -1.0, ALU.mult, ALU.add))
            then(dve.tensor_scalar(scol[:, 0:2], scol[:, 0:2], 2.0, None, ALU.mult))
            then(dve.tensor_scalar(wqkb[:, 0:1], wqkb[:, 0:1], SCALE, None, ALU.mult))
            then(dve.tensor_reduce(any0[:, :], half0[:, :], AX.X, ALU.add))
            then(dve.tensor_reduce(any1[:, :], half1[:, :], AX.X, ALU.add))
            then(dve.tensor_scalar(minus1[:, :], half1[:, :], -1.0, None, ALU.mult))
            dve.wait_ge(setup_pe, 1)
            then(dve.tensor_copy(wT[:, :, :], rows_of(psum[0], P)))
            then(dve.tensor_copy(cols[:, :, :], psum[1][:, 0:6].rearrange("p (v f) -> p v f", v=2)))
            dve.tensor_tensor(ub[:, :, :], up[:, :].unsqueeze(1).broadcast_to([P, SH, 4]), cast(blk[:, :], [P, SH, 4]),
                              ALU.mult).then_inc(u_spread, 1)
            dve.wait_ge(setup_pe, 2)
            dve.tensor_copy(uT[:, :], psum[3][0:32, 0:P]).then_inc(u_turned, 1)
            dve.wait_ge(setup_pe, 3)
            then(dve.tensor_copy(bdh[:, :, :], psum[2][:, 0:SE].unsqueeze(1).broadcast_to([P, SH, SE])))
            then(dve.tensor_tensor(bdh[:, :, :], bdh[:, :, :], cast(blk[:, :], [P, SH, SE]), ALU.mult))
            then(dve.tensor_copy(nb[:, 0:SH], blk[:, :]))
            dve.sem_inc(setup_v, 1)

            def norm(b, i, link, side, src, dst, var, rs, done_):
                l, st, m = ls[:, side], stat[:, side], mv[:, side]
                for u in range(NU):
                    ins = dve.bn_stats(st[:, u, :], src[:, u, :])
                link(ins, before_aggr=True)
                for u in range(NU):
                    ins = dve.bn_aggr(m[:, u, :], st[:, u, :])
                link(ins)
                dve.tensor_scalar(l[:, 0, :], m[:, :, 1], LN_EPS, None, ALU.add).then_inc(var.sem, 1)
                dve.wait_ge(*rs.at(b, i))
                link(dve.tensor_tensor(l[:, 3, :], l[:, 2, :], l[:, 2, :], ALU.mult))
                link(dve.tensor_tensor(l[:, 4, :], l[:, 3, :], l[:, 0, :], ALU.mult))
                link(dve.tensor_scalar(l[:, 5, :], l[:, 4, :], -0.5, 1.5, ALU.mult, ALU.add))
                link(dve.tensor_tensor(l[:, 6, :], l[:, 5, :], l[:, 2, :], ALU.mult))
                link(dve.scalar_tensor_tensor(out=l[:, 7, :], in0=m[:, :, 0], scalar=-1.0, in1=l[:, 6, :],
                                              op0=ALU.mult, op1=ALU.mult))
                for u in range(NU):
                    ins = dve.tensor_scalar(dst[:, u, :], src[:, u, :], l[:, 6, u:u + 1], l[:, 7, u:u + 1], ALU.mult, ALU.add)
                ins.then_inc(done_.sem, 1)

            def go(work, ba, bp):
                count_ = {"a": 0, "p": 0}
                for side, stage, n, k in work:
                    b = ba if side == "a" else bp

                    def link(ins, side=side, b=b, before_aggr=False):
                        count_[side] += 1
                        ins.then_inc(links[side].sem, 1)
                        dve.wait_ge(*links[side].at(b, count_[side]))
                        if before_aggr:
                            pass_waits(dve)

                    if stage == "ln1":
                        dve.wait_ge(*x_in.at(b, 1))
                        norm(b, 1, link, 0, xa, xna, var_a, rs_a, xn_a)
                    if stage == "qkv":
                        for i in range(2):
                            dve.wait_ge(*A.filled(b, k + 4 + i))
                            dve.tensor_tensor(Vg[:, 4 * i:4 * i + 4, :, 0:HD],
                                              A.bank(k + 4 + i)[:, :].rearrange("p (t h d) -> p t h d", t=4, d=HD),
                                              bvb[:, :].rearrange("p (h d) -> p h d", d=HD).unsqueeze(1).broadcast_to([P, 4, NH, HD]),
                                              ALU.add).then_inc(A.emptied(k + 4 + i), 1)
                    if stage == "max":
                        n, i = n
                        for y in range(4):
                            j, qt, h = (4 * i + y) // 16, (4 * i + y) // 2 % 8, y % 2
                            dve.wait_ge(*A.filled(b, k + y))
                            c = (2 * (j % 2) + j // 2) * NU + qt
                            dve.tensor_reduce(mred[:, c, h:h + 1], A.bank(k + y)[:, :], AX.X, ALU.max).then_inc(A.emptied(k + y), 1)
                    if stage == "mrow":
                        dve.wait_ge(*A.moved(b, k - 1))
                        dve.wait_ge(*A.moved(b, k - 2))
                        link(dve.tensor_reduce(nm[:, 0, :], mred[:, :, :], AX.X, ALU.max, negate=True))
                        link(dve.tensor_copy(mb[:, 0, :], nm[:, 0, :]))
                        link(dve.tensor_tensor(nm[:, 1, :], nm[:, 0, :], mb[:, 0, :], ALU.subtract))
                        link(dve.tensor_copy(mb[:, 1, :], nm[:, 1, :]))
                        dve.tensor_tensor(mb[:, 2, :], nm[:, 1, :], mb[:, 1, :], ALU.subtract).then_inc(m_red.sem, 1)
                    if stage == "otr":
                        dve.wait_ge(*A.filled(b, k))
                        ps = rows_of(A.bank(k), VW)
                        link(dve.reciprocal(rden[:, :], ps[:, :, HD]))
                        dve.tensor_tensor(on[:, :].rearrange("p (h d) -> p h d", d=HD), ps[:, :, 0:HD],
                                          cast(rden[:, :], [P, NH, HD]), ALU.mult).then_inc(A.emptied(k), 1)
                        dve.wait_ge(*A.filled(b, k + 2))
                        if n == 0:
                            dve.wait_ge(*xb_a.at(b, 1))
                            dve.wait_ge(*out_p.at(b, 0))
                        dve.tensor_tensor(xr[:, n, :], A.bank(k + 2)[:, 0:P], xa[:, n, :], ALU.add).then_inc(A.emptied(k + 2), 1)
                    if stage == "ln":
                        if n == 0:
                            dve.wait_ge(*A.moved(b, NA - 1))
                        else:
                            dve.wait_ge(*R.moved(b, k - 1))
                        norm(b, n + 1, link, 1, xr, xn, var_p, rs_p, xn_p)
                    if stage == "ffn":
                        dve.wait_ge(*R.filled(b, k + 8))
                        dst = xr[:, 4 * (n % 2):4 * (n % 2) + 4, :]
                        dve.scalar_tensor_tensor(out=dst, in0=rows_of(R.bank(k + 8), P), scalar=scol[:, 2:3], in1=dst,
                                                 op0=ALU.mult, op1=ALU.add).then_inc(R.emptied(k + 8), 1)
                    if stage == "proj":
                        dve.wait_ge(*R.moved(b, k + 1))
                        dve.tensor_copy(xrev[:, T:RPAD], xrev[:, T - 1:T].broadcast_to([P, WIN])).then_inc(xpad.sem, 1)
                        dve.wait_ge(*R.moved(b, k + 2))
                        dve.wait_ge(*R.moved(b, k + 3))
                        link(dve.tensor_reduce(sig[:, 2:3], qh[:, 0:T:8], AX.X, ALU.add))
                        link(dve.tensor_tensor(sig[:, 0:1], sig[:, 0:1], sig[:, 1:2], ALU.add))
                        link(dve.scalar_tensor_tensor(out=sig[:, 0:1], in0=sig[:, 2:3], scalar=4.0, in1=sig[:, 0:1],
                                                      op0=ALU.mult, op1=ALU.add))
                        dve.tensor_scalar(sig[:, 3:4], sig[:, 0:1], 1.0 / T, None, ALU.mult).then_inc(sig_p.sem, 1)
                        dve.wait_ge(*R.filled(b, k + 5))
                        dve.tensor_tensor(met[:, 1, :], R.bank(k + 5)[:, 0:3], cols[:, 0, :], ALU.add).then_inc(R.emptied(k + 5), 1)
                        dve.wait_ge(*R.moved(b, k + 5))
                        link(dve.scalar_tensor_tensor(out=met[:, 0, :], in0=met[:, 1, :], scalar=0.1, in1=cols[:, 1, :],
                                                      op0=ALU.mult, op1=ALU.add))
                        link(dve.tensor_scalar(met[:, 1, :], met[:, 0, :], -1.0, None, ALU.mult))
                        dve.tensor_tensor(met[:, 2, :], met[:, 0, :], met[:, 1, :], ALU.max).then_inc(met_z.sem, 1)
                        dve.wait_ge(*met_l.at(b, 1))
                        link(dve.scalar_tensor_tensor(out=met[:, 5, :], in0=met[:, 0, :], scalar=0.0, in1=met[:, 4, :],
                                                      op0=ALU.max, op1=ALU.add))
                        for f in range(2):
                            dve.tensor_scalar(alpha[:, 4 * f:4 * f + 4], half0[:, :], met[:, 5, f:f + 1], 2.0, ALU.mult, ALU.mult)
                        dve.tensor_scalar(beta[:, :], met[:, 5, 0:2], any1[:, :], None, ALU.mult)
                        link(dve.tensor_scalar(nb[:, SH:2 * SH], blk[:, :], met[:, 5, 2:3], None, ALU.mult))
                        dve.sem_inc(met_p.sem, 1)
                        dve.wait_ge(*R.moved(b, k + 13))
                        dve.wait_ge(*R.moved(b, k + 12))
                        dve.wait_ge(*R.moved(b, k + 14))
                        for f in range(2):
                            link(dve.tensor_scalar(Bs[:, :], B[:, f, :], beta[:, f:f + 1], any0[:, :], ALU.mult, ALU.add))
                            dve.tensor_tensor(B[:, f, :], Bs[:, :], B[:, f, :], ALU.mult).then_inc(bop.sem, 1)
                            dve.wait_ge(*bop.at(b, f + 1))
                        dve.wait_ge(*R.moved(b, k + 15))
                        dve.tensor_scalar(gn[:, 0, :, :], an[:, :, 0:SH], 1e-4, None, ALU.max).then_inc(gn_v.sem, 1)
                        link(dve.tensor_scalar(gn[:, 2, :, :], an[:, :, 0:SH], 0.04, 0.1, ALU.is_gt, ALU.mult))
                        dve.wait_ge(*gn_a.at(b, 1))
                        link(dve.tensor_tensor(gn[:, 2, :, :], gn[:, 2, :, :], gn[:, 1, :, :], ALU.mult))
                        for i in range(2):
                            dve.wait_ge(*R.filled(b, k + 18 + i))
                            dve.tensor_tensor(hb[:, 4 * i:4 * i + 4, :].rearrange("p u (h e) -> p (u h) e", e=SE),
                                              rows_of(R.bank(k + 18 + i), SE),
                                              cast(gn[:, 2, 4 * i:4 * i + 4, :].rearrange("p u h -> p (u h)"), [P, 4 * SH, SE]),
                                              ALU.mult).then_inc(R.emptied(k + 18 + i), 1)
                    if stage == "dist":
                        if n == 0:
                            dve.wait_ge(*R.moved(b, k_qd))
                            dve.wait_ge(*R.moved(b, k_qd + 1))
                        else:
                            dve.wait_ge(*R.filled(b, k - 1))
                        for h in range(SH):
                            ins = dve.tensor_scalar(Aop[:, h, :], qd[:, h // 4, P * n:P * n + P], alpha[:, h:h + 1],
                                                    minus1[:, h % 4:h % 4 + 1], ALU.mult, ALU.add)
                        ins.then_inc(aop_p.sem, 1)
                        for f in range(2):
                            dve.wait_ge(*R.filled(b, k + f))
                            dve.tensor_tensor(D[:, n % 2, 4 * f:4 * f + 4, :], rows_of(R.bank(k + f), P),
                                              cast(an[:, n, SH + 4 * f:SH + 4 * f + 4], [P, 4, P]),
                                              ALU.subtract).then_inc(R.emptied(k + f), 1)
                    if stage == "top":
                        dve.wait_ge(*d_pool.at(b, n + 1))
                        pass_waits(dve)
                        half = SH // 2
                        for r in range(TOPK // 8):
                            for h in range(SH):
                                src = D[:, n % 2, h, :] if r == 0 else Rm[:, h, :]
                                if r > 0 and h % half == 0:
                                    dve.wait_ge(*top8.at(b, (4 * n + r) * 2 * SH - SH + h + half))
                                    pass_waits(dve)
                                dve.max(out=m8[:, h, :], in_=src).then_inc(top8.sem, 1)
                            for h in range(SH):
                                src = D[:, n % 2, h, :] if r == 0 else Rm[:, h, :]
                                if h % half == 0:
                                    dve.wait_ge(*top8.at(b, (4 * n + r) * 2 * SH + h + half))
                                    pass_waits(dve)
                                dve.match_replace(out=Rm[:, h, :], in_to_replace=m8[:, h, :], in_values=src,
                                                  imm_value=-2 * BIG).then_inc(top8.sem, 1)
                        dve.wait_ge(*top8.at(b, (n + 1) * 8 * SH))
                        dve.wait_ge(*e_act.at(b, n + 1))
                        dve.scalar_tensor_tensor(out=E[:, n % 2, :, :], in0=Rm[:, :, :], scalar=-1.5 * BIG, in1=E[:, n % 2, :, :],
                                                 op0=ALU.is_lt, op1=ALU.mult).then_inc(w_v.sem, 1)
                    if stage == "ctx":
                        dve.wait_ge(*R.filled(b, k + 2))
                        ps = R.bank(k + 2)[:, 0:32 * SH].rearrange("p (h e) -> p h e", h=SH)
                        link(dve.tensor_scalar(rd[:, 0, :], ps[:, :, SE], 1e-8, None, ALU.add))
                        link(dve.reciprocal(rd[:, 1, :], rd[:, 0, :]))
                        s3 = s_tok[:, :].rearrange("p (h e) -> p h e", e=SE)
                        dve.tensor_tensor(s3, ps[:, :, 0:SE], cast(rd[:, 1, :], [P, SH, SE]), ALU.mult).then_inc(R.emptied(k + 2), 1)
                        dve.wait_ge(*R.moved(b, k + 2))
                        link(dve.tensor_tensor(s_tok[:, :], s_tok[:, :], hb[:, n, :], ALU.add))
                        dve.tensor_tensor(s_tok[:, :], s_tok[:, :], qtok[:, n, :], ALU.mult).then_inc(s_v.sem, 1)
                        dve.wait_ge(*R.filled(b, k + 4))
                        dve.tensor_tensor(xr[:, n, :], R.bank(k + 4)[:, 0:P], xr[:, n, :], ALU.add).then_inc(R.emptied(k + 4), 1)
                for side, n in count_.items():
                    assert n in (0, links[side].per), (side, n)

            with dve.Fori(0, NB) as b:
                go(WORK, b, b)


def kernel(**inputs):
    import numpy as _np
    import concourse.bacc as _bacc
    from concourse import mybir as _mybir
    from concourse.bass_utils import run_bass_kernel_spmd as _run

    nc = _bacc.Bacc("TRN2", target_bir_lowering=False, num_devices=1)
    arrays, args = {}, {}
    for name, a in inputs.items():
        a = _np.ascontiguousarray(a)
        if a.dtype == _np.bool_:
            a = a.view(_np.uint32)
        if a.ndim == 0:
            a = a.reshape(1)
        short = name.removeprefix("L0_attn_a_").removeprefix("L0_attn_b_").removeprefix("L0_ffn_")
        arrays[f"in_{short}"] = a
        args[short] = nc.dram_tensor(f"in_{short}", a.shape, _mybir.dt.from_np(a.dtype), kind="ExternalInput").ap()
    out = nc.dram_tensor("out", (NB, T, P), F32, kind="ExternalOutput").ap()
    hybrid_block_kernel(
        nc, args["hidden_states"], args["Wq"], args["bq"], args["Wk"], args["bk"], args["Wv"], args["bv"],
        args["Wo"], args["bo"], args["encoder_query"], args["encoder_value"], args["mn_w1"], args["mn_b1"],
        args["mn_w2"], args["mn_b2"], args["base_metric"], args["decoder"], args["hebbian_U"], args["hebbian_V"],
        args["k0"], args["k1"], args["k2"], args["s0"], args["s1"], args["s2"], out)
    r = _run(nc, [arrays], core_ids=[0])
    return r.results[0]["out"]
```

```python
from contextlib import ExitStack

import concourse.bass as bass
from concourse import mybir

F32 = mybir.dt.float32
BF16 = mybir.dt.bfloat16
U8 = mybir.dt.uint8
U32 = mybir.dt.uint32
ALU = mybir.AluOpType
ACT = mybir.ActivationFunctionType
AX = mybir.AxisListType

P = 128
NB, T = 8, 1024
NU = T // P
HALF = 512
NH, HD = 16, 8
NQUAD = NH // 4
SCALE = float(HD) ** -0.5
PARTS = 3
QPART = (0, 0, 0, 1, 1, 2)
KPART = (0, 1, 2, 0, 1, 0)
MROW = len(QPART) * HD
VW = 32
NF, FC = 512, 4
SH, SE = 8, 16
WIN, TOPK, BLK = 64, 32, 32
NBLK = P // BLK
WW = BLK + WIN
RPAD = T + WIN
BIG = 1.0e18
LN_EPS = 1e-5
EXP_LN = "natural_log_exp_and_others"
LOADS = 37
LINKS_A, LINKS_P = 31, 56

STEPS = 16
STAGES_A = [("ln1", 0), ("qkv", 0), ("load", 0)] + [("max", (0, i)) for i in range(STEPS)] + [("mrow", 0)]
for _n in range(NQUAD):
    if _n + 1 < NQUAD:
        STAGES_A.append(("load", _n + 1))
    for _i in range(STEPS):
        STAGES_A.append(("exp", (_n, _i)))
        if _n + 1 < NQUAD:
            STAGES_A.append(("max", (_n + 1, _i)))
    STAGES_A.append(("fin", _n))
    if _n + 1 < NQUAD:
        STAGES_A.append(("mrow", _n + 1))
for _u in range(NU + 2):
    STAGES_A += [(s, _u - d) for d, s in enumerate(("turn", "back", "wo")) if 0 <= _u - d < NU]



def ffn_slots(n):
    return [[(s, (n, o)), (s, (n, o + 1))] for s in ("fa", "fb") for o in (0, 2)] + [[("fc", n)]]


SLOTS_P = [[("ln", 0)], [("lnT", 0)]] + ffn_slots(0) + ffn_slots(1) + [[("ln", 1)], [("lnT", 1)]]
SLOTS_P += [[("flip", 0), ("flip", 1)], [("he", 0), ("he", 1)], [("qd", 0), ("qd", 1)], [("hid", 0), ("qd", 2)],
            [("mod", 0), ("qd", 3)], [("key", 0), ("key", 1)], [("key", 2), ("key", 3)], [("pad", 0), ("an", 0)],
            [("qtok", 0), ("qtok", 1)], [("keys", 0)], [("hebb", 0), ("hebb", 1)], [("dist", 0)]]
for _u in range(NU + 1):
    for _r in range(TOPK // 8):
        _slot = [("top", (_u, _r))] if _u < NU else []
        if _r == 1 and _u + 1 < NU:
            _slot += [("dist", _u + 1)]
        if _u >= 1:
            _slot += [([("vw", _u - 1), ("wt", _u - 1)], [("pv", _u - 1)], [("st", _u - 1)], [("dec", _u - 1)])[_r]]
        SLOTS_P.append([x for y in _slot for x in (y if isinstance(y, list) else [y])])
SLOTS_P += [[("ln", 2)], [("lnT", 2)]] + ffn_slots(2) + ffn_slots(3) + [[("out", 0)]]
USES = dict(ln1=2, qkv=6, max=4, mrow=1, turn=1, back=1, wo=1,
            lnT=2, fa=1, fb=1, fc=1, flip=1, he=1, qd=1, hid=1, mod=1, key=1, pad=1, an=1, qtok=1, hebb=1,
            dist=2, vw=1, wt=2, pv=1, st=1, dec=1)


def numbered(side, stages, uses):
    k, said = 0, []
    for stage, n in stages:
        uses[stage, n] = k
        said.append((side, stage, n, k))
        k += USES.get(stage, 0)
    assert k % 2 == 0
    return said, k


USE_A, USE_P = {}, {}
WORK_A, NA = numbered("a", STAGES_A, USE_A)
WORK_P, NP = numbered("p", [x for slot in SLOTS_P for x in slot], USE_P)


def merged():
    weight = {"max": 1.0, "exp": 1.0, "turn": 0.7, "ln1": 2.0, "qkv": 2.0}
    lead = 0.0
    total = sum(weight.get(x[1], 0.0) for x in WORK_A[:-LAST_A])
    work, p, spent = [], 0, 0.0
    at = 0
    for i, x in enumerate(WORK_A):
        work.append(x)
        spent += weight.get(x[1], 0.0)
        while at < len(SLOTS_P) and (at + 1) * total <= spent * len(SLOTS_P):
            work += WORK_P[p:p + len(SLOTS_P[at])]
            p += len(SLOTS_P[at])
            at += 1
    assert p == len(WORK_P)
    return work


LAST_A = 20
WORK = merged()


class Count:
    made = []

    def __init__(self, sem, per, unit=1):
        self.sem, self.per, self.unit = sem, per, unit
        Count.made.append(sem)

    def at(self, b, k):
        return self.sem, b * (self.per * self.unit) + (k * self.unit + 1)


class Ring:

    def __init__(self, banks, sem, name, uses):
        self.banks = banks
        self.ready = Count(sem(f"{name}_ready"), uses)
        self.evicted = [Count(sem(f"{name}_evicted{i}"), uses // 2) for i in range(2)]

    def bank(self, k):
        return self.banks[k % 2]

    def free(self, b, k):
        return self.evicted[k % 2].at(b, k // 2)

    def filled(self, b, k):
        return self.ready.at(b, k + 1)

    def moved(self, b, k):
        return self.evicted[k % 2].at(b, k // 2 + 1)

    def made(self, b, k, *uses):
        other = [u for u in uses if (u - k) % 2]
        return self.moved(b, max(other)) if other else self.free(b, k)

    def emptied(self, k):
        return self.evicted[k % 2].sem


def hybrid_block_kernel(nc, x, Wq, bq, Wk, bk, Wv, bv, Wo, bo, enc_q, enc_v, mn_w1, mn_b1, mn_w2, mn_b2,
                        base_metric, decoder, heb_U, heb_V, k0, k1, k2, s0, s1, s2, out):
    with ExitStack() as ctx:
        def sb(name, shape, dt=F32):
            return ctx.enter_context(nc.sbuf_tensor(name, shape, dt))

        def sem(name):
            return ctx.enter_context(nc.semaphore(name))

        def count(name, per, unit=1):
            return Count(sem(name), per, unit)

        Count.made.clear()
        psum = [ctx.enter_context(nc.psum_tensor(f"bank{i}", [P, HALF], F32)) for i in range(8)]
        A = Ring(psum[0:2], sem, "a", NA)
        R = Ring(psum[2:4], sem, "p", NP)
        st_bank = psum[4:7]
        ov_bank = psum[7]

        scratch_qk = nc.dram_tensor("scratch_qk", [2 * PARTS, P, T], BF16, kind="Internal").ap()
        scratch_m = nc.dram_tensor("scratch_m", [PARTS * 32, P], BF16, kind="Internal").ap()

        ident = sb("ident", [P, P])
        flip = sb("flip", [P, P])
        identb = sb("identb", [P, P], BF16)
        wT = sb("wT", [P, 4, P])
        wqkb = sb("wqkb", [P, 2])
        bvb = sb("bvb", [P, P])
        bob = sb("bob", [P, P])
        W0 = sb("W0", [P, NF])
        W1 = sb("W1", [P, FC, NF])
        W2 = sb("W2", [P, FC, P])
        scol = sb("scol", [P, 3])
        eq = sb("eq", [P, P])
        ev = sb("ev", [P, P])
        eqd = sb("eqd", [P, 2, P])
        w1m = sb("w1m", [P, P // 2])
        b1m = sb("b1m", [P // 2, 1])
        w2d = sb("w2d", [P // 2, 3, P])
        rows = sb("rows", [1, 2, 3, P])
        cols = sb("cols", [P, 2, 3])
        dec = sb("dec", [P, P])
        up = sb("up", [P, 4])
        ub = sb("ub", [P, SH, 4])
        uT = sb("uT", [32, P])
        vh = sb("vh", [32, SE])
        bdh = sb("bdh", [P, SH, SE])
        blk = sb("blk", [P, SH])
        half0 = sb("half0", [P, 4])
        half1 = sb("half1", [P, 4])
        any0 = sb("any0", [P, 1])
        any1 = sb("any1", [P, 1])
        minus1 = sb("minus1", [P, 4])
        offself = sb("offself", [P, 2, WW])
        outside = sb("outside", [P, WW])
        zeros3 = sb("zeros3", [PARTS, T], BF16)
        ones3 = sb("ones3", [PARTS, T], BF16)
        ones1 = sb("ones1", [1, 1])
        eps8 = sb("eps8", [P, 1])

        xa = sb("xa", [P, NU, P])
        xTa = sb("xTa", [P, T])
        pq = sb("pq", [P, 2 * PARTS, T], BF16)
        xna = pq[:, 0:2, :].bitcast(F32).rearrange("p a (u c) -> p (a u) c", c=P)
        Q = sb("Q", [P, 2, 2, T], BF16)
        K = sb("K", [P, 2, 4, T], BF16)
        Vg = sb("Vg", [P, NU, NH, VW])
        mred = sb("mred", [P, 32, 2])
        nm = sb("nm", [P, 3, 32])
        mb = sb("mb", [P, PARTS, 32], BF16)
        mT = sb("mT", [PARTS * 32, P], BF16)
        PT = sb("PT", [P, 8, HALF])
        oT = sb("oT", [P, NQUAD, T])
        qkf = oT[:, 0:2, :]
        rden = sb("rden", [P, 2, NH])
        on = sb("on", [P, 2, P])
        onT = sb("onT", [P, 2, P])

        xr = sb("xr", [P, NU, P])
        stat = sb("stat", [P, 2, NU, 6])
        mv = sb("mv", [P, 2, NU, 2])
        ls = sb("ls", [P, 2, 8, NU])
        xn = sb("xn", [P, NU, P])
        xT = sb("xT", [P, T])
        h1 = sb("h1", [P, FC, HALF])
        h2 = sb("h2", [P, FC, HALF])
        xrev = sb("xrev", [P, RPAD])
        qd = sb("qd", [P, 2, T])
        B = sb("B", [P, 2, RPAD])
        Bs = sb("Bs", [P, RPAD])
        qh = sb("qh", [P, T])
        sq = sb("sq", [P, T])
        sig = sb("sig", [P, 4])
        hid = sb("hid", [P // 2, 1])
        met = sb("met", [P, 6, 3])
        alpha = sb("alpha", [P, SH])
        beta = sb("beta", [P, 2])
        nb = sb("nb", [P, 16])
        an = sb("an", [P, NU, 16])
        gn = sb("gn", [P, 3, NU, SH])
        qtok = sb("qtok", [P, NU, P])
        hb = sq[:, :].rearrange("p (u c) -> p u c", c=P)
        Vw = sb("Vw", [WW, 2, NBLK, SH, SE + 1])
        Aop = sb("Aop", [P, SH, P])
        D = h1[:, 0:3, :].rearrange("p a c -> p (a c)").rearrange("p (i h c) -> p i h c", i=2, c=WW)
        E = h2[:, 0:3, :].rearrange("p a c -> p (a c)").rearrange("p (i h c) -> p i h c", i=2, c=WW)
        Rm = xn[:, :, 0:WW]
        m8 = sb("m8", [P, SH, 8])
        WT = Bs[:, 0:T].rearrange("p (h c) -> p h c", h=SH)
        rd = sb("rd", [P, 2, SH])
        s_tok = sb("s_tok", [P, P])
        s_T = sb("s_T", [P, P])
        wload = oT[:, 0, :].rearrange("p (a c) -> p a c", a=8)[:, 0:4, :]
        kw0, kw1, kw2 = (PT[:, a:b, 0:w].bitcast(U32) for a, b, w in ((0, 2, P), (2, 6, P), (6, 7, P)))
        kw2 = kw2.rearrange("p o (a c) -> p (o a) c", a=FC)
        kb0, kb1, kb2 = kw0.bitcast(U8), kw1.bitcast(U8), kw2.bitcast(U8)
        kf = h1[:, 0:2, :]

        loaded = sem("weights_loaded")
        loadk = sem("signs_loaded")
        masks = sem("masks_made")
        setup_pe = sem("setup_products")
        setup_v = sem("setup_vector")
        u_spread = sem("u_spread")
        u_turned = sem("u_turned")
        rows_set = sem("one_rows_set")
        waits_passed = sem("waits_passed")
        links = {"a": count("vector_steps_a", LINKS_A), "p": count("vector_steps_p", LINKS_P)}
        x_in = count("x_in", 1, 16)
        ln_a = count("ln_a", 1)
        ln_p = count("ln_p", 3)
        xpad = count("first_repeated", 1)
        met_z = count("metric_in", 1)
        met_e = count("metric_exp", 1)
        met_l = count("metric_ln", 1)
        gn_l = count("gate_ln", 1)
        e_steps = count("e_steps", 2 * NU)
        top8 = count("top8", NU * 8 * SH)
        var_a = count("var_a", 1)
        rs_a = count("rstd_a", 1)
        xn_a = count("xn_a", 1)
        xb_a = count("bias_added", 1)
        act_a = count("part_rounded", 4)
        pool_a = count("part_left", 4)
        split_out = count("split_out", 1, 16)
        quad_in = count("quad_in", NQUAD, 28 * 16)
        m_red = count("max_split", NQUAD)
        m_T = count("max_transposed", NQUAD)
        m_out = count("max_out", NQUAD, 16)
        m_in = count("max_in", NQUAD, 32)
        scores = count("scores", NQUAD * 64)
        probs = count("probs", NQUAD * 64)
        pv = count("pv", NQUAD * 16)
        o_out = count("o_out", NQUAD * 2)
        rd_a = count("rden_a", NU)
        var_p = count("var_p", 3)
        rs_p = count("rstd_p", 3)
        xn_p = count("xn_p", 3)
        sq_p = count("squares", 1)
        sig_p = count("sig_p", 1)
        met_p = count("metric", 1)
        bop = count("b_operand", 2)
        gn_v = count("gate_in", 1)
        gn_a = count("gate_norm", 1)
        aop_p = count("a_operand", NU)
        d_act = count("d_clamped", NU)
        d_scaled = count("d_scaled", NU)
        d_pool = count("d_masked", NU)
        e_act = count("e_done", NU)
        w_v = count("w_done", NU)
        s_v = count("s_done", NU)
        out_p = count("out_done", 1, 16)
        block = ctx.enter_context(nc.Block())

        x_t = x.rearrange("b (u p) c -> b p u c", p=P)
        out_t = out.rearrange("b (u p) c -> b p u c", p=P)
        qk_t = scratch_qk.rearrange("s (h d) t -> s d h t", d=HD)
        m_t = scratch_m.rearrange("(s a i u) t -> s a i (u t)", s=PARTS, a=2, i=2)

        def pass_waits(eng):
            eng.sem_inc(waits_passed, 1)

        def window(w):
            return slice(T - BLK * (w + 1), T - BLK * (w + 1) + WW)

        def rows_of(bank, r):
            return bank[:, :].rearrange("p (a r) -> p a r", r=r)

        def cast(ap, dims):
            return ap.unsqueeze(len(dims) - 1).broadcast_to(dims)

        @block.sync
        def _(sp):
            n = 0

            for s in Count.made:
                sp.sem_inc(s, 1)

            def load(dst, src):
                nonlocal n
                sp.dma_start(dst, src).then_inc(loaded, 16)
                n += 1

            for i, w in enumerate((Wq, Wk, Wv, Wo)):
                load(wload[:, i, :], w)
            load(wqkb[:, 0:1], bq.rearrange("(p o) -> p o", o=1))
            load(wqkb[:, 1:2], bk.rearrange("(p o) -> p o", o=1))
            load(bvb[:, :], bv.partition_broadcast(P))
            load(bob[:, :], bo.partition_broadcast(P))
            for i, s in enumerate((s0, s1, s2)):
                load(scol[:, i:i + 1], s.partition_broadcast(P))
            load(eq[:, :].rearrange("d (n e) -> d n e", e=SE), enc_q.rearrange("n d e -> d n e"))
            load(ev[:, :].rearrange("d (n e) -> d n e", e=SE), enc_v.rearrange("n d e -> d n e"))
            ed = eqd[:, :, :].rearrange("d f (g s e) -> d f g s e", g=4, s=2)
            wd = w2d[:, :, :].rearrange("d f (g s e) -> d f g s e", g=4, s=2)
            rw = rows[:, :, :, :].rearrange("o v f (g s e) -> o v f g s e", g=4, s=2)
            vecs = (mn_b2.rearrange("(o n) -> o n", o=1), base_metric.rearrange("h e -> (h e)").rearrange("(o n) -> o n", o=1))
            for f in range(2):
                for s in range(2):
                    load(ed[:, f, :, s, :], enc_q[4 * f:4 * f + 4].rearrange("n d e -> d n e"))
                    load(wd[:, f, :, s, :], mn_w2[:, 64 * f:64 * f + 64].rearrange("d (g e) -> d g e", e=SE))
                    for v in range(2):
                        load(rw[:, v, f, :, s, :], vecs[v][:, 64 * f:64 * f + 64].rearrange("o (g e) -> o g e", e=SE))
            load(w2d[:, 2, :], mn_w2)
            for v in range(2):
                load(rows[:, v, 2, :], vecs[v])
            load(w1m[:, :], mn_w1)
            load(b1m[:, :], mn_b1.rearrange("(p o) -> p o", o=1))
            load(dec[:, :], decoder)
            load(vh[:, :], heb_V.rearrange("h r e -> (h r) e"))
            load(up[:, :], heb_U.rearrange("h e r -> (h e) r"))
            assert n == LOADS, n
            sp.dma_start(kw0, k0.rearrange("(a p) n -> p a n", p=P)).then_inc(loadk, 16)
            sp.dma_start(kw1, k1.rearrange("(a p) n -> p a n", p=P)).then_inc(loadk, 16)
            sp.dma_start(kw2, k2.rearrange("(a p) n -> p a n", p=P)).then_inc(loadk, 16)
            sp.wait_ge(masks, 1)
            for slot in range(2):
                for j in range(4):
                    r = 64 * (j % 2) + MROW
                    sp.dma_start(K[r:r + PARTS, slot, j, :], ones3[:, :]).then_inc(rows_set, 16)

            def go(work, ba, bp):
                for side, stage, n, k in work:
                    b = ba if side == "a" else bp
                    if stage == "ln1":
                        sp.wait_ge(*A.ready.at(b, 0))
                        pass_waits(sp)
                        sp.wait_ge(*A.moved(b, -1))
                        pass_waits(sp)
                        sp.dma_start(xa[:, :, :], x_t[b]).then_inc(x_in.sem, 16)
                    if stage == "qkv":
                        sp.wait_ge(*act_a.at(b, 4))
                        pass_waits(sp)
                        sp.wait_ge(*pool_a.at(b, 4))
                        pass_waits(sp)
                        sp.wait_ge(*quad_in.at(b, 0))
                        pass_waits(sp)
                        sp.dma_start(scratch_qk.rearrange("s c t -> c s t"), pq[:, :, :]).then_inc(split_out.sem, 16)
                    if stage == "load":
                        slot = n % 2
                        sp.wait_ge(*split_out.at(b, 1))
                        pass_waits(sp)
                        sp.wait_ge(*scores.at(b, 4 * STEPS * max(n - 1, 0)))
                        pass_waits(sp)
                        for par in range(2):
                            for g in range(6):
                                r = 64 * par + HD * g
                                h = slice(4 * n + par, 4 * n + par + 3, 2)
                                sp.dma_start(Q[r:r + HD, slot, :, :], qk_t[QPART[g], :, h, :]).then_inc(quad_in.sem, 16)
                                sp.dma_start(K[r:r + HD, slot, par:par + 3:2, :], qk_t[PARTS + KPART[g], :, h, :]).then_inc(quad_in.sem, 16)
                            r = 64 * par + MROW
                            for i in range(2):
                                sp.dma_start(Q[r:r + PARTS, slot, i, :], zeros3[:, :]).then_inc(quad_in.sem, 16)
                    if stage == "mrow":
                        sp.wait_ge(*A.moved(b, k))
                        pass_waits(sp)
                        sp.wait_ge(*m_in.at(b, n))
                        pass_waits(sp)
                        sp.dma_start(scratch_m, mT[:, :]).then_inc(m_out.sem, 16)
                        sp.wait_ge(*m_out.at(b, n + 1))
                        pass_waits(sp)
                        for par in range(2):
                            r = 64 * par + MROW
                            sp.dma_start(Q[r:r + PARTS, n % 2, :, :], m_t[:, par]).then_inc(m_in.sem, 16)
                    if stage == "out":
                        sp.wait_ge(*R.moved(b, NP - 1))
                        pass_waits(sp)
                        sp.dma_start(out_t[b], xr[:, :, :]).then_inc(out_p.sem, 16)

            sp.wait_ge(rows_set, 16 * 8)
            go(WORK_A, 0, 0)
            with sp.Fori(0, NB - 1) as b:
                go(WORK, b + 1, b)
            go(WORK_P, NB - 1, NB - 1)
            sp.wait_ge(*out_p.at(NB, 0))
            pass_waits(sp)

        @block.gpsimd
        def _(pool):
            def select(dst, pattern, base, mult, fill, op=ALU.is_ge):
                link(pool.affine_select(out=dst, in_=dst, compare_op=op, fill=fill, base=base,
                                        pattern=pattern, channel_multiplier=mult))

            step = sem("pool_setup")
            done = [0]

            def link(ins):
                done[0] += 1
                ins.then_inc(step, 1)
                pool.wait_ge(step, done[0])

            link(pool.memset(K[:, :, :, :], 0.0))
            link(pool.memset(zeros3[:, :], 0.0))
            link(pool.memset(ones3[:, :], 1.0))
            pool.sem_inc(masks, 1)
            link(pool.memset(Q[:, :, :, :], 0.0))
            link(pool.memset(Vg[:, :, :, :], 0.0))
            link(pool.memset(Vg[:, :, :, HD:HD + 1], 1.0))
            link(pool.memset(Vw[:, :, :, :, SE:SE + 1], 1.0))
            link(pool.memset(ones1[:, :], 1.0))
            link(pool.memset(eps8[:, :], 1e-8))
            for t in (ident, flip, identb):
                link(pool.memset(t[:, :], 0.0))
            select(ident[:, :], [[-1, P]], 0, 1, 1.0, ALU.not_equal)
            select(identb[:, :], [[-1, P]], 0, 1, 1.0, ALU.not_equal)
            select(flip[:, :], [[1, P]], 1 - P, 1, 1.0, ALU.not_equal)
            for t, width, step_, lo in ((blk, SH, SE, 0), (half0, 4, 2 * SE, 0), (half1, 4, 2 * SE, SE)):
                link(pool.memset(t[:, :], 1.0))
                select(t[:, :], [[-step_, width]], -lo, 1, 0.0)
                select(t[:, :], [[step_, width]], lo + SE - 1, -1, 0.0)
            link(pool.memset(outside[:, :], 0.0))
            link(pool.memset(offself[:, :, :], -1.0))
            for i in range(NBLK):
                o = outside[BLK * i:BLK * i + BLK, :]
                select(o, [[1, WW]], 1 - BLK, 1, -BIG)
                select(o, [[-1, WW]], WIN + BLK - 2, -1, -BIG)
                for v in range(2):
                    select(offself[BLK * i:BLK * i + BLK, v, :], [[1, WW]], 1 - BLK, 1, 0.0, ALU.not_equal)
            link(pool.memset(offself[0:1, 1, :], 0.0))
            pool.sem_inc(masks, 1)

            def go(work, ba, bp):
                for side, stage, n, k in work:
                    b = ba if side == "a" else bp
                    if stage == "ln1":
                        pool.wait_ge(*xn_a.at(b, 1))
                        pool.tensor_tensor(xa[:, :, :], xa[:, :, :], bob[:, :].unsqueeze(1).broadcast_to([P, NU, P]),
                                           ALU.add).then_inc(xb_a.sem, 1)
                    if stage == "qkv":
                        for w in range(2):
                            pool.wait_ge(*act_a.at(b, w + 1))
                            pool.tensor_tensor(qkf[:, w, :], qkf[:, w, :], pq[:, 3 * w, :], ALU.subtract).then_inc(pool_a.sem, 1)
                        for w in range(2):
                            pool.wait_ge(*act_a.at(b, w + 3))
                            pool.tensor_tensor(pq[:, 3 * w + 2, :], qkf[:, w, :], pq[:, 3 * w + 1, :],
                                               ALU.subtract).then_inc(pool_a.sem, 1)
                    if (stage, n) == ("he", 1):
                        pool.wait_ge(*R.moved(b, k - 1))
                        pool.wait_ge(*R.moved(b, k))
                        pool.tensor_tensor(sq[:, :], qh[:, :], qh[:, :], ALU.mult).then_inc(sq_p.sem, 1)
                    if stage == "dist":
                        d = D[:, n % 2, :, :]
                        pool.wait_ge(*d_act.at(b, n + 1))
                        m = offself[:, 1 if n == 0 else 0, :].unsqueeze(1).broadcast_to([P, SH, WW])
                        pool.tensor_tensor(d, d, m, ALU.mult).then_inc(d_scaled.sem, 1)
                        pool.wait_ge(*d_scaled.at(b, n + 1))
                        pool.tensor_tensor(d, d, outside[:, :].unsqueeze(1).broadcast_to([P, SH, WW]),
                                           ALU.add).then_inc(d_pool.sem, 1)

            go(WORK_A, 0, 0)
            with pool.Fori(0, NB - 1) as b:
                go(WORK, b + 1, b)
            go(WORK_P, NB - 1, NB - 1)

        @block.tensor
        def _(pe):
            def mm(o, l, r, start=True, stop=True):
                return pe.matmul(o, l, r, start=start, stop=stop)

            pe.wait_ge(loaded, LOADS * 16)
            pe.wait_ge(masks, 2)
            for i in range(4):
                ins = pe.transpose(psum[0][:, P * i:P * i + P], wload[:, i, :], ident[:, :])
            for v in range(2):
                for f in range(3):
                    ins = mm(psum[1][:, 3 * v + f:3 * v + f + 1], rows[0:1, v, f, :], ones1[:, :])
            ins.then_inc(setup_pe, 1)
            pe.wait_ge(u_spread, 1)
            pe.transpose(psum[3][0:32, 0:P], ub[:, :, :].rearrange("p h r -> p (h r)"), ident[:, :]).then_inc(setup_pe, 1)
            pe.wait_ge(u_turned, 1)
            mm(psum[2][:, 0:SE], uT[:, :], vh[:, :]).then_inc(setup_pe, 1)

            def transposed(ring, b, k, src, perm, tiles):
                pe.wait_ge(*ring.free(b, k))
                for q, u in enumerate(tiles):
                    ins = pe.transpose(ring.bank(k)[:, P * q:P * q + P], src[:, u, :], perm)
                ins.then_inc(ring.ready.sem, 1)

            def one(ring, b, k, products):
                pe.wait_ge(*ring.free(b, k))
                for o, l, r, start, stop in products:
                    ins = mm(o, l, r, start, stop)
                ins.then_inc(ring.ready.sem, 1)

            def pv_step(b, n, i):
                s = STEPS * n + i
                pe.wait_ge(*probs.at(b, 4 * (s + 1)))
                if i % 8 == 0:
                    pe.wait_ge(*o_out.at(b, 2 * n + i // 8))
                for j in range(4):
                    ins = mm(ov_bank[VW * j:VW * j + VW, :], Vg[:, i % 8, 4 * n + j, :], PT[:, (4 * s + j) % 8, :],
                             i % 8 == 0, i % 8 == 7)
                ins.then_inc(pv.sem, 1)

            def go(work, ba, bp):
                for side, stage, n, k in work:
                    b = ba if side == "a" else bp
                    if stage == "ln1":
                        pe.wait_ge(*xn_a.at(b, 1))
                        for i in range(2):
                            transposed(A, b, k + i, xna, ident[:, :], range(4 * i, 4 * i + 4))
                    if stage == "qkv":
                        pe.wait_ge(*A.made(b, k, k - 2, k - 1))
                        for w in range(2):
                            for h in range(2):
                                use = k + 2 * w + h
                                one(A, b, use, [(A.bank(use)[:, :], wT[:, w, :], xTa[:, HALF * h:HALF * h + HALF], True, True)])
                        for i in range(2):
                            use = k + 4 + i
                            one(A, b, use, [(A.bank(use)[:, P * q:P * q + P], xTa[:, P * (4 * i + q):P * (4 * i + q) + P],
                                             wT[:, 2, :], True, True) for q in range(4)])
                    if stage == "max":
                        n, i = n
                        if i == 0:
                            pe.wait_ge(*quad_in.at(b, n + 1))
                        for y in range(4):
                            j, qt, h = (4 * i + y) // 16, (4 * i + y) // 2 % 8, y % 2
                            one(A, b, k + y, [(A.bank(k + y)[:, :], Q[:, n % 2, j // 2, P * qt:P * qt + P],
                                               K[:, n % 2, j, HALF * h:HALF * h + HALF], True, True)])
                    if stage == "mrow":
                        pe.wait_ge(*m_red.at(b, n + 1))
                        pe.wait_ge(*A.free(b, k))
                        pe.transpose(A.bank(k)[0:PARTS * 32, 0:P // 2].bitcast(BF16), mb[:, :], identb[:, :]).then_inc(A.ready.sem, 1)
                    if stage == "exp":
                        n, i = n
                        if i == 0:
                            pe.wait_ge(*m_in.at(b, n + 1))
                        for j in range(4):
                            g = 4 * (STEPS * n + i) + j
                            pe.wait_ge(*probs.at(b, max(g - 2, 0)))
                            ins = mm(st_bank[g % 3][:, :], K[:, n % 2, j, P * (i % 8):P * (i % 8) + P],
                                     Q[:, n % 2, j // 2, HALF * (i // 8):HALF * (i // 8) + HALF])
                            ins.then_inc(scores.sem, 1)
                        if i >= 1:
                            pv_step(b, n, i - 1)
                    if stage == "fin":
                        pv_step(b, n, STEPS - 1)
                    if stage == "turn":
                        if n == 0:
                            pe.wait_ge(*o_out.at(b, 2 * NQUAD))
                        pe.wait_ge(*A.free(b, k))
                        for q in range(NQUAD):
                            ins = pe.transpose(A.bank(k)[:, P * q:P * q + P], oT[:, q, P * n:P * n + P], ident[:, :])
                        ins.then_inc(A.ready.sem, 1)
                    if stage == "back":
                        pe.wait_ge(*A.made(b, k, USE_A["turn", n]))
                        pe.wait_ge(*A.free(b, k))
                        pe.transpose(A.bank(k)[:, 0:P], on[:, n % 2, :], ident[:, :]).then_inc(A.ready.sem, 1)
                    if stage == "wo":
                        pe.wait_ge(*A.made(b, k, USE_A["back", n]))
                        one(A, b, k, [(A.bank(k)[:, 0:P], onT[:, n % 2, :], wT[:, 3, :], True, True)])
                    if stage == "lnT":
                        pe.wait_ge(*xn_p.at(b, n + 1))
                        for i in range(2):
                            transposed(R, b, k + i, xn, ident[:, :], range(4 * i, 4 * i + 4))
                    if stage == "fa":
                        n, o = n
                        if o == 0 and n % 2 == 0:
                            pe.wait_ge(*R.made(b, k, USE_P["lnT", n], USE_P["lnT", n] + 1))
                        one(R, b, k, [(R.bank(k)[:, :], W0[:, P * o:P * o + P], xT[:, HALF * (n % 2):HALF * (n % 2) + HALF], True, True)])
                    if stage == "fb":
                        n, o = n
                        if o == 0:
                            pe.wait_ge(*R.made(b, k, USE_P["fa", (n, 2)], USE_P["fa", (n, 3)]))
                        one(R, b, k, [(R.bank(k)[:, :], W1[:, c, P * o:P * o + P], h1[:, c, :], c == 0, c == FC - 1)
                                      for c in range(FC)])
                    if stage == "fc":
                        pe.wait_ge(*R.made(b, k, USE_P["fb", (n, 2)], USE_P["fb", (n, 3)]))
                        one(R, b, k, [(R.bank(k)[:, P * q:P * q + P], h2[:, c, P * q:P * q + P], W2[:, c, :],
                                       c == 0, c == FC - 1) for q in range(4) for c in range(FC)])
                    if stage == "flip":
                        transposed(R, b, k, xn, flip[:, :], [NU - 1 - (4 * n + q) for q in range(4)])
                    if stage == "he":
                        if n == 0:
                            pe.wait_ge(*R.made(b, k, USE_P["lnT", 1], USE_P["lnT", 1] + 1))
                        one(R, b, k, [(R.bank(k)[:, :], eq[:, :], xT[:, HALF * n:HALF * n + HALF], True, True)])
                    if stage == "hid":
                        pe.wait_ge(*sig_p.at(b, 1))
                        one(R, b, k, [(R.bank(k)[0:P // 2, 0:1], w1m[:, :], sig[:, 3:4], True, True)])
                    if stage == "mod":
                        pe.wait_ge(*R.made(b, k, USE_P["hid", 0]))
                        one(R, b, k, [(R.bank(k)[:, f:f + 1], w2d[:, f, :], hid[:, :], True, True) for f in range(3)])
                    if stage == "qd":
                        h = n % 2
                        one(R, b, k, [(R.bank(k)[:, :], eqd[:, n // 2, :], xT[:, HALF * h:HALF * h + HALF], True, True)])
                    if stage == "key":
                        h = n % 2
                        if n == 0:
                            pe.wait_ge(*R.made(b, k, USE_P["flip", 0], USE_P["flip", 1]))
                        one(R, b, k, [(R.bank(k)[:, :], eqd[:, n // 2, :], xrev[:, HALF * h:HALF * h + HALF], True, True)])
                    if stage == "pad":
                        pe.wait_ge(*xpad.at(b, 1))
                        one(R, b, k, [(R.bank(k)[:, WIN * f:WIN * f + WIN], eqd[:, f, :], xrev[:, T:RPAD], True, True)
                                      for f in range(2)])
                    if stage == "an":
                        pe.wait_ge(*met_p.at(b, 1))
                        pe.wait_ge(*sq_p.at(b, 1))
                        one(R, b, k, [(R.bank(k)[:, 16 * u:16 * u + 16], sq[:, P * u:P * u + P], nb[:, :], True, True)
                                      for u in range(NU)])
                    if stage == "qtok":
                        one(R, b, k, [(R.bank(k)[:, P * q:P * q + P], xT[:, P * (4 * n + q):P * (4 * n + q) + P],
                                       eq[:, :], True, True) for q in range(4)])
                    if stage == "hebb":
                        one(R, b, k, [(R.bank(k)[:, P * q:P * q + P], qh[:, P * (4 * n + q):P * (4 * n + q) + P],
                                       bdh[:, :, :], True, True) for q in range(4)])
                    if stage == "dist":
                        pe.wait_ge(*aop_p.at(b, n + 1))
                        if n == 0:
                            pe.wait_ge(*bop.at(b, 2))
                        for f in range(2):
                            one(R, b, k + f, [(R.bank(k + f)[BLK * i:BLK * i + BLK, WW * j:WW * j + WW],
                                               Aop[:, 4 * f + j, BLK * i:BLK * i + BLK], B[:, f, window(NBLK * n + i)], True, True)
                                              for j in range(4) for i in range(NBLK)])
                    if stage == "vw":
                        one(R, b, k, [(R.bank(k)[0:WW, P * i:P * i + P], xrev[:, window(NBLK * n + i)], ev[:, :], True, True)
                                      for i in range(NBLK)])
                    if stage == "wt":
                        pe.wait_ge(*w_v.at(b, n + 1))
                        for i in range(2):
                            pe.wait_ge(*R.free(b, k + i))
                            for q in range(4):
                                ins = pe.transpose(R.bank(k + i)[0:WW, P * q:P * q + P], E[:, n % 2, 4 * i + q, :], ident[:, :])
                            ins.then_inc(R.ready.sem, 1)
                    if stage == "pv":
                        pe.wait_ge(*R.made(b, k, USE_P["vw", n], USE_P["wt", n], USE_P["wt", n] + 1))
                        one(R, b, k, [(R.bank(k)[BLK * i:BLK * i + BLK, 32 * h:32 * h + SE + 1], WT[0:WW, h, BLK * i:BLK * i + BLK],
                                       Vw[:, n % 2, i, h, :], True, True) for h in range(SH) for i in range(NBLK)])
                    if stage == "st":
                        pe.wait_ge(*s_v.at(b, n + 1))
                        pe.wait_ge(*R.free(b, k))
                        pe.transpose(R.bank(k)[:, 0:P], s_tok[:, :], ident[:, :]).then_inc(R.ready.sem, 1)
                    if stage == "dec":
                        pe.wait_ge(*R.made(b, k, USE_P["st", n]))
                        one(R, b, k, [(R.bank(k)[:, 0:P], s_T[:, :], dec[:, :], True, True)])

            pe.wait_ge(setup_v, 1)
            go(WORK_A, 0, 0)
            with pe.Fori(0, NB - 1) as b:
                go(WORK, b + 1, b)
            go(WORK_P, NB - 1, NB - 1)

        @block.scalar
        def _(act):
            def evict(ring, b, k, dst, src, func=ACT.Identity, **kw):
                act.wait_ge(*ring.filled(b, k))
                return act.activation(dst, src, func, **kw).then_inc(ring.emptied(k), 1)

            def copy_out(b, n, h):
                act.wait_ge(*pv.at(b, STEPS * n + 8 * (h + 1)))
                act.activation(oT[:, n, HALF * h:HALF * h + HALF], ov_bank[:, :], ACT.Identity).then_inc(o_out.sem, 1)

            act.wait_ge(setup_v, 1)
            act.preload_act_table_set(EXP_LN)

            def go(work, ba, bp):
                for side, stage, n, k in work:
                    b = ba if side == "a" else bp
                    ring, l, dst = (A, ls[:, 0], xTa) if side == "a" else (R, ls[:, 1], xT)
                    if stage in ("ln1", "ln"):
                        var, ln, rs, i = (var_a, ln_a, rs_a, 1) if stage == "ln1" else (var_p, ln_p, rs_p, n + 1)
                        act.wait_ge(*var.at(b, i))
                        act.activation(l[:, 1, :], l[:, 0, :], ACT.Ln).then_inc(ln.sem, 1)
                        act.wait_ge(*ln.at(b, i))
                        act.activation(l[:, 2, :], l[:, 1, :], ACT.Exp, scale=-0.5).then_inc(rs.sem, 1)
                    if stage in ("ln1", "lnT"):
                        for i in range(2):
                            evict(ring, b, k + i, dst[:, HALF * i:HALF * i + HALF], ring.bank(k + i)[:, :])
                    if stage == "qkv":
                        for w in range(2):
                            for h in range(2):
                                evict(A, b, k + 2 * w + h, qkf[:, w, HALF * h:HALF * h + HALF], A.bank(k + 2 * w + h)[:, :],
                                      bias=wqkb[:, w:w + 1], scale=SCALE if w == 0 else 1.0)
                            act.wait_ge(*A.moved(b, k + 2 * w))
                            act.wait_ge(*A.moved(b, k + 2 * w + 1))
                            if w == 0:
                                act.wait_ge(*split_out.at(b, 0))
                            act.activation(pq[:, 3 * w, :], qkf[:, w, :], ACT.Identity).then_inc(act_a.sem, 1)
                        for w in range(2):
                            act.wait_ge(*pool_a.at(b, w + 1))
                            act.activation(pq[:, 3 * w + 1, :], qkf[:, w, :], ACT.Identity).then_inc(act_a.sem, 1)
                    if stage == "mrow":
                        act.wait_ge(*m_out.at(b, n))
                        evict(A, b, k, mT[:, :], A.bank(k)[0:PARTS * 32, 0:P // 2].bitcast(BF16))
                    if stage == "exp":
                        n, i = n
                        s = STEPS * n + i
                        act.wait_ge(*pv.at(b, max(s - 1, 0)))
                        for j in range(4):
                            act.wait_ge(*scores.at(b, 4 * s + j + 1))
                            act.activation(PT[:, (4 * s + j) % 8, :], st_bank[(4 * s + j) % 3][:, :], ACT.Exp).then_inc(probs.sem, 1)
                        if i == 8:
                            copy_out(b, n, 0)
                    if stage == "fin":
                        copy_out(b, n, 1)
                    if stage == "back":
                        evict(A, b, k, onT[:, n % 2, :], A.bank(k)[:, 0:P])
                    if stage in ("fa", "fb"):
                        n, o = n
                        h, i = (h1, 0) if stage == "fa" else (h2, 1)
                        evict(R, b, k, h[:, o, :], R.bank(k)[:, :], ACT.Relu, scale=scol[:, i:i + 1])
                    if stage == "flip":
                        evict(R, b, k, xrev[:, HALF * n:HALF * n + HALF], R.bank(k)[:, :])
                    if stage == "he":
                        act.wait_ge(*R.filled(b, k))
                        act.activation(qh[:, HALF * n:HALF * n + HALF], R.bank(k)[:, :], ACT.Relu,
                                       accum_out=sig[:, n:n + 1]).then_inc(R.emptied(k), 1)
                    if stage == "hid":
                        evict(R, b, k, hid[:, :], R.bank(k)[0:P // 2, 0:1], ACT.Gelu, bias=b1m[:, :])
                        act.preload_act_table_set(EXP_LN)
                    if stage == "key" and n == 0:
                        act.wait_ge(*met_z.at(b, 1))
                        act.activation(met[:, 3, :], met[:, 2, :], ACT.Exp, scale=-1.0).then_inc(met_e.sem, 1)
                        act.wait_ge(*met_e.at(b, 1))
                        act.activation(met[:, 4, :], met[:, 3, :], ACT.Ln, bias=1.0).then_inc(met_l.sem, 1)
                    if stage in ("qd", "key"):
                        dst = qd if stage == "qd" else B
                        h = n % 2
                        evict(R, b, k, dst[:, n // 2, HALF * h:HALF * h + HALF], R.bank(k)[:, :], ACT.Relu)
                    if stage == "pad":
                        evict(R, b, k, B[:, :, T:RPAD], R.bank(k)[:, 0:2 * WIN].rearrange("p (f w) -> p f w", f=2), ACT.Relu)
                    if stage == "an":
                        evict(R, b, k, an[:, :, :], R.bank(k)[:, 0:P].rearrange("p (u h) -> p u h", u=NU))
                    if stage == "qtok":
                        evict(R, b, k, qtok[:, 4 * n:4 * n + 4, :], rows_of(R.bank(k), P), ACT.Relu)
                    if stage == "keys":
                        act.wait_ge(*gn_v.at(b, 1))
                        act.activation(gn[:, 1, :, :], gn[:, 0, :, :], ACT.Ln).then_inc(gn_l.sem, 1)
                        act.wait_ge(*gn_l.at(b, 1))
                        act.activation(gn[:, 1, :, :], gn[:, 1, :, :], ACT.Exp, scale=-0.5).then_inc(gn_a.sem, 1)
                    if stage == "dist":
                        d = D[:, n % 2, :, :]
                        act.wait_ge(*R.moved(b, k))
                        act.wait_ge(*R.moved(b, k + 1))
                        act.activation(d, d, ACT.Relu, scale=-1.0).then_inc(d_act.sem, 1)
                    if stage == "top":
                        n, r = n
                        e = E[:, n % 2, :, :]
                        if r == 0:
                            act.wait_ge(*d_pool.at(b, n + 1))
                            act.activation(e, D[:, n % 2, :, :], ACT.Ln, scale=-1.0, bias=eps8[:, :]).then_inc(e_steps.sem, 1)
                        if r == 1:
                            act.wait_ge(*e_steps.at(b, 2 * n + 1))
                            act.activation(e, e, ACT.Exp, scale=0.5).then_inc(e_steps.sem, 1)
                        if r == 2:
                            act.wait_ge(*e_steps.at(b, 2 * n + 2))
                            act.activation(e, e, ACT.Exp, scale=-1.0).then_inc(e_act.sem, 1)
                    if stage == "vw":
                        evict(R, b, k, Vw[:, n % 2, :, :, 0:SE],
                              R.bank(k)[0:WW, :].rearrange("p (w h e) -> p w h e", w=NBLK, h=SH), ACT.Relu)
                    if stage == "wt":
                        for i in range(2):
                            evict(R, b, k + i, WT[0:WW, 4 * i:4 * i + 4, :], rows_of(R.bank(k + i), P)[0:WW])
                    if stage == "st":
                        evict(R, b, k, s_T[:, :], R.bank(k)[:, 0:P])

            go(WORK_A, 0, 0)
            with act.Fori(0, NB - 1) as b:
                go(WORK, b + 1, b)
            go(WORK_P, NB - 1, NB - 1)

        @block.vector
        def _(dve):
            setup_step = sem("vector_setup")
            done = [0]

            def then(ins):
                done[0] += 1
                ins.then_inc(setup_step, 1)
                dve.wait_ge(setup_step, done[0])

            dve.wait_ge(loaded, LOADS * 16)
            dve.wait_ge(loadk, 48)
            dve.wait_ge(masks, 2)
            then(dve.tensor_copy(kf, kb0))
            then(dve.tensor_tensor(kf[:, 0, :], kf[:, 0, :], kf[:, 1, :], ALU.subtract))
            then(dve.tensor_scalar(W0[:, :], kf[:, 0, :], 2.0, None, ALU.mult))
            then(dve.tensor_scalar(W1[:, :, :], kb1, 2.0, -1.0, ALU.mult, ALU.add))
            then(dve.tensor_scalar(W2[:, :, :], kb2, 2.0, -1.0, ALU.mult, ALU.add))
            then(dve.tensor_scalar(scol[:, 0:2], scol[:, 0:2], 2.0, None, ALU.mult))
            then(dve.tensor_scalar(wqkb[:, 0:1], wqkb[:, 0:1], SCALE, None, ALU.mult))
            then(dve.tensor_reduce(any0[:, :], half0[:, :], AX.X, ALU.add))
            then(dve.tensor_reduce(any1[:, :], half1[:, :], AX.X, ALU.add))
            then(dve.tensor_scalar(minus1[:, :], half1[:, :], -1.0, None, ALU.mult))
            dve.wait_ge(setup_pe, 1)
            then(dve.tensor_copy(wT[:, :, :], rows_of(psum[0], P)))
            then(dve.tensor_copy(cols[:, :, :], psum[1][:, 0:6].rearrange("p (v f) -> p v f", v=2)))
            dve.tensor_tensor(ub[:, :, :], up[:, :].unsqueeze(1).broadcast_to([P, SH, 4]), cast(blk[:, :], [P, SH, 4]),
                              ALU.mult).then_inc(u_spread, 1)
            dve.wait_ge(setup_pe, 2)
            dve.tensor_copy(uT[:, :], psum[3][0:32, 0:P]).then_inc(u_turned, 1)
            dve.wait_ge(setup_pe, 3)
            then(dve.tensor_copy(bdh[:, :, :], psum[2][:, 0:SE].unsqueeze(1).broadcast_to([P, SH, SE])))
            then(dve.tensor_tensor(bdh[:, :, :], bdh[:, :, :], cast(blk[:, :], [P, SH, SE]), ALU.mult))
            then(dve.tensor_copy(nb[:, 0:SH], blk[:, :]))
            dve.sem_inc(setup_v, 1)

            def norm(b, i, link, side, src, dst, var, rs, done_):
                l, st, m = ls[:, side], stat[:, side], mv[:, side]
                for u in range(NU):
                    ins = dve.bn_stats(st[:, u, :], src[:, u, :])
                link(ins, before_aggr=True)
                for u in range(NU):
                    ins = dve.bn_aggr(m[:, u, :], st[:, u, :])
                link(ins)
                dve.tensor_scalar(l[:, 0, :], m[:, :, 1], LN_EPS, None, ALU.add).then_inc(var.sem, 1)
                dve.wait_ge(*rs.at(b, i))
                link(dve.tensor_tensor(l[:, 3, :], l[:, 2, :], l[:, 2, :], ALU.mult))
                link(dve.tensor_tensor(l[:, 4, :], l[:, 3, :], l[:, 0, :], ALU.mult))
                link(dve.tensor_scalar(l[:, 5, :], l[:, 4, :], -0.5, 1.5, ALU.mult, ALU.add))
                link(dve.tensor_tensor(l[:, 6, :], l[:, 5, :], l[:, 2, :], ALU.mult))
                link(dve.scalar_tensor_tensor(out=l[:, 7, :], in0=m[:, :, 0], scalar=-1.0, in1=l[:, 6, :],
                                              op0=ALU.mult, op1=ALU.mult))
                for u in range(NU):
                    ins = dve.tensor_scalar(dst[:, u, :], src[:, u, :], l[:, 6, u:u + 1], l[:, 7, u:u + 1], ALU.mult, ALU.add)
                ins.then_inc(done_.sem, 1)

            def go(work, ba, bp):
                count_ = {"a": 0, "p": 0}
                for side, stage, n, k in work:
                    b = ba if side == "a" else bp

                    def link(ins, side=side, b=b, before_aggr=False):
                        count_[side] += 1
                        ins.then_inc(links[side].sem, 1)
                        dve.wait_ge(*links[side].at(b, count_[side]))
                        if before_aggr:
                            pass_waits(dve)

                    if stage == "ln1":
                        dve.wait_ge(*x_in.at(b, 1))
                        norm(b, 1, link, 0, xa, xna, var_a, rs_a, xn_a)
                    if stage == "qkv":
                        for i in range(2):
                            dve.wait_ge(*A.filled(b, k + 4 + i))
                            dve.tensor_tensor(Vg[:, 4 * i:4 * i + 4, :, 0:HD],
                                              A.bank(k + 4 + i)[:, :].rearrange("p (t h d) -> p t h d", t=4, d=HD),
                                              bvb[:, :].rearrange("p (h d) -> p h d", d=HD).unsqueeze(1).broadcast_to([P, 4, NH, HD]),
                                              ALU.add).then_inc(A.emptied(k + 4 + i), 1)
                    if stage == "max":
                        n, i = n
                        for y in range(4):
                            j, qt, h = (4 * i + y) // 16, (4 * i + y) // 2 % 8, y % 2
                            dve.wait_ge(*A.filled(b, k + y))
                            c = (2 * (j % 2) + j // 2) * NU + qt
                            dve.tensor_reduce(mred[:, c, h:h + 1], A.bank(k + y)[:, :], AX.X, ALU.max).then_inc(A.emptied(k + y), 1)
                    if stage == "mrow":
                        dve.wait_ge(*A.moved(b, k - 1))
                        dve.wait_ge(*A.moved(b, k - 2))
                        link(dve.tensor_reduce(nm[:, 0, :], mred[:, :, :], AX.X, ALU.max, negate=True))
                        link(dve.tensor_copy(mb[:, 0, :], nm[:, 0, :]))
                        link(dve.tensor_tensor(nm[:, 1, :], nm[:, 0, :], mb[:, 0, :], ALU.subtract))
                        link(dve.tensor_copy(mb[:, 1, :], nm[:, 1, :]))
                        dve.tensor_tensor(mb[:, 2, :], nm[:, 1, :], mb[:, 1, :], ALU.subtract).then_inc(m_red.sem, 1)
                    if stage == "turn":
                        dve.wait_ge(*A.filled(b, k))
                        ps = rows_of(A.bank(k), VW)
                        link(dve.reciprocal(rden[:, n % 2, :], ps[:, :, HD]))
                        dve.tensor_tensor(on[:, n % 2, :].rearrange("p (h d) -> p h d", d=HD), ps[:, :, 0:HD],
                                          cast(rden[:, n % 2, :], [P, NH, HD]), ALU.mult).then_inc(A.emptied(k), 1)
                    if stage == "wo":
                        dve.wait_ge(*A.filled(b, k))
                        if n == 0:
                            dve.wait_ge(*xb_a.at(b, 1))
                            dve.wait_ge(*out_p.at(b, 0))
                        dve.tensor_tensor(xr[:, n, :], A.bank(k)[:, 0:P], xa[:, n, :], ALU.add).then_inc(A.emptied(k), 1)
                    if stage == "ln":
                        if n == 0:
                            dve.wait_ge(*A.moved(b, NA - 1))
                        else:
                            dve.wait_ge(*R.moved(b, k - 1))
                        norm(b, n + 1, link, 1, xr, xn, var_p, rs_p, xn_p)
                    if stage == "fc":
                        dve.wait_ge(*R.filled(b, k))
                        dst = xr[:, 4 * (n % 2):4 * (n % 2) + 4, :]
                        dve.scalar_tensor_tensor(out=dst, in0=rows_of(R.bank(k), P), scalar=scol[:, 2:3], in1=dst,
                                                 op0=ALU.mult, op1=ALU.add).then_inc(R.emptied(k), 1)
                    if (stage, n) == ("qd", 0):
                        dve.wait_ge(*R.moved(b, USE_P["flip", 1]))
                        dve.tensor_copy(xrev[:, T:RPAD], xrev[:, T - 1:T].broadcast_to([P, WIN])).then_inc(xpad.sem, 1)
                        dve.wait_ge(*R.moved(b, USE_P["he", 0]))
                        dve.wait_ge(*R.moved(b, USE_P["he", 1]))
                        link(dve.tensor_reduce(sig[:, 2:3], qh[:, 0:T:8], AX.X, ALU.add))
                        link(dve.tensor_tensor(sig[:, 0:1], sig[:, 0:1], sig[:, 1:2], ALU.add))
                        link(dve.scalar_tensor_tensor(out=sig[:, 0:1], in0=sig[:, 2:3], scalar=4.0, in1=sig[:, 0:1],
                                                      op0=ALU.mult, op1=ALU.add))
                        dve.tensor_scalar(sig[:, 3:4], sig[:, 0:1], 1.0 / T, None, ALU.mult).then_inc(sig_p.sem, 1)
                    if stage == "mod":
                        dve.wait_ge(*R.filled(b, k))
                        dve.tensor_tensor(met[:, 1, :], R.bank(k)[:, 0:3], cols[:, 0, :], ALU.add).then_inc(R.emptied(k), 1)
                        dve.wait_ge(*R.moved(b, k))
                        link(dve.scalar_tensor_tensor(out=met[:, 0, :], in0=met[:, 1, :], scalar=0.1, in1=cols[:, 1, :],
                                                      op0=ALU.mult, op1=ALU.add))
                        link(dve.tensor_scalar(met[:, 1, :], met[:, 0, :], -1.0, None, ALU.mult))
                        dve.tensor_tensor(met[:, 2, :], met[:, 0, :], met[:, 1, :], ALU.max).then_inc(met_z.sem, 1)
                    if (stage, n) == ("key", 3):
                        dve.wait_ge(*met_l.at(b, 1))
                        link(dve.scalar_tensor_tensor(out=met[:, 5, :], in0=met[:, 0, :], scalar=0.0, in1=met[:, 4, :],
                                                      op0=ALU.max, op1=ALU.add))
                        for f in range(2):
                            dve.tensor_scalar(alpha[:, 4 * f:4 * f + 4], half0[:, :], met[:, 5, f:f + 1], 2.0, ALU.mult, ALU.mult)
                        dve.tensor_scalar(beta[:, :], met[:, 5, 0:2], any1[:, :], None, ALU.mult)
                        link(dve.tensor_scalar(nb[:, SH:2 * SH], blk[:, :], met[:, 5, 2:3], None, ALU.mult))
                        dve.sem_inc(met_p.sem, 1)
                    if stage == "keys":
                        dve.wait_ge(*R.moved(b, USE_P["key", 3]))
                        dve.wait_ge(*R.moved(b, USE_P["pad", 0]))
                        for f in range(2):
                            link(dve.tensor_scalar(Bs[:, :], B[:, f, :], beta[:, f:f + 1], any0[:, :], ALU.mult, ALU.add))
                            dve.tensor_tensor(B[:, f, :], Bs[:, :], B[:, f, :], ALU.mult).then_inc(bop.sem, 1)
                            dve.wait_ge(*bop.at(b, f + 1))
                        dve.wait_ge(*R.moved(b, USE_P["an", 0]))
                        dve.tensor_scalar(gn[:, 0, :, :], an[:, :, 0:SH], 1e-4, None, ALU.max).then_inc(gn_v.sem, 1)
                        link(dve.tensor_scalar(gn[:, 2, :, :], an[:, :, 0:SH], 0.04, 0.1, ALU.is_gt, ALU.mult))
                        dve.wait_ge(*gn_a.at(b, 1))
                        link(dve.tensor_tensor(gn[:, 2, :, :], gn[:, 2, :, :], gn[:, 1, :, :], ALU.mult))
                    if stage == "hebb":
                        dve.wait_ge(*R.filled(b, k))
                        dve.tensor_tensor(hb[:, 4 * n:4 * n + 4, :].rearrange("p u (h e) -> p (u h) e", e=SE),
                                          rows_of(R.bank(k), SE),
                                          cast(gn[:, 2, 4 * n:4 * n + 4, :].rearrange("p u h -> p (u h)"), [P, 4 * SH, SE]),
                                          ALU.mult).then_inc(R.emptied(k), 1)
                    if stage == "dist":
                        if n == 0:
                            dve.wait_ge(*R.moved(b, USE_P["qd", 2]))
                            dve.wait_ge(*R.moved(b, USE_P["qd", 3]))
                        else:
                            dve.wait_ge(*R.filled(b, USE_P["dist", n - 1] + 1))
                        for h in range(SH):
                            ins = dve.tensor_scalar(Aop[:, h, :], qd[:, h // 4, P * n:P * n + P], alpha[:, h:h + 1],
                                                    minus1[:, h % 4:h % 4 + 1], ALU.mult, ALU.add)
                        ins.then_inc(aop_p.sem, 1)
                        for f in range(2):
                            dve.wait_ge(*R.filled(b, k + f))
                            dve.tensor_tensor(D[:, n % 2, 4 * f:4 * f + 4, :],
                                              R.bank(k + f)[:, 0:4 * WW].rearrange("p (h c) -> p h c", c=WW),
                                              cast(an[:, n, SH + 4 * f:SH + 4 * f + 4], [P, 4, WW]),
                                              ALU.subtract).then_inc(R.emptied(k + f), 1)
                    if stage == "top":
                        n, r = n
                        half = SH // 2
                        if r == 0:
                            dve.wait_ge(*d_pool.at(b, n + 1))
                            pass_waits(dve)
                        for h in range(SH):
                            src = D[:, n % 2, h, :] if r == 0 else Rm[:, h, :]
                            if r > 0 and h % half == 0:
                                dve.wait_ge(*top8.at(b, (4 * n + r) * 2 * SH - SH + h + half))
                                pass_waits(dve)
                            dve.max(out=m8[:, h, :], in_=src).then_inc(top8.sem, 1)
                        for h in range(SH):
                            src = D[:, n % 2, h, :] if r == 0 else Rm[:, h, :]
                            if h % half == 0:
                                dve.wait_ge(*top8.at(b, (4 * n + r) * 2 * SH + h + half))
                                pass_waits(dve)
                            dve.match_replace(out=Rm[:, h, :], in_to_replace=m8[:, h, :], in_values=src,
                                              imm_value=-2 * BIG).then_inc(top8.sem, 1)
                        if r == TOPK // 8 - 1:
                            dve.wait_ge(*top8.at(b, (n + 1) * 8 * SH))
                            dve.wait_ge(*e_act.at(b, n + 1))
                            dve.scalar_tensor_tensor(out=E[:, n % 2, :, :], in0=Rm[:, :, :], scalar=-1.5 * BIG,
                                                     in1=E[:, n % 2, :, :], op0=ALU.is_lt, op1=ALU.mult).then_inc(w_v.sem, 1)
                    if stage == "pv":
                        dve.wait_ge(*R.filled(b, k))
                        ps = R.bank(k)[:, 0:32 * SH].rearrange("p (h e) -> p h e", h=SH)
                        link(dve.tensor_scalar(rd[:, 0, :], ps[:, :, SE], 1e-8, None, ALU.add))
                        link(dve.reciprocal(rd[:, 1, :], rd[:, 0, :]))
                        s3 = s_tok[:, :].rearrange("p (h e) -> p h e", e=SE)
                        dve.tensor_tensor(s3, ps[:, :, 0:SE], cast(rd[:, 1, :], [P, SH, SE]), ALU.mult).then_inc(R.emptied(k), 1)
                        dve.wait_ge(*R.moved(b, k))
                        link(dve.tensor_tensor(s_tok[:, :], s_tok[:, :], hb[:, n, :], ALU.add))
                        dve.tensor_tensor(s_tok[:, :], s_tok[:, :], qtok[:, n, :], ALU.mult).then_inc(s_v.sem, 1)
                    if stage == "dec":
                        dve.wait_ge(*R.filled(b, k))
                        dve.tensor_tensor(xr[:, n, :], R.bank(k)[:, 0:P], xr[:, n, :], ALU.add).then_inc(R.emptied(k), 1)
                for side, n in count_.items():
                    assert n in (0, links[side].per), (side, n)

            go(WORK_A, 0, 0)
            with dve.Fori(0, NB - 1) as b:
                go(WORK, b + 1, b)
            go(WORK_P, NB - 1, NB - 1)


def kernel(**inputs):
    import numpy as _np
    import concourse.bacc as _bacc
    from concourse import mybir as _mybir
    from concourse.bass_utils import run_bass_kernel_spmd as _run

    nc = _bacc.Bacc("TRN2", target_bir_lowering=False, num_devices=1)
    arrays, args = {}, {}
    for name, a in inputs.items():
        a = _np.ascontiguousarray(a)
        if a.dtype == _np.bool_:
            a = a.view(_np.uint32)
        if a.ndim == 0:
            a = a.reshape(1)
        short = name.removeprefix("L0_attn_a_").removeprefix("L0_attn_b_").removeprefix("L0_ffn_")
        arrays[f"in_{short}"] = a
        args[short] = nc.dram_tensor(f"in_{short}", a.shape, _mybir.dt.from_np(a.dtype), kind="ExternalInput").ap()
    out = nc.dram_tensor("out", (NB, T, P), F32, kind="ExternalOutput").ap()
    hybrid_block_kernel(
        nc, args["hidden_states"], args["Wq"], args["bq"], args["Wk"], args["bk"], args["Wv"], args["bv"],
        args["Wo"], args["bo"], args["encoder_query"], args["encoder_value"], args["mn_w1"], args["mn_b1"],
        args["mn_w2"], args["mn_b2"], args["base_metric"], args["decoder"], args["hebbian_U"], args["hebbian_V"],
        args["k0"], args["k1"], args["k2"], args["s0"], args["s1"], args["s2"], out)
    r = _run(nc, [arrays], core_ids=[0])
    return r.results[0]["out"]
```

```python
from contextlib import ExitStack

import concourse.bass as bass
from concourse import mybir

F32 = mybir.dt.float32
BF16 = mybir.dt.bfloat16
U8 = mybir.dt.uint8
U32 = mybir.dt.uint32
ALU = mybir.AluOpType
ACT = mybir.ActivationFunctionType
AX = mybir.AxisListType

P = 128
NB, T = 8, 1024
NU = T // P
HALF = 512
NH, HD = 16, 8
NQUAD = NH // 4
SCALE = float(HD) ** -0.5
PARTS = 3
QPART = (0, 0, 0, 1, 1, 2)
KPART = (0, 1, 2, 0, 1, 0)
QLOAD = ((0, 3, 0), (3, 2, 1), (5, 1, 2))
KLOAD = ((0, 3, 0), (3, 2, 0), (5, 1, 0))
MROW = len(QPART) * HD
VW = 32
NF, FC = 512, 4
SH, SE = 8, 16
WIN, TOPK, BLK = 64, 32, 32
NBLK = P // BLK
WW = BLK + WIN
RPAD = T + WIN
BIG = 1.0e18
LN_EPS = 1e-5
EXP_LN = "natural_log_exp_and_others"
LOADS = 37
LINKS_P = 71
LINKS_Q = 0

STEPS = 16
USES = dict(qk=4, v=2, max=1, mrow=1, turn=1, back=1, wo=1,
            lnT=1, lnTa=2, fa=1, fb=1, fc=1, flip=1, he=1, qd=1, hid=1, mod=1, key=1, pad=1, an=1, qtok=1, hebb=1,
            dist=2, vw=1, wt=2, pv=1, st=1, dec=1)


def ffn_slots(n):
    return ([(1.8, [("fa", (n, o)), ("fa", (n, o + 1))]) for o in (0, 2)] + [(3.4, [("fb", (n, o))]) for o in range(FC)] +
            [(3.5, [("fc", n)]), (0.8, [("fcd", n)])])


def norm_slots(n):
    return [(1.0, [(stage, n)]) for stage in ("ln", "lnr", "lnf", "lnn", "lnT")]


def between(slots, *others):
    slots = list(slots)
    for at, extra in others:
        for i, (w, stages) in enumerate(extra):
            slots[at + i] = (slots[at + i][0] + w, slots[at + i][1] + stages)
    return slots


BAND = 0.9

SLOTS_P = norm_slots((0, 0)) + between(ffn_slots(0), (0, norm_slots((0, 1)))) + between(ffn_slots(1), (0, norm_slots((1, 0))))
SLOTS_P += norm_slots((1, 1))
SLOTS_P += [(1, [("flip", 0), ("flip", 1)]), (2, [("he", 0), ("he", 1)]), (2, [("qd", 0), ("qd", 1)]), (1, [("hid", 0)]),
            (1, [("qd", 2)]), (1, [("mod", 0)]), (1, [("qd", 3)]), (2, [("key", 0), ("key", 1)]), (2, [("key", 2), ("key", 3)]),
            (1, [("pad", 0), ("an", 0)]), (2, [("qtok", 0), ("qtok", 1)]), (4, [("keys", 0)]),
            (1, [("gate", 0)]), (2, [("hebb", 0), ("hebb", 1)]), (2, [("aop", 0)]), (2, [("dist", 0)]), (2, [("dev", 0)])]
for _u in range(NU + 1):
    _next, _last, _here = _u + 1 < NU, _u >= 1, _u < NU
    SLOTS_P += [(w * BAND, [(stage, n) for real, stage, n in stages if real]) for w, stages in (
        (3.0, [(_u >= 2, "decd", _u - 2), (_next, "aop", _u + 1), (_last, "vw", _u - 1), (_here, "top", (_u, 0))]),
        (2.0, [(_next, "dist", _u + 1), (_here, "top", (_u, 1))]),
        (2.5, [(_next, "dev", _u + 1), (_here, "top", (_u, 2))]),
        (2.5, [(_last, "wt", _u - 1), (_here, "top", (_u, 3))]),
        (2.0, [(_last, "pv", _u - 1), (_here, "top", (_u, 4))]),
        (2.0, [(_here, "top", (_u, 5)), (_last, "pvd", _u - 1)]),
        (1.5, [(_last, "st", _u - 1), (_here, "top", (_u, 6))]),
        (2.0, [(_here, "top", (_u, 7)), (_last, "dec", _u - 1)]))]
SLOTS_P += [(1.0, [("decd", NU - 1)])] + norm_slots((2, 0)) + between(ffn_slots(2), (0, norm_slots((2, 1)))) + ffn_slots(3) + [(0.1, [("out", 0)])]

CARRY = 9
SLOTS_Q = SLOTS_P[len(SLOTS_P) - CARRY:]
SLOTS_P = SLOTS_P[:len(SLOTS_P) - CARRY]
SLOTS_O = [[(s, _u - d) for d, s in enumerate(("turn", "back", "wo")) if 0 <= _u - d < NU] for _u in range(NU + 2)]
HEAD_AT = {(2, 4): [("x", 0)], (2, 14): [("ln", 0)], (2, 18): [("lnr", 0)], (2, 20): [("lnf", 0)],
           (2, 22): [("lnn", 0)], (2, 24): [("lnTa", 0)], (2, 28): [("qk", 0)], (3, 0): [("load", 0)], (3, 56): [("mrow", 0)]}
RES_AT = (3, 24)
UNITS = NQUAD * STEPS
MAXIMA = 4 * NU * 2
MAX_FROM = 13
MAX_TO = 56
O_EVERY = 3
Q_FROM = 1
P_FROM = 28
MAX_STEP = 1.6


def turn_of(ahead, behind, carried):
    room = [0.0 if s < P_FROM else 1.0 if (ahead or s < 3 * UNITS) and MAX_FROM <= s % UNITS < MAX_TO else MAX_STEP
            for s in range(NQUAD * UNITS)]
    whole, weight = sum(room), sum(w for w, _ in SLOTS_P)
    work, used, at, spent = [("a", "v", 0)], 0.0, 0, 0.0
    for s in range(NQUAD * UNITS):
        n, i = divmod(s, UNITS)
        if behind:
            work += [("o",) + x for slot in SLOTS_O[s // O_EVERY:s // O_EVERY + 1] for x in slot if s % O_EVERY == 0]
        if i == 0 and n + 1 < NQUAD:
            work.append(("a", "load", n + 1))
        if (n, i) == RES_AT:
            work.append(("a", "residual", 0))
        if ahead:
            work += [("h",) + x for x in HEAD_AT.get((n, i), ())]
        if carried:
            work += [("q",) + x for d in range(CARRY) if Q_FROM + d * (P_FROM - Q_FROM) // CARRY == s for x in SLOTS_Q[d][1]]
        side, to = ("a", n + 1) if n + 1 < NQUAD else ("h", 0)
        if side == "a" or ahead:
            work += [(side, "max", (to, c)) for c in range(MAXIMA) if MAX_FROM + c * (MAX_TO - MAX_FROM) // MAXIMA == i]
        if side == "a" and i == MAX_TO:
            work.append(("a", "mrow", n + 1))
        work.append(("a", "exp", (n, i)))
        if i == UNITS - 1:
            work.append(("a", "fin", n))
        used += room[s]
        while behind and at < len(SLOTS_P) and (spent + SLOTS_P[at][0]) * whole <= used * weight * 1.0001:
            work += [("p",) + x for x in SLOTS_P[at][1]]
            spent += SLOTS_P[at][0]
            at += 1
    assert at == (len(SLOTS_P) if behind else 0)
    return work


def numbered(work, first):
    k, use, said = {"A": first, "p": 0, "q": NP - NQ}, dict(P_USE), []
    for side, stage, n in work:
        ring = side if side in "pq" else "A"
        use[stage, n] = k[ring]
        said.append((side, stage, n, k[ring]))
        k[ring] += USES.get(stage, 0)
    return said, use, k["A"]


NQ = sum(USES.get(stage, 0) for _, slot in SLOTS_Q for stage, _ in slot)
NP = sum(USES.get(stage, 0) for _, slot in SLOTS_P for stage, _ in slot) + NQ
P_USE, _k = {}, 0
for _, _slot in SLOTS_P + SLOTS_Q:
    for _stage in _slot:
        P_USE[_stage] = _k
        _k += USES.get(_stage[0], 0)
HEAD = [("h", "x", 0), ("h", "ln", 0), ("h", "lnr", 0), ("h", "lnf", 0), ("h", "lnn", 0), ("h", "lnTa", 0), ("h", "qk", 0), ("h", "load", 0)] + [("h", "max", (0, c)) for c in range(MAXIMA)] + \
       [("h", "mrow", 0)]
TAIL_Q = [("q",) + x for _, slot in SLOTS_Q for x in slot]
TAIL = [("o",) + x for slot in SLOTS_O for x in slot] + [("p",) + x for _, slot in SLOTS_P for x in slot]
FIRST, FIRST_USE, _k = numbered(HEAD, 0)
TURN0, TURN0_USE, _k0 = numbered(turn_of(True, False, False), _k)
TURN1, TURN1_USE, _k1 = numbered(turn_of(True, True, False), _k0)
NA = _k1 - _k0
TURN, TURN_USE, _ = numbered(turn_of(True, True, True), _k0 - NA)
TURN1, TURN1_USE, _ = numbered(turn_of(True, True, False), _k0 - NA)
TURN7, TURN7_USE, _k7 = numbered(turn_of(False, True, True), _k0 - NA)
LAST, LAST_USE, _ = numbered(TAIL_Q + TAIL, _k7)
DONE, DONE_USE, _ = numbered(TAIL_Q, 0)
assert NA % 2 == 0 and NP % 2 == 0


class Count:
    made = []

    def __init__(self, sem, per, unit=1):
        self.sem, self.per, self.unit = sem, per, unit
        Count.made.append(sem)

    def at(self, b, k):
        return self.sem, b * (self.per * self.unit) + (k * self.unit + 1)


class Ring:

    def __init__(self, banks, sem, name, uses):
        self.banks = banks
        self.ready = Count(sem(f"{name}_ready"), uses)
        self.evicted = [Count(sem(f"{name}_evicted{i}"), uses // 2) for i in range(2)]

    def bank(self, k):
        return self.banks[k % 2]

    def free(self, b, k):
        return self.evicted[k % 2].at(b, k // 2)

    def filled(self, b, k):
        return self.ready.at(b, k + 1)

    def moved(self, b, k):
        return self.evicted[k % 2].at(b, k // 2 + 1)

    def made(self, b, k, *uses):
        other = [u for u in uses if (u - k) % 2]
        return self.moved(b, max(other)) if other else self.free(b, k)

    def emptied(self, k):
        return self.evicted[k % 2].sem


def hybrid_block_kernel(nc, x, Wq, bq, Wk, bk, Wv, bv, Wo, bo, enc_q, enc_v, mn_w1, mn_b1, mn_w2, mn_b2,
                        base_metric, decoder, heb_U, heb_V, k0, k1, k2, s0, s1, s2, out):
    with ExitStack() as ctx:
        def sb(name, shape, dt=F32):
            return ctx.enter_context(nc.sbuf_tensor(name, shape, dt))

        def sem(name):
            return ctx.enter_context(nc.semaphore(name))

        def count(name, per, unit=1):
            return Count(sem(name), per, unit)

        Count.made.clear()
        psum = [ctx.enter_context(nc.psum_tensor(f"bank{i}", [P, HALF], F32)) for i in range(8)]
        A = Ring(psum[0:2], sem, "a", NA)
        R = Ring(psum[2:4], sem, "p", NP)
        st_bank = psum[4:7]
        ov_bank = psum[7]

        scratch_qk = nc.dram_tensor("scratch_qk", [2 * PARTS, P, T], BF16, kind="Internal").ap()
        scratch_m = nc.dram_tensor("scratch_m", [PARTS * 32, P], BF16, kind="Internal").ap()

        ident = sb("ident", [P, P])
        flip = sb("flip", [P, P])
        identb = sb("identb", [P, P], BF16)
        wT = sb("wT", [P, 4, P])
        wqkb = sb("wqkb", [P, 2])
        bvb = sb("bvb", [P, P])
        bob = sb("bob", [P, P])
        W0 = sb("W0", [P, NF])
        W1 = sb("W1", [P, FC, NF])
        W2 = sb("W2", [P, FC, P])
        scol = sb("scol", [P, 3])
        eq = sb("eq", [P, P])
        ev = sb("ev", [P, P])
        eqd = sb("eqd", [P, 2, P])
        w1m = sb("w1m", [P, P // 2])
        b1m = sb("b1m", [P // 2, 1])
        w2d = sb("w2d", [P // 2, 3, P])
        rows = sb("rows", [1, 2, 3, P])
        cols = sb("cols", [P, 2, 3])
        dec = sb("dec", [P, P])
        up = sb("up", [P, 4])
        ub = sb("ub", [P, SH, 4])
        uT = sb("uT", [32, P])
        vh = sb("vh", [32, SE])
        bdh = sb("bdh", [P, SH, SE])
        blk = sb("blk", [P, SH])
        half0 = sb("half0", [P, 4])
        half1 = sb("half1", [P, 4])
        any0 = sb("any0", [P, 1])
        any1 = sb("any1", [P, 1])
        minus1 = sb("minus1", [P, 4])
        offself = sb("offself", [P, 2, WW])
        outside = sb("outside", [P, WW])
        zeros3 = sb("zeros3", [PARTS, T], BF16)
        ones3 = sb("ones3", [PARTS, T], BF16)
        ones1 = sb("ones1", [1, 1])
        eps8 = sb("eps8", [P, 1])

        qkf = sb("qkf", [P, 2, T])
        xa = qkf[:, 0, :].rearrange("p (u c) -> p u c", c=P)
        xres = qkf[:, 1, :].rearrange("p (u c) -> p u c", c=P)
        xTa = sb("xTa", [P, T])
        pq = sb("pq", [P, 2 * PARTS, T], BF16)
        xna = pq[:, 0:2, :].bitcast(F32).rearrange("p a (u c) -> p (a u) c", c=P)
        Q = sb("Q", [P, 2, 2, T], BF16)
        K = sb("K", [P, 2, 4, T], BF16)
        Vg = sb("Vg", [P, NU, NH, VW])
        mred = sb("mred", [P, 32, 2])
        nm = sb("nm", [P, 3, 32])
        mb = sb("mb", [P, PARTS, 32], BF16)
        mT = sb("mT", [PARTS * 32, P], BF16)
        PT = sb("PT", [P, 8, HALF])
        oT = sb("oT", [P, NQUAD, T])
        rden = sb("rden", [P, 2, NH])
        on = sb("on", [P, 2, P])
        onT = sb("onT", [P, 2, P])

        xr = sb("xr", [P, NU, P])
        stat = sb("stat", [P, 2, NU, 6])
        mv = sb("mv", [P, 2, NU, 2])
        ls = sb("ls", [P, 2, 8, NU])
        xn = sb("xn", [P, NU, P])
        xT = sb("xT", [P, T])
        h1 = sb("h1", [P, FC, HALF])
        h2 = sb("h2", [P, FC, HALF])
        xrev = sb("xrev", [P, RPAD])
        qd = sb("qd", [P, 2, T])
        B = sb("B", [P, 2, RPAD])
        Bs = sb("Bs", [P, RPAD])
        qh = sb("qh", [P, T])
        sq = sb("sq", [P, T])
        sig = sb("sig", [P, 4])
        hid = sb("hid", [P // 2, 1])
        met = sb("met", [P, 6, 3])
        alpha = sb("alpha", [P, SH])
        beta = sb("beta", [P, 2])
        nb = sb("nb", [P, 16])
        an = sb("an", [P, NU, 16])
        gn = sb("gn", [P, 3, NU, SH])
        qtok = sb("qtok", [P, NU, P])
        hb = sq[:, :].rearrange("p (u c) -> p u c", c=P)
        Vw = sb("Vw", [WW, 2, NBLK, SH, SE + 1])
        Aop = sb("Aop", [P, SH, P])
        D = h1[:, 0:3, :].rearrange("p a c -> p (a c)").rearrange("p (i h c) -> p i h c", i=2, c=WW)
        E = h2[:, 0:3, :].rearrange("p a c -> p (a c)").rearrange("p (i h c) -> p i h c", i=2, c=WW)
        Rm = xn[:, :, 0:WW]
        m8 = h2[:, 3, P:P + 8 * SH].rearrange("p (h e) -> p h e", e=8)
        WT = Bs[:, 0:T].rearrange("p (h c) -> p h c", h=SH)
        rd = sb("rd", [P, 2, SH])
        s_tok, s_T = h1[:, 3, 0:P], h2[:, 3, 0:P]
        wload = oT[:, 0, :].rearrange("p (a c) -> p a c", a=8)[:, 0:4, :]
        kw0, kw1, kw2 = (PT[:, a:b, 0:w].bitcast(U32) for a, b, w in ((0, 2, P), (2, 6, P), (6, 7, P)))
        kw2 = kw2.rearrange("p o (a c) -> p (o a) c", a=FC)
        kb0, kb1, kb2 = kw0.bitcast(U8), kw1.bitcast(U8), kw2.bitcast(U8)
        kf = h1[:, 0:2, :]

        loaded = sem("weights_loaded")
        loadk = sem("signs_loaded")
        masks = sem("masks_made")
        setup_pe = sem("setup_products")
        setup_v = sem("setup_vector")
        u_spread = sem("u_spread")
        u_turned = sem("u_turned")
        rows_set = sem("one_rows_set")
        waits_passed = sem("waits_passed")
        steps_h = count("norm_steps", 6)
        steps_m = count("max_steps", 4 * NQUAD)
        steps_o = count("turn_steps", NU)
        steps_p = count("vector_steps", LINKS_P)
        res_in = count("residual_in", 1, 16)
        x_in = count("x_in", 1, 16)
        ln_a = count("ln_a", 1)
        ln_p = count("ln_p", 6)
        xpad = count("first_repeated", 1)
        met_z = count("metric_in", 1)
        met_e = count("metric_exp", 1)
        met_l = count("metric_ln", 1)
        gn_l = count("gate_ln", 1)
        e_steps = count("e_steps", 2 * NU)
        top8 = count("top8", NU * 8 * SH)
        var_a = count("var_a", 1)
        rs_a = count("rstd_a", 1)
        coef_a = count("norm_factors_a", 1)
        coef_p = count("norm_factors_p", 6)
        xn_a = count("xn_a", 1)
        xb_a = count("bias_added", 1)
        act_a = count("part_rounded", 4)
        pool_a = count("part_left", 4)
        split_out = count("split_out", 1, 16)
        quad_in = count("quad_in", NQUAD, 26 * 16)
        m_red = count("max_split", NQUAD)
        m_T = count("max_transposed", NQUAD)
        m_out = count("max_out", NQUAD, 16)
        m_in = count("max_in", NQUAD, 32)
        scores = count("scores", NQUAD * 64)
        probs = count("probs", NQUAD * 64)
        pv = count("pv", NQUAD * 16)
        o_out = count("o_out", NQUAD * 2)
        rd_a = count("rden_a", NU)
        var_p = count("var_p", 6)
        rs_p = count("rstd_p", 6)
        xn_p = count("xn_p", 6)
        sq_p = count("squares", 1)
        sig_p = count("sig_p", 1)
        met_p = count("metric", 1)
        bop = count("b_operand", 2)
        gn_v = count("gate_in", 1)
        gn_a = count("gate_norm", 1)
        aop_p = count("a_operand", NU)
        d_scaled = count("d_scaled", NU)
        d_pool = count("d_masked", NU)
        e_act = count("e_done", NU)
        w_v = count("w_done", NU)
        s_v = count("s_done", NU)
        out_p = count("out_done", 1, 16)
        block = ctx.enter_context(nc.Block())

        x_t = x.rearrange("b (u p) c -> b p u c", p=P)
        out_t = out.rearrange("b (u p) c -> b p u c", p=P)
        qk_s = scratch_qk.rearrange("s (h d) t -> s h d t", d=HD)
        m_t = scratch_m.rearrange("(s a i u) t -> s a i (u t)", s=PARTS, a=2, i=2)

        def pass_waits(eng):
            eng.sem_inc(waits_passed, 1)

        def window(w):
            return slice(T - BLK * (w + 1), T - BLK * (w + 1) + WW)

        def rows_of(bank, r):
            return bank[:, :].rearrange("p (a r) -> p a r", r=r)

        def cast(ap, dims):
            return ap.unsqueeze(len(dims) - 1).broadcast_to(dims)

        @block.sync
        def _(sp):
            n = 0

            for s in Count.made:
                sp.sem_inc(s, 1)

            def load(dst, src):
                nonlocal n
                sp.dma_start(dst, src).then_inc(loaded, 16)
                n += 1

            for i, w in enumerate((Wq, Wk, Wv, Wo)):
                load(wload[:, i, :], w)
            load(wqkb[:, 0:1], bq.rearrange("(p o) -> p o", o=1))
            load(wqkb[:, 1:2], bk.rearrange("(p o) -> p o", o=1))
            load(bvb[:, :], bv.partition_broadcast(P))
            load(bob[:, :], bo.partition_broadcast(P))
            for i, s in enumerate((s0, s1, s2)):
                load(scol[:, i:i + 1], s.partition_broadcast(P))
            load(eq[:, :].rearrange("d (n e) -> d n e", e=SE), enc_q.rearrange("n d e -> d n e"))
            load(ev[:, :].rearrange("d (n e) -> d n e", e=SE), enc_v.rearrange("n d e -> d n e"))
            ed = eqd[:, :, :].rearrange("d f (g s e) -> d f g s e", g=4, s=2)
            wd = w2d[:, :, :].rearrange("d f (g s e) -> d f g s e", g=4, s=2)
            rw = rows[:, :, :, :].rearrange("o v f (g s e) -> o v f g s e", g=4, s=2)
            vecs = (mn_b2.rearrange("(o n) -> o n", o=1), base_metric.rearrange("h e -> (h e)").rearrange("(o n) -> o n", o=1))
            for f in range(2):
                for s in range(2):
                    load(ed[:, f, :, s, :], enc_q[4 * f:4 * f + 4].rearrange("n d e -> d n e"))
                    load(wd[:, f, :, s, :], mn_w2[:, 64 * f:64 * f + 64].rearrange("d (g e) -> d g e", e=SE))
                    for v in range(2):
                        load(rw[:, v, f, :, s, :], vecs[v][:, 64 * f:64 * f + 64].rearrange("o (g e) -> o g e", e=SE))
            load(w2d[:, 2, :], mn_w2)
            for v in range(2):
                load(rows[:, v, 2, :], vecs[v])
            load(w1m[:, :], mn_w1)
            load(b1m[:, :], mn_b1.rearrange("(p o) -> p o", o=1))
            load(dec[:, :], decoder)
            load(vh[:, :], heb_V.rearrange("h r e -> (h r) e"))
            load(up[:, :], heb_U.rearrange("h e r -> (h e) r"))
            assert n == LOADS, n
            sp.dma_start(kw0, k0.rearrange("(a p) n -> p a n", p=P)).then_inc(loadk, 16)
            sp.dma_start(kw1, k1.rearrange("(a p) n -> p a n", p=P)).then_inc(loadk, 16)
            sp.dma_start(kw2, k2.rearrange("(a p) n -> p a n", p=P)).then_inc(loadk, 16)
            sp.wait_ge(masks, 1)
            for slot in range(2):
                for j in range(4):
                    r = 64 * (j % 2) + MROW
                    sp.dma_start(K[r:r + PARTS, slot, j, :], ones3[:, :]).then_inc(rows_set, 16)

            def go(work, use, c, **sequences):
                for side, stage, n, k in work:
                    b = sequences[side]
                    if stage == "x":
                        sp.wait_ge(*split_out.at(b, 0))
                        pass_waits(sp)
                        sp.dma_start(xa[:, :, :], x_t[b]).then_inc(x_in.sem, 16)
                    if stage == "residual":
                        if work is not TURN0:
                            sp.wait_ge(*R.moved(b - 1, use["fc", 1]))
                            pass_waits(sp)
                        sp.dma_start(xres[:, :, :], x_t[b]).then_inc(res_in.sem, 16)
                    if stage == "qk":
                        sp.wait_ge(*act_a.at(b, 4))
                        pass_waits(sp)
                        sp.wait_ge(*pool_a.at(b, 4))
                        pass_waits(sp)
                        sp.wait_ge(*quad_in.at(b, 0))
                        pass_waits(sp)
                        sp.dma_start(scratch_qk.rearrange("s c t -> c s t"), pq[:, :, :]).then_inc(split_out.sem, 16)
                    if stage == "load":
                        slot = n % 2
                        sp.wait_ge(*split_out.at(b, 1))
                        pass_waits(sp)
                        if work is not FIRST:
                            sp.wait_ge(*scores.at(b, 4 * STEPS * (n - 1)))
                            pass_waits(sp)
                        for par in range(2):
                            h = slice(4 * n + par, 4 * n + par + 3, 2)
                            for first, parts, part in QLOAD:
                                for i in range(2):
                                    r = 64 * par + HD * first
                                    sp.dma_start(Q[r:r + HD * parts, slot, i, :],
                                                 qk_s[part:part + 1, 4 * n + par + 2 * i].broadcast_to([parts, HD, T])).then_inc(quad_in.sem, 16)
                            for first, parts, part in KLOAD:
                                for i in range(2):
                                    r = 64 * par + HD * first
                                    sp.dma_start(K[r:r + HD * parts, slot, par + 2 * i, :],
                                                 qk_s[PARTS + part:PARTS + part + parts, 4 * n + par + 2 * i]).then_inc(quad_in.sem, 16)
                            r = 64 * par + MROW
                            sp.dma_start(Q[r:r + PARTS, slot, :, :],
                                         zeros3[:, :].unsqueeze(1).broadcast_to([PARTS, 2, T])).then_inc(quad_in.sem, 16)
                    if stage == "mrow":
                        sp.wait_ge(*A.moved(c, k))
                        pass_waits(sp)
                        sp.wait_ge(*m_in.at(b, n))
                        pass_waits(sp)
                        sp.dma_start(scratch_m, mT[:, :]).then_inc(m_out.sem, 16)
                        sp.wait_ge(*m_out.at(b, n + 1))
                        pass_waits(sp)
                        for par in range(2):
                            r = 64 * par + MROW
                            sp.dma_start(Q[r:r + PARTS, n % 2, :, :], m_t[:, par]).then_inc(m_in.sem, 16)
                    if stage == "out":
                        sp.wait_ge(*R.moved(b, NP - 1))
                        pass_waits(sp)
                        sp.dma_start(out_t[b], xr[:, :, :]).then_inc(out_p.sem, 16)

            sp.wait_ge(rows_set, 16 * 8)
            go(FIRST, FIRST_USE, 0, h=0)
            go(TURN0, TURN0_USE, 0, h=1, a=0)
            go(TURN1, TURN1_USE, 1, h=2, a=1, o=0, p=0)
            with sp.Fori(2, NB - 1) as c:
                go(TURN, TURN_USE, c, h=c + 1, a=c, o=c - 1, p=c - 1, q=c - 2)
            go(TURN7, TURN7_USE, NB - 1, a=NB - 1, o=NB - 2, p=NB - 2, q=NB - 3)
            go(LAST, LAST_USE, NB - 1, o=NB - 1, p=NB - 1, q=NB - 2)
            go(DONE, DONE_USE, NB - 1, q=NB - 1)
            sp.wait_ge(*out_p.at(NB, 0))
            pass_waits(sp)

        @block.gpsimd
        def _(pool):
            def select(dst, pattern, base, mult, fill, op=ALU.is_ge):
                link(pool.affine_select(out=dst, in_=dst, compare_op=op, fill=fill, base=base,
                                        pattern=pattern, channel_multiplier=mult))

            step = sem("pool_setup")
            done = [0]

            def link(ins):
                done[0] += 1
                ins.then_inc(step, 1)
                pool.wait_ge(step, done[0])

            link(pool.memset(K[:, :, :, :], 0.0))
            link(pool.memset(zeros3[:, :], 0.0))
            link(pool.memset(ones3[:, :], 1.0))
            pool.sem_inc(masks, 1)
            link(pool.memset(Q[:, :, :, :], 0.0))
            link(pool.memset(Vg[:, :, :, :], 0.0))
            link(pool.memset(Vg[:, :, :, HD:HD + 1], 1.0))
            link(pool.memset(Vw[:, :, :, :, SE:SE + 1], 1.0))
            link(pool.memset(ones1[:, :], 1.0))
            link(pool.memset(eps8[:, :], 1e-8))
            for t in (ident, flip, identb):
                link(pool.memset(t[:, :], 0.0))
            select(ident[:, :], [[-1, P]], 0, 1, 1.0, ALU.not_equal)
            select(identb[:, :], [[-1, P]], 0, 1, 1.0, ALU.not_equal)
            select(flip[:, :], [[1, P]], 1 - P, 1, 1.0, ALU.not_equal)
            for t, width, step_, lo in ((blk, SH, SE, 0), (half0, 4, 2 * SE, 0), (half1, 4, 2 * SE, SE)):
                link(pool.memset(t[:, :], 1.0))
                select(t[:, :], [[-step_, width]], -lo, 1, 0.0)
                select(t[:, :], [[step_, width]], lo + SE - 1, -1, 0.0)
            link(pool.memset(outside[:, :], 0.0))
            link(pool.memset(offself[:, :, :], -1.0))
            for i in range(NBLK):
                o = outside[BLK * i:BLK * i + BLK, :]
                select(o, [[1, WW]], 1 - BLK, 1, -BIG)
                select(o, [[-1, WW]], WIN + BLK - 2, -1, -BIG)
                for v in range(2):
                    select(offself[BLK * i:BLK * i + BLK, v, :], [[1, WW]], 1 - BLK, 1, 0.0, ALU.not_equal)
            link(pool.memset(offself[0:1, 1, :], 0.0))
            pool.sem_inc(masks, 1)

            def go(work, use, c, **sequences):
                for side, stage, n, k in work:
                    b = sequences[side]
                    if stage == "residual":
                        pool.wait_ge(*res_in.at(b, 1))
                        pool.tensor_tensor(xres[:, :, :], xres[:, :, :], bob[:, :].unsqueeze(1).broadcast_to([P, NU, P]),
                                           ALU.add).then_inc(xb_a.sem, 1)
                    if stage == "qk":
                        for w in range(2):
                            pool.wait_ge(*act_a.at(b, w + 1))
                            pool.tensor_tensor(qkf[:, w, :], qkf[:, w, :], pq[:, 3 * w, :], ALU.subtract).then_inc(pool_a.sem, 1)
                        for w in range(2):
                            pool.wait_ge(*act_a.at(b, w + 3))
                            pool.tensor_tensor(pq[:, 3 * w + 2, :], qkf[:, w, :], pq[:, 3 * w + 1, :],
                                               ALU.subtract).then_inc(pool_a.sem, 1)
                    if (stage, n) == ("he", 1):
                        pool.wait_ge(*R.moved(b, k - 1))
                        pool.wait_ge(*R.moved(b, k))
                        pool.tensor_tensor(sq[:, :], qh[:, :], qh[:, :], ALU.mult).then_inc(sq_p.sem, 1)
                    if stage == "aop":
                        if n == 0:
                            pool.wait_ge(*met_p.at(b, 1))
                            pool.wait_ge(*R.moved(b, use["qd", 2]))
                            pool.wait_ge(*R.moved(b, use["qd", 3]))
                        else:
                            pool.wait_ge(*R.filled(b, use["dist", n - 1] + 1))
                        pass_waits(pool)
                        for h in range(SH):
                            ins = pool.tensor_scalar(Aop[:, h, :], qd[:, h // 4, P * n:P * n + P], alpha[:, h:h + 1],
                                                     minus1[:, h % 4:h % 4 + 1], ALU.mult, ALU.add)
                        ins.then_inc(aop_p.sem, 1)
                    if stage == "dev":
                        d = D[:, n % 2, :, :]
                        pool.wait_ge(*R.moved(b, use["dist", n]))
                        pool.wait_ge(*R.moved(b, use["dist", n] + 1))
                        m = offself[:, 1 if n == 0 else 0, :].unsqueeze(1).broadcast_to([P, SH, WW])
                        pool.tensor_tensor(d, d, m, ALU.mult).then_inc(d_scaled.sem, 1)
                        pool.wait_ge(*d_scaled.at(b, n + 1))
                        pool.tensor_tensor(d, d, outside[:, :].unsqueeze(1).broadcast_to([P, SH, WW]),
                                           ALU.add).then_inc(d_pool.sem, 1)

            go(FIRST, FIRST_USE, 0, h=0)
            go(TURN0, TURN0_USE, 0, h=1, a=0)
            go(TURN1, TURN1_USE, 1, h=2, a=1, o=0, p=0)
            with pool.Fori(2, NB - 1) as c:
                go(TURN, TURN_USE, c, h=c + 1, a=c, o=c - 1, p=c - 1, q=c - 2)
            go(TURN7, TURN7_USE, NB - 1, a=NB - 1, o=NB - 2, p=NB - 2, q=NB - 3)
            go(LAST, LAST_USE, NB - 1, o=NB - 1, p=NB - 1, q=NB - 2)
            go(DONE, DONE_USE, NB - 1, q=NB - 1)

        @block.tensor
        def _(pe):
            def mm(o, l, r, start=True, stop=True):
                return pe.matmul(o, l, r, start=start, stop=stop)

            pe.wait_ge(loaded, LOADS * 16)
            pe.wait_ge(masks, 2)
            for i in range(4):
                ins = pe.transpose(psum[0][:, P * i:P * i + P], wload[:, i, :], ident[:, :])
            for v in range(2):
                for f in range(3):
                    ins = mm(psum[1][:, 3 * v + f:3 * v + f + 1], rows[0:1, v, f, :], ones1[:, :])
            ins.then_inc(setup_pe, 1)
            pe.wait_ge(u_spread, 1)
            pe.transpose(psum[3][0:32, 0:P], ub[:, :, :].rearrange("p h r -> p (h r)"), ident[:, :]).then_inc(setup_pe, 1)
            pe.wait_ge(u_turned, 1)
            mm(psum[2][:, 0:SE], uT[:, :], vh[:, :]).then_inc(setup_pe, 1)

            def transposed(ring, b, k, src, perm, tiles):
                pe.wait_ge(*ring.free(b, k))
                for q, u in enumerate(tiles):
                    ins = pe.transpose(ring.bank(k)[:, P * q:P * q + P], src[:, u, :], perm)
                ins.then_inc(ring.ready.sem, 1)

            def one(ring, b, k, products):
                pe.wait_ge(*ring.free(b, k))
                for o, l, r, start, stop in products:
                    ins = mm(o, l, r, start, stop)
                ins.then_inc(ring.ready.sem, 1)

            def pv_step(b, n, i):
                s = STEPS * n + i
                pe.wait_ge(*probs.at(b, 4 * (s + 1)))
                if i % 8 == 0:
                    pe.wait_ge(*o_out.at(b, 2 * n + i // 8))
                for j in range(4):
                    ins = mm(ov_bank[VW * j:VW * j + VW, :], Vg[:, i % 8, 4 * n + j, :], PT[:, (4 * s + j) % 8, :],
                             i % 8 == 0, i % 8 == 7)
                ins.then_inc(pv.sem, 1)

            def go(work, use, c, **sequences):
                for side, stage, n, k in work:
                    b = sequences[side]
                    if stage == "lnTa":
                        pe.wait_ge(*xn_a.at(b, 1))
                        for i in range(2):
                            transposed(A, c, k + i, xna, ident[:, :], range(4 * i, 4 * i + 4))
                    if stage == "qk":
                        pe.wait_ge(*A.made(c, k, use["lnTa", 0], use["lnTa", 0] + 1))
                        for w in range(2):
                            for h in range(2):
                                at = k + 2 * w + h
                                one(A, c, at, [(A.bank(at)[:, :], wT[:, w, :], xTa[:, HALF * h:HALF * h + HALF], True, True)])
                    if stage == "v":
                        for i in range(2):
                            at = k + i
                            one(A, c, at, [(A.bank(at)[:, P * q:P * q + P], xTa[:, P * (4 * i + q):P * (4 * i + q) + P],
                                             wT[:, 2, :], True, True) for q in range(4)])
                    if stage == "max":
                        n, i = n
                        if i == 0:
                            pe.wait_ge(*quad_in.at(b, n + 1))
                        j, qt, h = i // 2 // NU, i // 2 % NU, i % 2
                        one(A, c, k, [(A.bank(k)[:, :], Q[:, n % 2, j // 2, P * qt:P * qt + P],
                                       K[:, n % 2, j, HALF * h:HALF * h + HALF], True, True)])
                    if stage == "mrow":
                        pe.wait_ge(*m_red.at(b, n + 1))
                        pe.wait_ge(*A.free(c, k))
                        pe.transpose(A.bank(k)[0:PARTS * 32, 0:P // 2].bitcast(BF16), mb[:, :], identb[:, :]).then_inc(A.ready.sem, 1)
                    if stage == "exp":
                        n, (i, j) = n[0], divmod(n[1], 4)
                        if (i, j) == (0, 0):
                            pe.wait_ge(*m_in.at(b, n + 1))
                        g = 4 * (STEPS * n + i) + j
                        pe.wait_ge(*probs.at(b, max(g - 2, 0)))
                        mm(st_bank[g % 3][:, :], K[:, n % 2, j, P * (i % 8):P * (i % 8) + P],
                           Q[:, n % 2, j // 2, HALF * (i // 8):HALF * (i // 8) + HALF]).then_inc(scores.sem, 1)
                        if (n, i, j) == (0, 1, 1):
                            pe.wait_ge(*A.moved(c, use["v", 0]))
                            pe.wait_ge(*A.moved(c, use["v", 0] + 1))
                        if i >= 1 and j == 1:
                            pv_step(b, n, i - 1)
                    if stage == "fin":
                        pv_step(b, n, STEPS - 1)
                    if stage == "turn":
                        if n == 0:
                            pe.wait_ge(*o_out.at(b, 2 * NQUAD))
                        pe.wait_ge(*A.free(c, k))
                        for q in range(NQUAD):
                            ins = pe.transpose(A.bank(k)[:, P * q:P * q + P], oT[:, q, P * n:P * n + P], ident[:, :])
                        ins.then_inc(A.ready.sem, 1)
                    if stage == "back":
                        pe.wait_ge(*A.made(c, k, use["turn", n]))
                        pe.wait_ge(*A.free(c, k))
                        pe.transpose(A.bank(k)[:, 0:P], on[:, n % 2, :], ident[:, :]).then_inc(A.ready.sem, 1)
                    if stage == "wo":
                        pe.wait_ge(*A.made(c, k, use["back", n]))
                        one(A, c, k, [(A.bank(k)[:, 0:P], onT[:, n % 2, :], wT[:, 3, :], True, True)])
                    if stage == "lnT":
                        n, i = n
                        pe.wait_ge(*xn_p.at(b, 2 * n + i + 1))
                        transposed(R, b, k, xn, ident[:, :], range(4 * i, 4 * i + 4))
                    if stage == "fa":
                        n, o = n
                        if o == 0:
                            pe.wait_ge(*R.made(b, k, use["lnT", (n // 2 * 2, n % 2)]))
                        one(R, b, k, [(R.bank(k)[:, :], W0[:, P * o:P * o + P], xT[:, HALF * (n % 2):HALF * (n % 2) + HALF], True, True)])
                    if stage == "fb":
                        n, o = n
                        if o == 0:
                            pe.wait_ge(*R.made(b, k, use["fa", (n, 2)], use["fa", (n, 3)]))
                        one(R, b, k, [(R.bank(k)[:, :], W1[:, c, P * o:P * o + P], h1[:, c, :], c == 0, c == FC - 1)
                                      for c in range(FC)])
                    if stage == "fc":
                        pe.wait_ge(*R.made(b, k, use["fb", (n, 2)], use["fb", (n, 3)]))
                        one(R, b, k, [(R.bank(k)[:, P * q:P * q + P], h2[:, c, P * q:P * q + P], W2[:, c, :],
                                       c == 0, c == FC - 1) for q in range(4) for c in range(FC)])
                    if stage == "flip":
                        transposed(R, b, k, xn, flip[:, :], [NU - 1 - (4 * n + q) for q in range(4)])
                    if stage == "he":
                        if n == 0:
                            pe.wait_ge(*R.made(b, k, use["lnT", (1, 0)], use["lnT", (1, 1)]))
                        one(R, b, k, [(R.bank(k)[:, :], eq[:, :], xT[:, HALF * n:HALF * n + HALF], True, True)])
                    if stage == "hid":
                        pe.wait_ge(*sig_p.at(b, 1))
                        one(R, b, k, [(R.bank(k)[0:P // 2, 0:1], w1m[:, :], sig[:, 3:4], True, True)])
                    if stage == "mod":
                        pe.wait_ge(*R.made(b, k, use["hid", 0]))
                        one(R, b, k, [(R.bank(k)[:, f:f + 1], w2d[:, f, :], hid[:, :], True, True) for f in range(3)])
                    if stage == "qd":
                        h = n % 2
                        one(R, b, k, [(R.bank(k)[:, :], eqd[:, n // 2, :], xT[:, HALF * h:HALF * h + HALF], True, True)])
                    if stage == "key":
                        h = n % 2
                        if n == 0:
                            pe.wait_ge(*R.made(b, k, use["flip", 0], use["flip", 1]))
                        one(R, b, k, [(R.bank(k)[:, :], eqd[:, n // 2, :], xrev[:, HALF * h:HALF * h + HALF], True, True)])
                    if stage == "pad":
                        pe.wait_ge(*xpad.at(b, 1))
                        one(R, b, k, [(R.bank(k)[:, WIN * f:WIN * f + WIN], eqd[:, f, :], xrev[:, T:RPAD], True, True)
                                      for f in range(2)])
                    if stage == "an":
                        pe.wait_ge(*met_p.at(b, 1))
                        pe.wait_ge(*sq_p.at(b, 1))
                        one(R, b, k, [(R.bank(k)[:, 16 * u:16 * u + 16], sq[:, P * u:P * u + P], nb[:, :], True, True)
                                      for u in range(NU)])
                    if stage == "qtok":
                        one(R, b, k, [(R.bank(k)[:, P * q:P * q + P], xT[:, P * (4 * n + q):P * (4 * n + q) + P],
                                       eq[:, :], True, True) for q in range(4)])
                    if stage == "hebb":
                        one(R, b, k, [(R.bank(k)[:, P * q:P * q + P], qh[:, P * (4 * n + q):P * (4 * n + q) + P],
                                       bdh[:, :, :], True, True) for q in range(4)])
                    if stage == "dist":
                        pe.wait_ge(*aop_p.at(b, n + 1))
                        if n == 0:
                            pe.wait_ge(*bop.at(b, 2))
                        for f in range(2):
                            one(R, b, k + f, [(R.bank(k + f)[BLK * i:BLK * i + BLK, WW * j:WW * j + WW],
                                               Aop[:, 4 * f + j, BLK * i:BLK * i + BLK], B[:, f, window(NBLK * n + i)], True, True)
                                              for j in range(4) for i in range(NBLK)])
                    if stage == "vw":
                        one(R, b, k, [(R.bank(k)[0:WW, P * i:P * i + P], xrev[:, window(NBLK * n + i)], ev[:, :], True, True)
                                      for i in range(NBLK)])
                    if stage == "wt":
                        pe.wait_ge(*w_v.at(b, n + 1))
                        for i in range(2):
                            pe.wait_ge(*R.free(b, k + i))
                            for q in range(4):
                                ins = pe.transpose(R.bank(k + i)[0:WW, P * q:P * q + P], E[:, n % 2, 4 * i + q, :], ident[:, :])
                            ins.then_inc(R.ready.sem, 1)
                    if stage == "pv":
                        pe.wait_ge(*R.made(b, k, use["vw", n], use["wt", n], use["wt", n] + 1))
                        one(R, b, k, [(R.bank(k)[BLK * i:BLK * i + BLK, 32 * h:32 * h + SE + 1], WT[0:WW, h, BLK * i:BLK * i + BLK],
                                       Vw[:, n % 2, i, h, :], True, True) for h in range(SH) for i in range(NBLK)])
                    if stage == "st":
                        pe.wait_ge(*s_v.at(b, n + 1))
                        pe.wait_ge(*R.free(b, k))
                        pe.transpose(R.bank(k)[:, 0:P], s_tok[:, :], ident[:, :]).then_inc(R.ready.sem, 1)
                    if stage == "dec":
                        pe.wait_ge(*R.made(b, k, use["st", n]))
                        one(R, b, k, [(R.bank(k)[:, 0:P], s_T[:, :], dec[:, :], True, True)])

            pe.wait_ge(setup_v, 1)
            go(FIRST, FIRST_USE, 0, h=0)
            go(TURN0, TURN0_USE, 0, h=1, a=0)
            go(TURN1, TURN1_USE, 1, h=2, a=1, o=0, p=0)
            with pe.Fori(2, NB - 1) as c:
                go(TURN, TURN_USE, c, h=c + 1, a=c, o=c - 1, p=c - 1, q=c - 2)
            go(TURN7, TURN7_USE, NB - 1, a=NB - 1, o=NB - 2, p=NB - 2, q=NB - 3)
            go(LAST, LAST_USE, NB - 1, o=NB - 1, p=NB - 1, q=NB - 2)
            go(DONE, DONE_USE, NB - 1, q=NB - 1)

        @block.scalar
        def _(act):
            def evict(ring, b, k, dst, src, func=ACT.Identity, **kw):
                act.wait_ge(*ring.filled(b, k))
                return act.activation(dst, src, func, **kw).then_inc(ring.emptied(k), 1)

            def copy_out(b, n, h):
                act.wait_ge(*pv.at(b, STEPS * n + 8 * (h + 1)))
                act.activation(oT[:, n, HALF * h:HALF * h + HALF], ov_bank[:, :], ACT.Identity).then_inc(o_out.sem, 1)

            act.wait_ge(setup_v, 1)
            act.preload_act_table_set(EXP_LN)

            def go(work, use, c, **sequences):
                for side, stage, n, k in work:
                    b = sequences[side]
                    ring, r, l, dst = (R, b, ls[:, 1], xT) if side in "pq" else (A, c, ls[:, 0], xTa)
                    if stage in ("lnr", "lnn"):
                        var, ln, rs, coef, done = (var_a, ln_a, rs_a, coef_a, xn_a) if side == "h" else (var_p, ln_p, rs_p, coef_p, xn_p)
                        tiles, i, of, to = (range(NU), 1, xa, xna) if side == "h" else \
                            (range(4 * n[1], 4 * n[1] + 4), 2 * n[0] + n[1] + 1, xr if n[0] else xres, xn)
                        us = slice(tiles[0], tiles[-1] + 1)
                    if stage == "lnr":
                        act.wait_ge(*var.at(b, i))
                        act.activation(l[:, 1, us], l[:, 0, us], ACT.Ln).then_inc(ln.sem, 1)
                        act.wait_ge(*ln.at(b, i))
                        act.activation(l[:, 2, us], l[:, 1, us], ACT.Exp, scale=-0.5).then_inc(rs.sem, 1)
                    if stage == "lnn":
                        act.wait_ge(*coef.at(b, i))
                        for u in tiles:
                            ins = act.activation(to[:, u, :], of[:, u, :], ACT.Identity, scale=l[:, 6, u:u + 1], bias=l[:, 7, u:u + 1])
                        ins.then_inc(done.sem, 1)
                    if stage == "lnTa":
                        for i in range(2):
                            evict(ring, r, k + i, dst[:, HALF * i:HALF * i + HALF], ring.bank(k + i)[:, :])
                    if stage == "lnT":
                        evict(ring, r, k, dst[:, HALF * n[1]:HALF * n[1] + HALF], ring.bank(k)[:, :])
                    if stage == "qk":
                        for w in range(2):
                            for h in range(2):
                                evict(A, c, k + 2 * w + h, qkf[:, w, HALF * h:HALF * h + HALF], A.bank(k + 2 * w + h)[:, :],
                                      bias=wqkb[:, w:w + 1], scale=SCALE if w == 0 else 1.0)
                            act.wait_ge(*A.moved(c, k + 2 * w))
                            act.wait_ge(*A.moved(c, k + 2 * w + 1))
                            if w == 0:
                                act.wait_ge(*split_out.at(b, 0))
                            act.activation(pq[:, 3 * w, :], qkf[:, w, :], ACT.Identity).then_inc(act_a.sem, 1)
                        for w in range(2):
                            act.wait_ge(*pool_a.at(b, w + 1))
                            act.activation(pq[:, 3 * w + 1, :], qkf[:, w, :], ACT.Identity).then_inc(act_a.sem, 1)
                    if stage == "mrow":
                        act.wait_ge(*m_out.at(b, n))
                        evict(A, c, k, mT[:, :], A.bank(k)[0:PARTS * 32, 0:P // 2].bitcast(BF16))
                    if stage == "exp":
                        n, (i, j) = n[0], divmod(n[1], 4)
                        s = STEPS * n + i
                        if j == 0:
                            act.wait_ge(*pv.at(b, max(s - 1, 0)))
                        act.wait_ge(*scores.at(b, 4 * s + j + 1))
                        act.activation(PT[:, (4 * s + j) % 8, :], st_bank[(4 * s + j) % 3][:, :], ACT.Exp).then_inc(probs.sem, 1)
                        if (i, j) == (8, 3):
                            copy_out(b, n, 0)
                    if stage == "fin":
                        copy_out(b, n, 1)
                    if stage == "back":
                        evict(A, c, k, onT[:, n % 2, :], A.bank(k)[:, 0:P])
                    if stage in ("fa", "fb"):
                        n, o = n
                        h, i = (h1, 0) if stage == "fa" else (h2, 1)
                        evict(R, b, k, h[:, o, :], R.bank(k)[:, :], ACT.Relu, scale=scol[:, i:i + 1])
                    if stage == "flip":
                        evict(R, b, k, xrev[:, HALF * n:HALF * n + HALF], R.bank(k)[:, :])
                    if stage == "he":
                        act.wait_ge(*R.filled(b, k))
                        act.activation(qh[:, HALF * n:HALF * n + HALF], R.bank(k)[:, :], ACT.Relu,
                                       accum_out=sig[:, n:n + 1]).then_inc(R.emptied(k), 1)
                    if stage == "hid":
                        evict(R, b, k, hid[:, :], R.bank(k)[0:P // 2, 0:1], ACT.Gelu, bias=b1m[:, :])
                        act.preload_act_table_set(EXP_LN)
                    if stage == "key" and n == 0:
                        act.wait_ge(*met_z.at(b, 1))
                        act.activation(met[:, 3, :], met[:, 2, :], ACT.Exp, scale=-1.0).then_inc(met_e.sem, 1)
                        act.wait_ge(*met_e.at(b, 1))
                        act.activation(met[:, 4, :], met[:, 3, :], ACT.Ln, bias=1.0).then_inc(met_l.sem, 1)
                    if stage in ("qd", "key"):
                        dst = qd if stage == "qd" else B
                        h = n % 2
                        evict(R, b, k, dst[:, n // 2, HALF * h:HALF * h + HALF], R.bank(k)[:, :], ACT.Relu)
                    if stage == "pad":
                        evict(R, b, k, B[:, :, T:RPAD], R.bank(k)[:, 0:2 * WIN].rearrange("p (f w) -> p f w", f=2), ACT.Relu)
                    if stage == "an":
                        evict(R, b, k, an[:, :, :], R.bank(k)[:, 0:P].rearrange("p (u h) -> p u h", u=NU))
                    if stage == "qtok":
                        evict(R, b, k, qtok[:, 4 * n:4 * n + 4, :], rows_of(R.bank(k), P), ACT.Relu)
                    if stage == "gate":
                        act.wait_ge(*gn_v.at(b, 1))
                        act.activation(gn[:, 1, :, :], gn[:, 0, :, :], ACT.Ln).then_inc(gn_l.sem, 1)
                        act.wait_ge(*gn_l.at(b, 1))
                        act.activation(gn[:, 1, :, :], gn[:, 1, :, :], ACT.Exp, scale=-0.5).then_inc(gn_a.sem, 1)
                    if stage == "dev":
                        if n == 0:
                            act.wait_ge(*R.moved(b, use["an", 0]))
                        if n >= 2:
                            act.wait_ge(*top8.at(b, (4 * (n - 2) + 1) * 2 * SH))
                        for f in range(2):
                            k = use["dist", n] + f
                            act.wait_ge(*R.filled(b, k))
                            for j in range(4):
                                h = 4 * f + j
                                ins = act.activation(D[:, n % 2, h, :], R.bank(k)[:, WW * j:WW * j + WW], ACT.Relu,
                                                     scale=-1.0, bias=an[:, n, SH + h:SH + h + 1])
                            ins.then_inc(R.emptied(k), 1)
                    if stage == "top":
                        n, r = n[0], n[1] / 2
                        e = E[:, n % 2, :, :]
                        if r == 0:
                            act.wait_ge(*d_pool.at(b, n + 1))
                            act.activation(e, D[:, n % 2, :, :], ACT.Ln, scale=-1.0, bias=eps8[:, :]).then_inc(e_steps.sem, 1)
                        if r == 1:
                            act.wait_ge(*e_steps.at(b, 2 * n + 1))
                            act.activation(e, e, ACT.Exp, scale=0.5).then_inc(e_steps.sem, 1)
                        if r == 2:
                            act.wait_ge(*e_steps.at(b, 2 * n + 2))
                            act.activation(e, e, ACT.Exp, scale=-1.0).then_inc(e_act.sem, 1)
                    if stage == "vw":
                        evict(R, b, k, Vw[:, n % 2, :, :, 0:SE],
                              R.bank(k)[0:WW, :].rearrange("p (w h e) -> p w h e", w=NBLK, h=SH), ACT.Relu)
                    if stage == "wt":
                        for i in range(2):
                            evict(R, b, k + i, WT[0:WW, 4 * i:4 * i + 4, :], rows_of(R.bank(k + i), P)[0:WW])
                    if stage == "st":
                        evict(R, b, k, s_T[:, :], R.bank(k)[:, 0:P])

            go(FIRST, FIRST_USE, 0, h=0)
            go(TURN0, TURN0_USE, 0, h=1, a=0)
            go(TURN1, TURN1_USE, 1, h=2, a=1, o=0, p=0)
            with act.Fori(2, NB - 1) as c:
                go(TURN, TURN_USE, c, h=c + 1, a=c, o=c - 1, p=c - 1, q=c - 2)
            go(TURN7, TURN7_USE, NB - 1, a=NB - 1, o=NB - 2, p=NB - 2, q=NB - 3)
            go(LAST, LAST_USE, NB - 1, o=NB - 1, p=NB - 1, q=NB - 2)
            go(DONE, DONE_USE, NB - 1, q=NB - 1)

        @block.vector
        def _(dve):
            setup_step = sem("vector_setup")
            done = [0]

            def then(ins):
                done[0] += 1
                ins.then_inc(setup_step, 1)
                dve.wait_ge(setup_step, done[0])

            dve.wait_ge(loaded, LOADS * 16)
            dve.wait_ge(loadk, 48)
            dve.wait_ge(masks, 2)
            then(dve.tensor_copy(kf, kb0))
            then(dve.tensor_tensor(kf[:, 0, :], kf[:, 0, :], kf[:, 1, :], ALU.subtract))
            then(dve.tensor_scalar(W0[:, :], kf[:, 0, :], 2.0, None, ALU.mult))
            then(dve.tensor_scalar(W1[:, :, :], kb1, 2.0, -1.0, ALU.mult, ALU.add))
            then(dve.tensor_scalar(W2[:, :, :], kb2, 2.0, -1.0, ALU.mult, ALU.add))
            then(dve.tensor_scalar(scol[:, 0:2], scol[:, 0:2], 2.0, None, ALU.mult))
            then(dve.tensor_scalar(wqkb[:, 0:1], wqkb[:, 0:1], SCALE, None, ALU.mult))
            then(dve.tensor_reduce(any0[:, :], half0[:, :], AX.X, ALU.add))
            then(dve.tensor_reduce(any1[:, :], half1[:, :], AX.X, ALU.add))
            then(dve.tensor_scalar(minus1[:, :], half1[:, :], -1.0, None, ALU.mult))
            dve.wait_ge(setup_pe, 1)
            then(dve.tensor_copy(wT[:, :, :], rows_of(psum[0], P)))
            then(dve.tensor_copy(cols[:, :, :], psum[1][:, 0:6].rearrange("p (v f) -> p v f", v=2)))
            dve.tensor_tensor(ub[:, :, :], up[:, :].unsqueeze(1).broadcast_to([P, SH, 4]), cast(blk[:, :], [P, SH, 4]),
                              ALU.mult).then_inc(u_spread, 1)
            dve.wait_ge(setup_pe, 2)
            dve.tensor_copy(uT[:, :], psum[3][0:32, 0:P]).then_inc(u_turned, 1)
            dve.wait_ge(setup_pe, 3)
            then(dve.tensor_copy(bdh[:, :, :], psum[2][:, 0:SE].unsqueeze(1).broadcast_to([P, SH, SE])))
            then(dve.tensor_tensor(bdh[:, :, :], bdh[:, :, :], cast(blk[:, :], [P, SH, SE]), ALU.mult))
            then(dve.tensor_copy(nb[:, 0:SH], blk[:, :]))
            dve.sem_inc(setup_v, 1)

            def variances(b, link, side, us, src, var):
                l, st, m = ls[:, side], stat[:, side], mv[:, side]
                for u in range(us.start, us.stop):
                    ins = dve.bn_stats(st[:, u, :], src[:, u, :])
                link(ins, carried=True)
                for u in range(us.start, us.stop):
                    ins = dve.bn_aggr(m[:, u, :], st[:, u, :])
                link(ins)
                dve.tensor_scalar(l[:, 0, us], m[:, us, 1], LN_EPS, None, ALU.add).then_inc(var.sem, 1)

            def factors(b, i, link, side, us, rs, coef):
                l, m = ls[:, side], mv[:, side]
                dve.wait_ge(*rs.at(b, i))
                link(dve.tensor_tensor(l[:, 3, us], l[:, 2, us], l[:, 2, us], ALU.mult))
                link(dve.tensor_tensor(l[:, 4, us], l[:, 3, us], l[:, 0, us], ALU.mult))
                link(dve.tensor_scalar(l[:, 5, us], l[:, 4, us], -0.5, 1.5, ALU.mult, ALU.add))
                link(dve.tensor_tensor(l[:, 6, us], l[:, 5, us], l[:, 2, us], ALU.mult))
                dve.scalar_tensor_tensor(out=l[:, 7, us], in0=m[:, us, 0], scalar=-1.0, in1=l[:, 6, us],
                                         op0=ALU.mult, op1=ALU.mult).then_inc(coef.sem, 1)

            def chain(steps, b, done):
                n = [done]

                def link(ins, carried=False):
                    n[0] += 1
                    ins.then_inc(steps.sem, 1)
                    dve.wait_ge(*steps.at(b, n[0]))
                    if carried:
                        pass_waits(dve)

                link.done = n
                return link

            def go(work, use, c, **sequences):
                link_p, link_q = chain(steps_p, sequences.get("p"), 0), chain(steps_p, sequences.get("q"), LINKS_P - LINKS_Q)
                for side, stage, n, k in work:
                    b = sequences[side]
                    link = link_q if side == "q" else link_p
                    if (side, stage) == ("h", "ln"):
                        dve.wait_ge(*x_in.at(b, 1))
                        variances(b, chain(steps_h, b, 0), 0, slice(0, NU), xa, var_a)
                    if (side, stage) == ("h", "lnf"):
                        factors(b, 1, chain(steps_h, b, 2), 0, slice(0, NU), rs_a, coef_a)
                    if stage == "v":
                        dve.wait_ge(*pv.at(b, 0))
                        for i in range(2):
                            dve.wait_ge(*A.filled(c, k + i))
                            dve.tensor_tensor(Vg[:, 4 * i:4 * i + 4, :, 0:HD],
                                              A.bank(k + i)[:, :].rearrange("p (t h d) -> p t h d", t=4, d=HD),
                                              bvb[:, :].rearrange("p (h d) -> p h d", d=HD).unsqueeze(1).broadcast_to([P, 4, NH, HD]),
                                              ALU.add).then_inc(A.emptied(k + i), 1)
                    if stage == "max":
                        n, i = n
                        j, qt, h = i // 2 // NU, i // 2 % NU, i % 2
                        col = (2 * (j % 2) + j // 2) * NU + qt
                        dve.wait_ge(*A.filled(c, k))
                        dve.tensor_reduce(mred[:, col, h:h + 1], A.bank(k)[:, :], AX.X, ALU.max).then_inc(A.emptied(k), 1)
                    if stage == "mrow":
                        link = chain(steps_m, b, 4 * n)
                        for last in (MAXIMA - 2, MAXIMA - 1):
                            dve.wait_ge(*A.moved(c, use["max", (n, last)]))
                        link(dve.tensor_reduce(nm[:, 0, :], mred[:, :, :], AX.X, ALU.max, negate=True))
                        link(dve.tensor_copy(mb[:, 0, :], nm[:, 0, :]))
                        link(dve.tensor_tensor(nm[:, 1, :], nm[:, 0, :], mb[:, 0, :], ALU.subtract))
                        link(dve.tensor_copy(mb[:, 1, :], nm[:, 1, :]))
                        dve.tensor_tensor(mb[:, 2, :], nm[:, 1, :], mb[:, 1, :], ALU.subtract).then_inc(m_red.sem, 1)
                    if stage == "turn":
                        link = chain(steps_o, b, n)
                        dve.wait_ge(*A.filled(c, k))
                        ps = rows_of(A.bank(k), VW)
                        link(dve.reciprocal(rden[:, n % 2, :], ps[:, :, HD]))
                        dve.tensor_tensor(on[:, n % 2, :].rearrange("p (h d) -> p h d", d=HD), ps[:, :, 0:HD],
                                          cast(rden[:, n % 2, :], [P, NH, HD]), ALU.mult).then_inc(A.emptied(k), 1)
                    if stage == "wo":
                        dve.wait_ge(*A.filled(c, k))
                        if n == 0:
                            dve.wait_ge(*xb_a.at(b, 1))
                        dve.tensor_tensor(xres[:, n, :], A.bank(k)[:, 0:P], xres[:, n, :], ALU.add).then_inc(A.emptied(k), 1)
                    if (side, stage) == ("p", "ln"):
                        n, i = n
                        if n == 0:
                            for last in (4 * i + 2, 4 * i + 3):
                                dve.wait_ge(*A.moved(c, use["wo", last]))
                        elif n == 1:
                            dve.wait_ge(*R.moved(b, use["fc", i]))
                        else:
                            for last in (4 * i + 2, 4 * i + 3):
                                dve.wait_ge(*R.moved(b, use["dec", last]))
                        variances(b, link, 1, slice(4 * i, 4 * i + 4), xr if n else xres, var_p)
                    if (side, stage) == ("p", "lnf"):
                        n, i = n
                        factors(b, 2 * n + i + 1, link, 1, slice(4 * i, 4 * i + 4), rs_p, coef_p)
                    if stage == "fcd":
                        k = use["fc", n]
                        dve.wait_ge(*R.filled(b, k))
                        half = slice(4 * (n % 2), 4 * (n % 2) + 4)
                        if n == 0:
                            dve.wait_ge(*out_p.at(b, 0))
                        dve.scalar_tensor_tensor(out=xr[:, half, :], in0=rows_of(R.bank(k), P), scalar=scol[:, 2:3],
                                                 in1=(xr if n >= 2 else xres)[:, half, :],
                                                 op0=ALU.mult, op1=ALU.add).then_inc(R.emptied(k), 1)
                    if (stage, n) == ("qd", 0):
                        dve.wait_ge(*R.moved(b, use["flip", 1]))
                        dve.tensor_copy(xrev[:, T:RPAD], xrev[:, T - 1:T].broadcast_to([P, WIN])).then_inc(xpad.sem, 1)
                        dve.wait_ge(*R.moved(b, use["he", 0]))
                        dve.wait_ge(*R.moved(b, use["he", 1]))
                        link(dve.tensor_reduce(sig[:, 2:3], qh[:, 0:T:8], AX.X, ALU.add))
                        link(dve.tensor_tensor(sig[:, 0:1], sig[:, 0:1], sig[:, 1:2], ALU.add))
                        link(dve.scalar_tensor_tensor(out=sig[:, 0:1], in0=sig[:, 2:3], scalar=4.0, in1=sig[:, 0:1],
                                                      op0=ALU.mult, op1=ALU.add))
                        dve.tensor_scalar(sig[:, 3:4], sig[:, 0:1], 1.0 / T, None, ALU.mult).then_inc(sig_p.sem, 1)
                    if stage == "mod":
                        dve.wait_ge(*R.filled(b, k))
                        dve.tensor_tensor(met[:, 1, :], R.bank(k)[:, 0:3], cols[:, 0, :], ALU.add).then_inc(R.emptied(k), 1)
                        dve.wait_ge(*R.moved(b, k))
                        link(dve.scalar_tensor_tensor(out=met[:, 0, :], in0=met[:, 1, :], scalar=0.1, in1=cols[:, 1, :],
                                                      op0=ALU.mult, op1=ALU.add))
                        link(dve.tensor_scalar(met[:, 1, :], met[:, 0, :], -1.0, None, ALU.mult))
                        dve.tensor_tensor(met[:, 2, :], met[:, 0, :], met[:, 1, :], ALU.max).then_inc(met_z.sem, 1)
                    if (stage, n) == ("key", 3):
                        dve.wait_ge(*met_l.at(b, 1))
                        link(dve.scalar_tensor_tensor(out=met[:, 5, :], in0=met[:, 0, :], scalar=0.0, in1=met[:, 4, :],
                                                      op0=ALU.max, op1=ALU.add))
                        for f in range(2):
                            dve.tensor_scalar(alpha[:, 4 * f:4 * f + 4], half0[:, :], met[:, 5, f:f + 1], 2.0, ALU.mult, ALU.mult)
                        dve.tensor_scalar(beta[:, :], met[:, 5, 0:2], any1[:, :], None, ALU.mult)
                        link(dve.tensor_scalar(nb[:, SH:2 * SH], blk[:, :], met[:, 5, 2:3], None, ALU.mult))
                        dve.sem_inc(met_p.sem, 1)
                    if stage == "keys":
                        dve.wait_ge(*R.moved(b, use["an", 0]))
                        dve.tensor_scalar(gn[:, 0, :, :], an[:, :, 0:SH], 1e-4, None, ALU.max).then_inc(gn_v.sem, 1)
                        dve.wait_ge(*R.moved(b, use["key", 3]))
                        dve.wait_ge(*R.moved(b, use["pad", 0]))
                        for f in range(2):
                            link(dve.tensor_scalar(Bs[:, :], B[:, f, :], beta[:, f:f + 1], any0[:, :], ALU.mult, ALU.add))
                            dve.tensor_tensor(B[:, f, :], Bs[:, :], B[:, f, :], ALU.mult).then_inc(bop.sem, 1)
                            dve.wait_ge(*bop.at(b, f + 1))
                    if stage == "gate":
                        link(dve.tensor_scalar(gn[:, 2, :, :], an[:, :, 0:SH], 0.04, 0.1, ALU.is_gt, ALU.mult))
                        dve.wait_ge(*gn_a.at(b, 1))
                        link(dve.tensor_tensor(gn[:, 2, :, :], gn[:, 2, :, :], gn[:, 1, :, :], ALU.mult))
                    if stage == "hebb":
                        dve.wait_ge(*R.filled(b, k))
                        dve.tensor_tensor(hb[:, 4 * n:4 * n + 4, :].rearrange("p u (h e) -> p (u h) e", e=SE),
                                          rows_of(R.bank(k), SE),
                                          cast(gn[:, 2, 4 * n:4 * n + 4, :].rearrange("p u h -> p (u h)"), [P, 4 * SH, SE]),
                                          ALU.mult).then_inc(R.emptied(k), 1)
                    if stage == "top":
                        n, (r, mark) = n[0], divmod(n[1], 2)
                        half = SH // 2
                        if (r, mark) == (0, 0):
                            dve.wait_ge(*d_pool.at(b, n + 1))
                            pass_waits(dve)
                        for h in range(SH):
                            src = D[:, n % 2, h, :] if r == 0 else Rm[:, h, :]
                            if (r > 0 or mark) and h % half == 0:
                                dve.wait_ge(*top8.at(b, (4 * n + r) * 2 * SH + (h + half if mark else h + half - SH)))
                                pass_waits(dve)
                            if mark:
                                dve.match_replace(out=Rm[:, h, :], in_to_replace=m8[:, h, :], in_values=src,
                                                  imm_value=-2 * BIG).then_inc(top8.sem, 1)
                            else:
                                dve.max(out=m8[:, h, :], in_=src).then_inc(top8.sem, 1)
                        if (r, mark) == (TOPK // 8 - 1, 1):
                            dve.wait_ge(*top8.at(b, (n + 1) * 8 * SH))
                            dve.wait_ge(*e_act.at(b, n + 1))
                            dve.scalar_tensor_tensor(out=E[:, n % 2, :, :], in0=Rm[:, :, :], scalar=-1.5 * BIG,
                                                     in1=E[:, n % 2, :, :], op0=ALU.is_lt, op1=ALU.mult).then_inc(w_v.sem, 1)
                    if stage == "pvd":
                        k = use["pv", n]
                        dve.wait_ge(*R.filled(b, k))
                        ps = R.bank(k)[:, 0:32 * SH].rearrange("p (h e) -> p h e", h=SH)
                        link(dve.tensor_scalar(rd[:, 0, :], ps[:, :, SE], 1e-8, None, ALU.add))
                        link(dve.reciprocal(rd[:, 1, :], rd[:, 0, :]))
                        s3 = s_tok[:, :].rearrange("p (h e) -> p h e", e=SE)
                        dve.tensor_tensor(s3, ps[:, :, 0:SE], cast(rd[:, 1, :], [P, SH, SE]), ALU.mult).then_inc(R.emptied(k), 1)
                        dve.wait_ge(*R.moved(b, k))
                        link(dve.tensor_tensor(s_tok[:, :], s_tok[:, :], hb[:, n, :], ALU.add))
                        dve.tensor_tensor(s_tok[:, :], s_tok[:, :], qtok[:, n, :], ALU.mult).then_inc(s_v.sem, 1)
                    if stage == "decd":
                        k = use["dec", n]
                        dve.wait_ge(*R.filled(b, k))
                        dve.tensor_tensor(xr[:, n, :], R.bank(k)[:, 0:P], xr[:, n, :], ALU.add).then_inc(R.emptied(k), 1)
                assert link_p.done[0] in (0, LINKS_P - LINKS_Q) and link_q.done[0] in (LINKS_P - LINKS_Q, LINKS_P)

            go(FIRST, FIRST_USE, 0, h=0)
            go(TURN0, TURN0_USE, 0, h=1, a=0)
            go(TURN1, TURN1_USE, 1, h=2, a=1, o=0, p=0)
            with dve.Fori(2, NB - 1) as c:
                go(TURN, TURN_USE, c, h=c + 1, a=c, o=c - 1, p=c - 1, q=c - 2)
            go(TURN7, TURN7_USE, NB - 1, a=NB - 1, o=NB - 2, p=NB - 2, q=NB - 3)
            go(LAST, LAST_USE, NB - 1, o=NB - 1, p=NB - 1, q=NB - 2)
            go(DONE, DONE_USE, NB - 1, q=NB - 1)


def kernel(**inputs):
    import numpy as _np
    import concourse.bacc as _bacc
    from concourse import mybir as _mybir
    from concourse.bass_utils import run_bass_kernel_spmd as _run

    nc = _bacc.Bacc("TRN2", target_bir_lowering=False, num_devices=1)
    arrays, args = {}, {}
    for name, a in inputs.items():
        a = _np.ascontiguousarray(a)
        if a.dtype == _np.bool_:
            a = a.view(_np.uint32)
        if a.ndim == 0:
            a = a.reshape(1)
        short = name.removeprefix("L0_attn_a_").removeprefix("L0_attn_b_").removeprefix("L0_ffn_")
        arrays[f"in_{short}"] = a
        args[short] = nc.dram_tensor(f"in_{short}", a.shape, _mybir.dt.from_np(a.dtype), kind="ExternalInput").ap()
    out = nc.dram_tensor("out", (NB, T, P), F32, kind="ExternalOutput").ap()
    hybrid_block_kernel(
        nc, args["hidden_states"], args["Wq"], args["bq"], args["Wk"], args["bk"], args["Wv"], args["bv"],
        args["Wo"], args["bo"], args["encoder_query"], args["encoder_value"], args["mn_w1"], args["mn_b1"],
        args["mn_w2"], args["mn_b2"], args["base_metric"], args["decoder"], args["hebbian_U"], args["hebbian_V"],
        args["k0"], args["k1"], args["k2"], args["s0"], args["s1"], args["s2"], out)
    r = _run(nc, [arrays], core_ids=[0])
    return r.results[0]["out"]
```
